# Optimizing a Trainium2 kernel written in Bass

```python
import numpy as np
import jax
import jax.numpy as jnp

def _softmax(x, axis=-1):
    return jax.nn.softmax(x, axis=axis)

def _gelu(x):
    return jax.nn.gelu(x, approximate=True)

def _silu(x):
    return jax.nn.silu(x)

def _sigmoid(x):
    return jax.nn.sigmoid(x)

def _layernorm(x, axis=-1, eps=1e-05):
    m = jnp.mean(x, axis=axis, keepdims=True)
    v = jnp.var(x, axis=axis, keepdims=True)
    return (x - m) / jnp.sqrt(v + eps)

def _scatter_add(tgt, idx, src, axis=0):
    return tgt.at[idx].add(src)

def _segment_sum(src, seg, n):
    return jax.ops.segment_sum(src, seg, n)
kernel_name = 'mk_audio_tower_d2_tok_audfeat1024_r4_62bf5f'

def setup_inputs(seed: int=0):
    np.random.seed(seed)
    _w = jnp.asarray

    def _rec_inputs():
        import jax
        import jax.numpy as jnp
        _rk = jax.random.key(seed)
        x = 7.22013e-05 + 1.00017 * jax.random.normal(jax.random.fold_in(_rk, 1), (64, 64, 256), jnp.float32)
        return x
    x = _rec_inputs()

    def _L0_tok_setup():
        import jax, jax.numpy as jnp
        import numpy as np
        PATCH_LEN = 16
        STRIDE = 8
        D_MODEL = 256

        def _patchify(x):
            B, V, T = x.shape
            pad = jnp.broadcast_to(x[:, :, -1:], (B, V, STRIDE))
            xp = jnp.concatenate([x, pad], axis=-1)
            L = (T + STRIDE - PATCH_LEN) // STRIDE + 1
            idx = jnp.arange(L)[:, None] * STRIDE + jnp.arange(PATCH_LEN)[None, :]
            patches = xp[:, :, idx]
            patches = jnp.transpose(patches, (0, 2, 1, 3))
            return patches.reshape(B, L, V * PATCH_LEN)
        key = jax.random.key(seed)
        k0, k1, k2, k3, k4 = jax.random.split(key, 5)
        B, V, T = (32, 64, 1024)
        c_in = V * PATCH_LEN
        x = jax.random.normal(k0, (B, V, T), dtype=jnp.float32)
        s1 = 1.0 / np.sqrt(c_in)
        s2 = 1.0 / np.sqrt(D_MODEL)
        W1 = jax.random.uniform(k1, (c_in, D_MODEL), jnp.float32, -s1, s1)
        b1 = jax.random.uniform(k2, (D_MODEL,), jnp.float32, -s1, s1)
        W2 = jax.random.uniform(k3, (D_MODEL, D_MODEL), jnp.float32, -s2, s2)
        b2 = jax.random.uniform(k4, (D_MODEL,), jnp.float32, -s2, s2)
        return {'x': x, 'W1': W1, 'b1': b1, 'W2': W2, 'b2': b2}
    _L0_tok_all = _L0_tok_setup()
    _L0_tok_in = {k: v for k, v in _L0_tok_all.items() if k in ('W1', 'b1', 'W2', 'b2')}
    del _L0_tok_all

    def _L0_attn_setup():
        import jax, jax.numpy as jnp
        import numpy as np
        B, T, HID, H, DH, K = (2, 256, 256, 16, 64, 4)
        ROPE_BASE = 10000.0
        EPS = 1e-06

        def _causal_dwconv(x, w, b):
            xc = jnp.transpose(x, (0, 2, 1))
            y = jax.lax.conv_general_dilated(xc, w, window_strides=(1,), padding=[(K - 1, 0)], dimension_numbers=('NCH', 'OIH', 'NCH'), feature_group_count=xc.shape[1])
            y = y + b[None, :, None]
            return jax.nn.silu(jnp.transpose(y, (0, 2, 1)))

        def _rope(x, cos, sin):
            c = cos[None, :, None, :]
            s = sin[None, :, None, :]
            x1, x2 = (x[..., ::2], x[..., 1::2])
            return jnp.concatenate([x1 * c[..., ::2] - x2 * s[..., ::2], x1 * s[..., ::2] + x2 * c[..., ::2]], axis=-1)

        def _delta_rule(q, k, v, alpha, beta, D_param):
            qs = jnp.moveaxis(q, 1, 0).astype(jnp.float32)
            ks = jnp.moveaxis(k, 1, 0).astype(jnp.float32)
            vs = jnp.moveaxis(v, 1, 0).astype(jnp.float32)
            als = jnp.moveaxis(alpha, 1, 0).astype(jnp.float32)
            bes = jnp.moveaxis(beta, 1, 0).astype(jnp.float32)

            def step(S, inp):
                qt, kt, vt, at, bt = inp
                ot = jnp.einsum('bhd,bhde->bhe', qt, S)
                ot = ot + D_param[None, :, None] * jnp.sum(qt * kt, -1, keepdims=True) * vt
                kS = jnp.einsum('bhd,bhde->bhe', kt, S)
                at_ = at[..., None, None]
                bt_ = bt[..., None, None]
                S_new = at_ * (S - bt_ * kt[..., :, None] * kS[..., None, :]) + bt_ * kt[..., :, None] * vt[..., None, :]
                return (S_new, ot)
            S0 = jnp.zeros((q.shape[0], H, DH, DH), jnp.float32)
            _, outs = jax.lax.scan(step, S0, (qs, ks, vs, als, bes))
            return jnp.moveaxis(outs, 0, 1)

        def _forward(x, Wq, Wk, Wv, Wg, Wo, bw, bb, gkw, gkb, qcw, qcb, kcw, kcb, vcw, vcb, A_log, D_param, dt_bias, onorm_w):
            Bb, Tt, _ = x.shape
            q = _causal_dwconv(x @ Wq, qcw, qcb).reshape(Bb, Tt, H, DH)
            k = _causal_dwconv(x @ Wk, kcw, kcb).reshape(Bb, Tt, H, DH)
            v = _causal_dwconv(x @ Wv, vcw, vcb).reshape(Bb, Tt, H, DH)
            t = jnp.arange(Tt, dtype=jnp.float32)
            inv_freq = 1.0 / ROPE_BASE ** (jnp.arange(0, DH, 2, dtype=jnp.float32) / DH)
            freqs = jnp.outer(t, inv_freq)
            emb = jnp.concatenate([freqs, freqs], -1)
            cos, sin = (jnp.cos(emb), jnp.sin(emb))
            q = _rope(q, cos, sin)
            k = _rope(k, cos, sin)
            q = q * jax.lax.rsqrt(jnp.sum(q * q, -1, keepdims=True) + EPS)
            k = k * jax.lax.rsqrt(jnp.sum(k * k, -1, keepdims=True) + EPS)
            beta = jax.nn.sigmoid(x @ bw + bb)
            alpha = jnp.exp(-jnp.exp(A_log) * jax.nn.softplus(x @ gkw + gkb + dt_bias))
            o = _delta_rule(q, k, v, alpha, beta, D_param)
            g = (x @ Wg).reshape(Bb, Tt, H, DH)
            on = o * jax.lax.rsqrt(jnp.mean(o * o, -1, keepdims=True) + EPS) * onorm_w
            o = g * jax.nn.silu(on)
            return o.reshape(Bb, Tt, H * DH) @ Wo
        key = jax.random.key(seed)
        ks = jax.random.split(key, 20)
        w = lambda i, shape, s=0.02: jax.random.normal(ks[i], shape, jnp.float32) * s
        return {'x': jax.random.normal(ks[0], (B, T, HID), jnp.float32), 'Wq': w(1, (HID, H * DH)), 'Wk': w(2, (HID, H * DH)), 'Wv': w(3, (HID, H * DH)), 'Wg': w(4, (HID, H * DH)), 'Wo': w(5, (H * DH, HID)), 'bw': w(6, (HID, H)), 'bb': jnp.zeros((H,), jnp.float32), 'gkw': w(7, (HID, H)), 'gkb': jnp.zeros((H,), jnp.float32), 'qcw': w(8, (H * DH, 1, K), 0.3), 'qcb': jnp.zeros((H * DH,), jnp.float32), 'kcw': w(9, (H * DH, 1, K), 0.3), 'kcb': jnp.zeros((H * DH,), jnp.float32), 'vcw': w(10, (H * DH, 1, K), 0.3), 'vcb': jnp.zeros((H * DH,), jnp.float32), 'A_log': jnp.log(jax.random.uniform(ks[11], (H,), jnp.float32, 1.0, 16.0)), 'D_param': jnp.ones((H,), jnp.float32), 'dt_bias': jax.random.uniform(ks[12], (H,), jnp.float32, -0.01, 0.01), 'onorm_w': jnp.ones((DH,), jnp.float32)}
    _L0_attn_all = _L0_attn_setup()
    _L0_attn_in = {k: v for k, v in _L0_attn_all.items() if k in ('Wq', 'Wk', 'Wv', 'Wg', 'Wo', 'bw', 'bb', 'gkw', 'gkb', 'qcw', 'qcb', 'kcw', 'kcb', 'vcw', 'vcb', 'A_log', 'D_param', 'dt_bias', 'onorm_w')}
    del _L0_attn_all

    def _L0_ffn_setup():
        import jax, jax.numpy as jnp
        import numpy as np
        E, K, H, F, R = (8, 2, 256, 512, 64)
        B, S = (2, 512)
        key = jax.random.key(seed)
        k0, k1, k2, k3, k4 = jax.random.split(key, 5)
        return {'hidden_states': jax.random.normal(k0, (B, S, H), dtype=jnp.float32), 'W_A': jax.random.normal(k1, (E, R, H), dtype=jnp.float32) * 0.02, 'W_B': jax.random.normal(k2, (E, F, R), dtype=jnp.float32) * 0.02, 'W_up': jax.random.normal(k3, (E, F, H), dtype=jnp.float32) * 0.02, 'W_down': jax.random.normal(k4, (E, H, F), dtype=jnp.float32) * 0.02}
    _L0_ffn_all = _L0_ffn_setup()
    _L0_ffn_in = {k: v for k, v in _L0_ffn_all.items() if k in ('W_A', 'W_B', 'W_up', 'W_down')}
    del _L0_ffn_all

    def _L1_attn_setup():
        import jax, jax.numpy as jnp
        import numpy as np
        D_MODEL = 256
        D_STATE = 16
        D_CONV = 4
        EXPAND = 2
        D_INNER = EXPAND * D_MODEL
        DT_RANK = (D_MODEL + 15) // 16
        BATCH = 2
        SEQLEN = 512
        key = jax.random.key(seed)
        ks = jax.random.split(key, 8)
        s = lambda k, shape, scale: jax.random.normal(k, shape, dtype=jnp.float32) * scale
        return {'x': s(ks[0], (BATCH, SEQLEN, D_MODEL), 1.0), 'W_in': s(ks[1], (D_MODEL, 2 * D_INNER), D_MODEL ** (-0.5)), 'conv_w': s(ks[2], (D_INNER, 1, D_CONV), 0.3), 'conv_b': jnp.zeros((D_INNER,), dtype=jnp.float32), 'W_x': s(ks[3], (D_INNER, DT_RANK + 2 * D_STATE), D_INNER ** (-0.5)), 'W_dt': s(ks[4], (DT_RANK, D_INNER), 2.0 * DT_RANK ** (-0.5)), 'b_dt': s(ks[5], (D_INNER,), 0.1), 'A_log': jnp.log(jnp.tile(jnp.arange(1, D_STATE + 1, dtype=jnp.float32), (D_INNER, 1))), 'D': jnp.ones((D_INNER,), dtype=jnp.float32), 'W_out': s(ks[6], (D_INNER, D_MODEL), D_INNER ** (-0.5))}
    _L1_attn_all = _L1_attn_setup()
    _L1_attn_in = {k: v for k, v in _L1_attn_all.items() if k in ('W_in', 'conv_w', 'conv_b', 'W_x', 'W_dt', 'b_dt', 'A_log', 'D', 'W_out')}
    del _L1_attn_all

    def _L1_ffn_setup():
        import jax, jax.numpy as jnp
        import numpy as np
        D_MODEL = 256
        key = jax.random.key(seed)
        k_x, k_w, k_a1, k_a2 = jax.random.split(key, 4)
        x = jax.random.normal(k_x, (4, 512, D_MODEL), dtype=jnp.float32)
        weight = jax.random.normal(k_w, (D_MODEL, D_MODEL), dtype=jnp.float32) * 0.02
        aux_weight1 = jax.random.normal(k_a1, (D_MODEL, D_MODEL), dtype=jnp.float32) * 0.02
        aux_weight2 = jax.random.normal(k_a2, (D_MODEL, D_MODEL), dtype=jnp.float32) * 0.02
        bias = jnp.zeros((D_MODEL,), dtype=jnp.float32)
        return {'x': x, 'weight': weight, 'aux_weight1': aux_weight1, 'aux_weight2': aux_weight2, 'bias': bias}
    _L1_ffn_all = _L1_ffn_setup()
    _L1_ffn_in = {k: v for k, v in _L1_ffn_all.items() if k in ('weight', 'aux_weight1', 'aux_weight2', 'bias')}
    del _L1_ffn_all
    return {'x': x, 'L0_tok_W1': _L0_tok_in['W1'], 'L0_tok_b1': _L0_tok_in['b1'], 'L0_tok_W2': _L0_tok_in['W2'], 'L0_tok_b2': _L0_tok_in['b2'], 'L0_attn_Wq': _L0_attn_in['Wq'], 'L0_attn_Wk': _L0_attn_in['Wk'], 'L0_attn_Wv': _L0_attn_in['Wv'], 'L0_attn_Wg': _L0_attn_in['Wg'], 'L0_attn_Wo': _L0_attn_in['Wo'], 'L0_attn_bw': _L0_attn_in['bw'], 'L0_attn_bb': _L0_attn_in['bb'], 'L0_attn_gkw': _L0_attn_in['gkw'], 'L0_attn_gkb': _L0_attn_in['gkb'], 'L0_attn_qcw': _L0_attn_in['qcw'], 'L0_attn_qcb': _L0_attn_in['qcb'], 'L0_attn_kcw': _L0_attn_in['kcw'], 'L0_attn_kcb': _L0_attn_in['kcb'], 'L0_attn_vcw': _L0_attn_in['vcw'], 'L0_attn_vcb': _L0_attn_in['vcb'], 'L0_attn_A_log': _L0_attn_in['A_log'], 'L0_attn_D_param': _L0_attn_in['D_param'], 'L0_attn_dt_bias': _L0_attn_in['dt_bias'], 'L0_attn_onorm_w': _L0_attn_in['onorm_w'], 'L0_ffn_W_A': _L0_ffn_in['W_A'], 'L0_ffn_W_B': _L0_ffn_in['W_B'], 'L0_ffn_W_up': _L0_ffn_in['W_up'], 'L0_ffn_W_down': _L0_ffn_in['W_down'], 'L1_attn_W_in': _L1_attn_in['W_in'], 'L1_attn_conv_w': _L1_attn_in['conv_w'], 'L1_attn_conv_b': _L1_attn_in['conv_b'], 'L1_attn_W_x': _L1_attn_in['W_x'], 'L1_attn_W_dt': _L1_attn_in['W_dt'], 'L1_attn_b_dt': _L1_attn_in['b_dt'], 'L1_attn_A_log': _L1_attn_in['A_log'], 'L1_attn_D': _L1_attn_in['D'], 'L1_attn_W_out': _L1_attn_in['W_out'], 'L1_ffn_weight': _L1_ffn_in['weight'], 'L1_ffn_aux_weight1': _L1_ffn_in['aux_weight1'], 'L1_ffn_aux_weight2': _L1_ffn_in['aux_weight2'], 'L1_ffn_bias': _L1_ffn_in['bias']}

def reference(x, L0_tok_W1, L0_tok_b1, L0_tok_W2, L0_tok_b2, L0_attn_Wq, L0_attn_Wk, L0_attn_Wv, L0_attn_Wg, L0_attn_Wo, L0_attn_bw, L0_attn_bb, L0_attn_gkw, L0_attn_gkb, L0_attn_qcw, L0_attn_qcb, L0_attn_kcw, L0_attn_kcb, L0_attn_vcw, L0_attn_vcb, L0_attn_A_log, L0_attn_D_param, L0_attn_dt_bias, L0_attn_onorm_w, L0_ffn_W_A, L0_ffn_W_B, L0_ffn_W_up, L0_ffn_W_down, L1_attn_W_in, L1_attn_conv_w, L1_attn_conv_b, L1_attn_W_x, L1_attn_W_dt, L1_attn_b_dt, L1_attn_A_log, L1_attn_D, L1_attn_W_out, L1_ffn_weight, L1_ffn_aux_weight1, L1_ffn_aux_weight2, L1_ffn_bias):
    import jax
    import jax.numpy as jnp

    def _L0_tok_ref(x, W1, b1, W2, b2):
        import jax, jax.numpy as jnp
        import numpy as np
        PATCH_LEN = 16
        STRIDE = 8
        D_MODEL = 256

        def _patchify(x):
            B, V, T = x.shape
            pad = jnp.broadcast_to(x[:, :, -1:], (B, V, STRIDE))
            xp = jnp.concatenate([x, pad], axis=-1)
            L = (T + STRIDE - PATCH_LEN) // STRIDE + 1
            idx = jnp.arange(L)[:, None] * STRIDE + jnp.arange(PATCH_LEN)[None, :]
            patches = xp[:, :, idx]
            patches = jnp.transpose(patches, (0, 2, 1, 3))
            return patches.reshape(B, L, V * PATCH_LEN)
        p = _patchify(x)
        h = jax.nn.relu(jnp.einsum('blc,cd->bld', p, W1) + b1)
        out = jnp.einsum('bld,de->ble', h, W2) + b2
        return out

    def _L0_attn_ref(x, Wq, Wk, Wv, Wg, Wo, bw, bb, gkw, gkb, qcw, qcb, kcw, kcb, vcw, vcb, A_log, D_param, dt_bias, onorm_w):
        import jax, jax.numpy as jnp
        import numpy as np
        B, T, HID, H, DH, K = (2, 256, 256, 16, 64, 4)
        ROPE_BASE = 10000.0
        EPS = 1e-06

        def _causal_dwconv(x, w, b):
            xc = jnp.transpose(x, (0, 2, 1))
            y = jax.lax.conv_general_dilated(xc, w, window_strides=(1,), padding=[(K - 1, 0)], dimension_numbers=('NCH', 'OIH', 'NCH'), feature_group_count=xc.shape[1])
            y = y + b[None, :, None]
            return jax.nn.silu(jnp.transpose(y, (0, 2, 1)))

        def _rope(x, cos, sin):
            c = cos[None, :, None, :]
            s = sin[None, :, None, :]
            x1, x2 = (x[..., ::2], x[..., 1::2])
            return jnp.concatenate([x1 * c[..., ::2] - x2 * s[..., ::2], x1 * s[..., ::2] + x2 * c[..., ::2]], axis=-1)

        def _delta_rule(q, k, v, alpha, beta, D_param):
            qs = jnp.moveaxis(q, 1, 0).astype(jnp.float32)
            ks = jnp.moveaxis(k, 1, 0).astype(jnp.float32)
            vs = jnp.moveaxis(v, 1, 0).astype(jnp.float32)
            als = jnp.moveaxis(alpha, 1, 0).astype(jnp.float32)
            bes = jnp.moveaxis(beta, 1, 0).astype(jnp.float32)

            def step(S, inp):
                qt, kt, vt, at, bt = inp
                ot = jnp.einsum('bhd,bhde->bhe', qt, S)
                ot = ot + D_param[None, :, None] * jnp.sum(qt * kt, -1, keepdims=True) * vt
                kS = jnp.einsum('bhd,bhde->bhe', kt, S)
                at_ = at[..., None, None]
                bt_ = bt[..., None, None]
                S_new = at_ * (S - bt_ * kt[..., :, None] * kS[..., None, :]) + bt_ * kt[..., :, None] * vt[..., None, :]
                return (S_new, ot)
            S0 = jnp.zeros((q.shape[0], H, DH, DH), jnp.float32)
            _, outs = jax.lax.scan(step, S0, (qs, ks, vs, als, bes))
            return jnp.moveaxis(outs, 0, 1)

        def _forward(x, Wq, Wk, Wv, Wg, Wo, bw, bb, gkw, gkb, qcw, qcb, kcw, kcb, vcw, vcb, A_log, D_param, dt_bias, onorm_w):
            Bb, Tt, _ = x.shape
            q = _causal_dwconv(x @ Wq, qcw, qcb).reshape(Bb, Tt, H, DH)
            k = _causal_dwconv(x @ Wk, kcw, kcb).reshape(Bb, Tt, H, DH)
            v = _causal_dwconv(x @ Wv, vcw, vcb).reshape(Bb, Tt, H, DH)
            t = jnp.arange(Tt, dtype=jnp.float32)
            inv_freq = 1.0 / ROPE_BASE ** (jnp.arange(0, DH, 2, dtype=jnp.float32) / DH)
            freqs = jnp.outer(t, inv_freq)
            emb = jnp.concatenate([freqs, freqs], -1)
            cos, sin = (jnp.cos(emb), jnp.sin(emb))
            q = _rope(q, cos, sin)
            k = _rope(k, cos, sin)
            q = q * jax.lax.rsqrt(jnp.sum(q * q, -1, keepdims=True) + EPS)
            k = k * jax.lax.rsqrt(jnp.sum(k * k, -1, keepdims=True) + EPS)
            beta = jax.nn.sigmoid(x @ bw + bb)
            alpha = jnp.exp(-jnp.exp(A_log) * jax.nn.softplus(x @ gkw + gkb + dt_bias))
            o = _delta_rule(q, k, v, alpha, beta, D_param)
            g = (x @ Wg).reshape(Bb, Tt, H, DH)
            on = o * jax.lax.rsqrt(jnp.mean(o * o, -1, keepdims=True) + EPS) * onorm_w
            o = g * jax.nn.silu(on)
            return o.reshape(Bb, Tt, H * DH) @ Wo
        return _forward(x, Wq, Wk, Wv, Wg, Wo, bw, bb, gkw, gkb, qcw, qcb, kcw, kcb, vcw, vcb, A_log, D_param, dt_bias, onorm_w)

    def _L0_ffn_ref(hidden_states, W_A, W_B, W_up, W_down):
        import jax, jax.numpy as jnp
        import numpy as np
        E, K, H, F, R = (8, 2, 256, 512, 64)
        B, S = (2, 512)
        orig_shape = hidden_states.shape
        x = hidden_states.reshape(-1, orig_shape[-1])
        num_experts = W_A.shape[0]
        gate_hidden = jnp.einsum('nh,erh->ner', x, W_A)
        scores = jnp.sqrt(jnp.sum(gate_hidden * gate_hidden, axis=-1))
        topk_scores, topk_idx = jax.lax.top_k(scores, K)
        topk_w = jax.nn.softmax(topk_scores, axis=-1)
        w_full = jnp.sum(jax.nn.one_hot(topk_idx, num_experts, dtype=topk_w.dtype) * topk_w[..., None], axis=1)
        g = jnp.einsum('ner,efr->nef', gate_hidden, W_B)
        up = jnp.einsum('nh,efh->nef', x, W_up)
        y = jnp.einsum('nef,ehf->neh', jax.nn.silu(g) * up, W_down)
        out = jnp.einsum('neh,ne->nh', y, w_full)
        return out.reshape(orig_shape)

    def _L1_attn_ref(x, W_in, conv_w, conv_b, W_x, W_dt, b_dt, A_log, D, W_out):
        import jax, jax.numpy as jnp
        import numpy as np
        D_MODEL = 256
        D_STATE = 16
        D_CONV = 4
        EXPAND = 2
        D_INNER = EXPAND * D_MODEL
        DT_RANK = (D_MODEL + 15) // 16
        BATCH = 2
        SEQLEN = 512
        dt_rank = W_dt.shape[0]
        d_state = A_log.shape[1]
        Bsz, L, _ = x.shape
        d_inner = conv_w.shape[0]
        xr = x @ W_in
        xi, res = jnp.split(xr, 2, axis=-1)
        xc = jax.lax.conv_general_dilated(xi.transpose(0, 2, 1), conv_w, window_strides=(1,), padding=[(conv_w.shape[-1] - 1, 0)], feature_group_count=d_inner) + conv_b[None, :, None]
        u = jax.nn.silu(xc.transpose(0, 2, 1))
        dbc = u @ W_x
        delta_r = dbc[..., :dt_rank]
        Bm = dbc[..., dt_rank:dt_rank + d_state]
        Cm = dbc[..., dt_rank + d_state:]
        delta = jax.nn.softplus(delta_r @ W_dt + b_dt)
        A = -jnp.exp(A_log)
        deltaA = jnp.exp(delta[..., None] * A)
        dBu = delta[..., None] * Bm[:, :, None, :] * u[..., None]

        def step(h, inp):
            dA_t, dBu_t, C_t = inp
            h = dA_t * h + dBu_t
            y_t = jnp.einsum('bdn,bn->bd', h, C_t)
            return (h, y_t)
        h0 = jnp.zeros((Bsz, d_inner, d_state), dtype=x.dtype)
        _, ys = jax.lax.scan(step, h0, (deltaA.transpose(1, 0, 2, 3), dBu.transpose(1, 0, 2, 3), Cm.transpose(1, 0, 2)))
        y = ys.transpose(1, 0, 2) + u * D
        y = y * jax.nn.silu(res)
        return y @ W_out

    def _L1_ffn_ref(x, weight, aux_weight1, aux_weight2, bias):
        import jax, jax.numpy as jnp
        import numpy as np
        D_MODEL = 256
        h = jnp.einsum('btc,cd->btd', x, weight)
        h = jnp.einsum('btc,cd->btd', h, aux_weight1)
        h = jnp.einsum('btc,cd->btd', h, aux_weight2)
        return jnp.tanh(h + bias)
    h = _L0_tok_ref(x, L0_tok_W1, L0_tok_b1, L0_tok_W2, L0_tok_b2)
    h = h + _L0_attn_ref(_layernorm(h, axis=-1), L0_attn_Wq, L0_attn_Wk, L0_attn_Wv, L0_attn_Wg, L0_attn_Wo, L0_attn_bw, L0_attn_bb, L0_attn_gkw, L0_attn_gkb, L0_attn_qcw, L0_attn_qcb, L0_attn_kcw, L0_attn_kcb, L0_attn_vcw, L0_attn_vcb, L0_attn_A_log, L0_attn_D_param, L0_attn_dt_bias, L0_attn_onorm_w)
    h = h + _L0_ffn_ref(_layernorm(h, axis=-1), L0_ffn_W_A, L0_ffn_W_B, L0_ffn_W_up, L0_ffn_W_down)
    h = h + _L1_attn_ref(_layernorm(h, axis=-1), L1_attn_W_in, L1_attn_conv_w, L1_attn_conv_b, L1_attn_W_x, L1_attn_W_dt, L1_attn_b_dt, L1_attn_A_log, L1_attn_D, L1_attn_W_out)
    h = h + _L1_ffn_ref(_layernorm(h, axis=-1), L1_ffn_weight, L1_ffn_aux_weight1, L1_ffn_aux_weight2, L1_ffn_bias)
    return h

_drawn_inputs = setup_inputs


def setup_inputs(seed=0):
    import zlib

    import numpy as np

    out = dict(_drawn_inputs(seed))
    spreads = {'L0_attn_bb': (0.0, 0.6),
     'L0_attn_gkb': (0.0, 0.8),
     'L0_attn_qcb': (0.0, 0.1),
     'L0_attn_kcb': (0.0, 0.1),
     'L0_attn_vcb': (0.0, 0.1),
     'L0_attn_D_param': (1.0, 0.2),
     'L0_attn_onorm_w': (1.0, 0.2),
     'L1_attn_conv_b': (0.0, 0.271),
     'L1_attn_D': (1.0, 0.586),
     'L1_ffn_bias': (0.0, 0.1)}
    factors = {'L0_attn_gkw': 4.487,
     'L0_attn_dt_bias': 8.0,
     'L0_ffn_W_A': 4.391,
     'L0_ffn_W_B': 4.444,
     'L0_ffn_W_up': 4.467,
     'L0_ffn_W_down': 4.439,
     'L1_attn_b_dt': 16.066,
     'L1_attn_A_log': 6.589,
     'L1_ffn_aux_weight1': 2.687,
     'L1_ffn_aux_weight2': 2.667}
    for name, (base, spread) in spreads.items():
        noise = np.random.default_rng([zlib.crc32(name.encode()), seed]).standard_normal(out[name].shape)
        drawn = base * np.exp(spread * noise) if base else spread * noise
        out[name] = jnp.asarray(drawn.astype(out[name].dtype))
    for name, factor in factors.items():
        out[name] = (out[name] * factor).astype(out[name].dtype)
    return out
```

```python
from contextlib import ExitStack

import numpy as np

import concourse.bass as bass
from concourse import mybir

F32 = mybir.dt.float32
ALU = mybir.AluOpType
ACT = mybir.ActivationFunctionType
AX = mybir.AxisListType

LAST_PHASE = 5

P = 128
B, V, T, D = 64, 64, 256, 256
PATCH, STRIDE = 16, 8
L = (T + STRIDE - PATCH) // STRIDE + 1
N = B * L
TILE = 512
TILES = N // TILE
SEQ = TILE // L
KD = D // P


class Columns:

    def __init__(self):
        self.at, self.parts, self.n = {}, [], 0

    def add(self, name, a):
        self.at[name] = self.n
        self.parts.append(a)
        self.n += a.shape[1]


def phase_tokens(nc, mem, dram, sems):
    hT, vec, cols = mem.hT, mem.vec, mem.cols
    x = mem.part([P, B, T])
    w1 = mem.part([P, PATCH // 2, D])
    w2 = mem.part([P, KD, D])
    hid = mem.part([P, KD, TILE])
    with ExitStack() as ctx:
        ps_hid = ctx.enter_context(nc.psum_tensor("ps_hid", [P, KD, TILE], F32))
        ps_out = ctx.enter_context(nc.psum_tensor("ps_out", [P, KD, TILE], F32))
        weights_in, x_in, x_padded, hid_summed, hid_ready, out_summed, out_added = (
            mem.ctx.enter_context(nc.semaphore(n)) for n in
            ("tok_weights_in", "x_in", "x_padded", "hid_summed", "hid_ready", "tok_summed", "tok_added"))
        block = ctx.enter_context(nc.Block())
        xv = dram["x"].rearrange("b v t -> v b t")

        @block.sync
        def _(sp):
            open_phase(sp, [weights_in, x_in, x_padded, hid_summed, hid_ready, out_summed, out_added])
            sp.dma_start(w1[:], dram["W1"]).then_inc(weights_in, 16)
            sp.dma_start(w2[:], dram["W2"]).then_inc(weights_in, 16)
            sp.dma_start(vec[:], dram["vec"]).then_inc(weights_in, 16)
            sp.dma_start(mem.const[:], dram["const"]).then_inc(weights_in, 16)
            with sp.Fori(0, TILES) as i:
                sp.wait_ge(x_in, i * 32 + START)
                sp.dma_start(x[0:V, bass.ds(i * SEQ, SEQ), :], xv[:, bass.ds(i * SEQ, SEQ), :]).then_inc(x_in, 16)
                sp.dma_start(x[V:P, bass.ds(i * SEQ, SEQ), 0:T - STRIDE],
                             xv[:, bass.ds(i * SEQ, SEQ), STRIDE:T]).then_inc(x_in, 16)

        @block.gpsimd
        def _(pool):
            with pool.Fori(0, TILES) as i:
                pool.wait_ge(x_in, i * 32 + 32 + START)
                s = bass.ds(i * SEQ, SEQ)
                pool.tensor_copy(x[V:P, s, T - STRIDE:T],
                                 x[V:P, s, T - STRIDE - 1:T - STRIDE].broadcast_to([V, SEQ, STRIDE])
                                 ).then_inc(x_padded, 1)

        @block.tensor
        def _(pe):
            pe.wait_ge(weights_in, 64 + START)
            with pe.Fori(0, TILES) as i:
                pe.wait_ge(x_padded, i + 1 + START)
                pe.wait_ge(hid_ready, i * KD + START)
                for m in range(KD):
                    for p in range(PATCH // 2):
                        mm = pe.matmul(ps_hid[:, m, :], w1[:, p, m * P:(m + 1) * P],
                                       x[:, bass.ds(i * SEQ, SEQ), p:T:STRIDE],
                                       start=(p == 0), stop=(p == PATCH // 2 - 1))
                    mm.then_inc(hid_summed, 1)
                pe.wait_ge(hid_ready, i * KD + KD + START)
                pe.wait_ge(out_added, i * KD + START)
                for m in range(KD):
                    for k in range(KD):
                        mm = pe.matmul(ps_out[:, m, :], w2[:, k, m * P:(m + 1) * P], hid[:, k, :],
                                       start=(k == 0), stop=(k == KD - 1))
                    mm.then_inc(out_summed, 1)

        @block.scalar
        def _(act):
            act.wait_ge(weights_in, 64 + START)
            with act.Fori(0, TILES) as i:
                act.wait_ge(out_summed, i * KD + START)
                for m in range(KD):
                    act.wait_ge(hid_summed, i * KD + m + 1 + START)
                    c = cols["b1"] + m
                    act.activation(hid[:, m, :], ps_hid[:, m, :], ACT.Relu,
                                   bias=vec[:, c:c + 1]).then_inc(hid_ready, 1)

        @block.vector
        def _(dve):
            dve.wait_ge(weights_in, 64 + START)
            with dve.Fori(0, TILES) as i:
                for m in range(KD):
                    dve.wait_ge(out_summed, i * KD + m + 1 + START)
                    c = cols["b2"] + m
                    dve.tensor_scalar(hT[:, m, bass.ds(i * TILE, TILE)], ps_out[:, m, :],
                                      vec[:, c:c + 1], None, ALU.add).then_inc(out_added, 1)


HEADS, DH, CONV = 16, 64, 4
INNER = HEADS * DH
HC = INNER // P
HALVES = 2
HALF = N // HALVES
HT = HALF // TILE
SUBS = HALF // P
SPB = P // L
UNITS = HT * HC
START = 1


def open_phase(eng, sems):
    for s in sems:
        eng.sem_inc(s, START)


def named(nc, ctx, names):
    return [ctx.enter_context(nc.semaphore(n)) for n in names.split()]


def diagonal(rows, seq):
    return rows[:, seq * L:seq * L + (L - 1) * (P + 1) + 1:P + 1]


def phase_attention(nc, mem, dram):
    hT, vec, cols, cst = mem.hT, mem.vec, mem.cols, mem.cst
    part = mem.part
    w_qkv = part([P, 3, KD, INNER])
    w_g = part([P, KD, INNER])
    w_o = part([P, HC, D])
    w_ab = part([P, KD, 2 * HEADS])
    xn = part([P, KD, HALF])
    at_v = mem.used
    v_rows = part([P, SUBS, INNER])
    at_scores = mem.used
    scores = part([P, 2 * L, SUBS, HEADS])
    table_rows = part([P, L, SUBS, HEADS], at_scores)
    spread = [part([P, HEADS, P], at_scores + 4096 + b * 2048) for b in range(2)]
    decay = part([P, L, SPB, L])
    ab = part([P, 3, SUBS, HEADS])
    gates = part([P, 3, P])
    g_small = part([P, 12, P])
    nega = part([P, 2])
    work = mem.used
    kq_rows = part([P, 2 * L, P])
    k_flat = kq_rows[:, 0:L, :].rearrange("p a b -> p (a b)")
    q_flat = kq_rows[:, L:2 * L, :].rearrange("p a b -> p (a b)")
    a_rows = kq_rows[:, 0:L, :]
    g_rows = kq_rows[:, L:2 * L, :]
    a4 = a_rows.rearrange("p t (j s) -> p t j s", j=SPB)
    g4 = g_rows.rearrange("p t (j s) -> p t j s", j=SPB)
    product = part([P, 1024])
    end = mem.used
    mem.used = work
    padded = [part([P, SEQ, L + CONV - 1]) for _ in range(3)]
    conv = [part([P, TILE]) for _ in range(3)]
    acted = [[part([P, TILE]) for _ in range(3)] for _ in range(3)]
    swapped = [part([P, TILE]) for _ in range(2)]
    cosine = [part([P, TILE]) for _ in range(2)]
    sine = swapped
    kq = [part([P, 2, TILE]) for _ in range(2)]
    q_square = part([P, TILE])
    end = max(end, mem.used)
    mem.used = end
    centred = part([P, KD, TILE], at_v)
    squared = part([P, KD, TILE], at_v + 1024)
    deviation = part([P, TILE], at_v + 2048)
    inverse = part([P, TILE], at_v + 2560)
    o_sb = part([P, HC, P], work)
    o_sq = part([P, HC, P], work + 1024)
    o_sd = part([P, HC, P], work + 2048)
    o_inv = part([P, HC, P], work + 3072)
    o_norm = part([P, HC, P], work + 4096)
    o_act = part([P, HC, P], work + 5120)
    gate = [part([P, HC, P], work + 6144 + b * 1024) for b in range(2)]
    gated = part([P, HC, P], work + 8192)

    with ExitStack() as ctx:
        ps = ctx.enter_context(nc.psum_tensor("ps_attention", [P, 8, 512], F32))
        (w_in, wo_in, summed_mean, centred_s, squared_s, summed_var, rooted, inverted, normed,
         pads_clear, projected, raw_copied, shuffled, cosined, sined, kq_ready, v_act, q_squared,
         scored, v_turned, score_kept, v_kept, lengths_summed) = named(nc, mem.ctx, (
            "w_in wo_in summed_mean centred squared summed_var rooted inverted normed "
            "pads_clear projected raw_copied shuffled cosined sined kq_ready v_act q_squared "
            "scored v_turned score_kept v_kept lengths_summed"))
        conv_step = named(nc, mem.ctx, "conv_q conv_k conv_v")
        acted_s = named(nc, mem.ctx, "acted_q acted_k acted_v")
        (ab_summed, ab_kept, gates_turned, gates_kept, act_gate, dve_gate, decay_ready, rows_turned, rows_kept_act,
         rows_kept_dve, key_rooted, tables_ready, solved_dve, solved_pool, diag_step, table_scaled, table_turned,
         table_kept_act, table_kept_dve, spread_clear, spread_dve, spread_act, o_summed, o_kept, o_squared,
         o_var, o_rooted, o_inverted, o_normed, o_acted, g_summed, g_kept, gated_s, out_summed,
         residual) = named(nc, mem.ctx, (
            "ab_summed ab_kept gates_turned gates_kept act_gate dve_gate decay_ready rows_turned rows_kept_act "
            "rows_kept_dve key_rooted tables_ready solved_dve solved_pool diag_step table_scaled table_turned "
            "table_kept_act table_kept_dve spread_clear spread_dve spread_act o_summed o_kept o_squared "
            "o_var o_rooted o_inverted o_normed o_acted g_summed g_kept gated out_summed residual"))
        block = ctx.enter_context(nc.Block())
        ACT_GATE, DVE_GATE = 7, 11
        ROW_GROUPS = 2 * L // 4
        TURNS = L // 4
        SOLVE = 2 * (L - 2)
        POOL_SEQ = 1
        DVE_SEQ = SPB - POOL_SEQ

        def b(x):
            return x.rearrange("p (a b) -> p a b", b=L)

        every = [w_in, wo_in, summed_mean, centred_s, squared_s, summed_var, rooted, inverted, normed,
                 pads_clear, projected, raw_copied, shuffled, cosined, sined, kq_ready, v_act, q_squared,
                 scored, v_turned, score_kept, v_kept, lengths_summed, *conv_step, *acted_s,
                 ab_summed, ab_kept, gates_turned, gates_kept, act_gate, dve_gate, decay_ready, rows_turned,
                 rows_kept_act, rows_kept_dve, key_rooted, tables_ready, solved_dve, solved_pool, diag_step, table_scaled,
                 table_turned, table_kept_act, table_kept_dve, spread_clear, spread_dve, spread_act, o_summed,
                 o_kept, o_squared, o_var, o_rooted, o_inverted, o_normed, o_acted, g_summed, g_kept, gated_s,
                 out_summed, residual]

        @block.sync
        def _(sp):
            open_phase(sp, every)
            sp.dma_start(w_qkv, dram["Wqkv"]).then_inc(w_in, 16)
            sp.dma_start(w_ab, dram["Wab"]).then_inc(w_in, 16)
            sp.dma_start(w_g, dram["Wg"]).then_inc(wo_in, 16)
            sp.dma_start(w_o, dram["Wo"]).then_inc(wo_in, 16)

        @block.gpsimd
        def _(pool):
            pool.memset(decay[:], 0.0).then_inc(decay_ready, 1)
            pool.wait_ge(decay_ready, 1 + START)
            dflat = decay.rearrange("p a b c -> p (a b c)")
            for j in range(SPB):
                pool.memset(diagonal(dflat, j), 1.0).then_inc(decay_ready, 1)
            with pool.Fori(0, HALVES) as i:
                for n in range(UNITS):
                    for kind in range(2):
                        pool.wait_ge(shuffled, i * 2 * UNITS + 2 * n + kind + 1 + START)
                        pool.tensor_tensor(b(sine[kind]), b(swapped[kind]),
                                           cst["sin"].unsqueeze(1).broadcast_to([P, SEQ, L]),
                                           ALU.mult).then_inc(sined, 1)
                        if kind == 0:
                            pool.wait_ge(lengths_summed, i * UNITS + n + START)
                            s = acted[n % 3][0]
                            pool.tensor_tensor(q_square, s, s, ALU.mult).then_inc(q_squared, 1)
                pool.wait_ge(act_gate, i * ACT_GATE + ACT_GATE + START)
                for t in range(1, L):
                    pool.wait_ge(decay_ready, i * (L - 1) + SPB + t + START)
                    pool.tensor_tensor(decay[:, t, :, 0:t], decay[:, t - 1, :, 0:t],
                                       g_small[:, 0, :].rearrange("p (j t) -> p j t", j=SPB)[:, :, t:t + 1]
                                       .broadcast_to([P, SPB, t]), ALU.mult).then_inc(decay_ready, 1)
                pool.wait_ge(tables_ready, i + 1 + START)
                tmp = product[:, 768:1024]
                k = 0
                for t in range(L - 2, 0, -1):
                    j, r = slice(DVE_SEQ, SPB), L - 1 - t
                    out = tmp[:, 0:r * POOL_SEQ * t].rearrange("p (r j s) -> p r j s", r=r, j=POOL_SEQ)
                    if k:
                        pool.wait_ge(solved_pool, i * SOLVE + k + START)
                    pool.tensor_tensor(out, g4[:, t + 1:L, j, t:t + 1].broadcast_to([P, r, POOL_SEQ, t]),
                                       a4[:, t:t + 1, j, 0:t].broadcast_to([P, r, POOL_SEQ, t]),
                                       ALU.mult).then_inc(solved_pool, 1)
                    if k == 0:
                        for s in range(2):
                            pool.memset(spread[s], 0.0).then_inc(spread_clear, 1)
                    pool.wait_ge(solved_pool, i * SOLVE + k + 1 + START)
                    pool.tensor_tensor(g4[:, t + 1:L, j, 0:t], g4[:, t + 1:L, j, 0:t], out,
                                       ALU.subtract).then_inc(solved_pool, 1)
                    k += 2

        @block.tensor
        def _(pe):
            pe.wait_ge(w_in, 32 + START)
            with pe.Fori(0, HALVES) as i:
                for a in range(HT):
                    src = bass.ds(i * HALF + a * TILE, TILE)
                    if a == 0:
                        pe.wait_ge(residual, i * SUBS + START)
                    else:
                        pe.wait_ge(centred_s, i * HT + a + START)
                    for k in range(KD):
                        mm = pe.matmul(ps[:, 6, :], cst["mean"], hT[:, k, src], start=(k == 0), stop=(k == KD - 1))
                    mm.then_inc(summed_mean, 1)
                    pe.wait_ge(squared_s, i * HT + a + 1 + START)
                    if a:
                        pe.wait_ge(rooted, i * HT + a + START)
                    for k in range(KD):
                        mm = pe.matmul(ps[:, 5, :], cst["mean"], squared[:, k, :], start=(k == 0), stop=(k == KD - 1))
                    mm.then_inc(summed_var, 1)
                pe.wait_ge(normed, i * HT + HT + START)
                for s in range(SUBS):
                    for k in range(KD):
                        mm = pe.matmul(ps[:, 6, s * 32:s * 32 + 32], xn[:, k, s * P:(s + 1) * P], w_ab[:, k, :],
                                       start=(k == 0), stop=(k == KD - 1))
                mm.then_inc(ab_summed, 1)

                def project(n):
                    a, c = divmod(n, HC)
                    for kind in range(3):
                        if n:
                            pe.wait_ge(raw_copied, i * 3 * UNITS + 3 * (n - 1) + kind + 1 + START)
                        for k in range(KD):
                            mm = pe.matmul(ps[:, kind, :], w_qkv[:, kind, k, c * P:(c + 1) * P],
                                           xn[:, k, a * TILE:(a + 1) * TILE], start=(k == 0), stop=(k == KD - 1))
                        mm.then_inc(projected, 1)

                def compare(n):
                    a, c = divmod(n, HC)
                    pe.wait_ge(q_squared, i * UNITS + n + 1 + START)
                    for s in range(TILE // P):
                        sub = a * (TILE // P) + s
                        mm = pe.matmul(ps[:, 7, sub * HEADS + 2 * c:sub * HEADS + 2 * c + 2],
                                       q_square[:, s * P:(s + 1) * P], cst["pick2"], start=True, stop=True)
                    mm.then_inc(lengths_summed, 1)
                    pe.wait_ge(kq_ready, i * 2 * UNITS + 2 * n + 2 + START)
                    if n:
                        pe.wait_ge(score_kept, i * 2 * UNITS + 2 * n + START)
                        pe.wait_ge(v_kept, i * UNITS + n + START)
                    pe.wait_ge(acted_s[2], i * UNITS + n + 1 + START)
                    for s in range(TILE // P):
                        mm = pe.transpose(ps[:, 5, s * P:(s + 1) * P], acted[n % 3][2][:, s * P:(s + 1) * P],
                                          cst["ident"])
                    mm.then_inc(v_turned, 1)
                    for e in range(2):
                        h = slice(e * DH, e * DH + DH)
                        for q in range(SEQ):
                            sub, j = divmod(q, SPB)
                            mm = pe.matmul(ps[j * L:j * L + L, 3 + e, sub * 2 * L:(sub + 1) * 2 * L],
                                           kq[n % 2][h, 0, q * L:(q + 1) * L],
                                           kq[n % 2][h, :, q * L:(q + 1) * L], start=True, stop=True)
                        mm.then_inc(scored, 1)

                for n in range(UNITS + 2):
                    if n < UNITS:
                        project(n)
                    if n >= 2:
                        compare(n - 2)
                pe.wait_ge(ab_kept, i * 2 + 2 + START)
                for g in range(3):
                    mm = pe.transpose(ps[:, 6, g * P:(g + 1) * P], ab[:, g].rearrange("p a b -> p (a b)"),
                                      cst["ident"])
                mm.then_inc(gates_turned, 1)
                pe.wait_ge(score_kept, (i + 1) * 2 * UNITS + START)
                for g in range(ROW_GROUPS):
                    if g >= 4:
                        which = rows_kept_dve if g % 2 else rows_kept_act
                        pe.wait_ge(which, i * (ROW_GROUPS // 2) + (g - 4) // 2 + 1 + START)
                    for r in range(4):
                        mm = pe.transpose(ps[:, g % 4, r * P:(r + 1) * P],
                                          scores[:, 4 * g + r].rearrange("p a b -> p (a b)"), cst["ident"])
                    mm.then_inc(rows_turned, 1)
                pe.wait_ge(table_scaled, i * (1 + SPB) + 1 + SPB + START)
                for g in range(TURNS):
                    if g >= 4:
                        which = table_kept_dve if g % 2 else table_kept_act
                        pe.wait_ge(which, i * (TURNS // 2) + (g - 4) // 2 + 1 + START)
                    for r in range(4):
                        mm = pe.transpose(ps[:, g % 4, r * P:(r + 1) * P], g_rows[:, 4 * g + r, :], cst["ident"])
                    mm.then_inc(table_turned, 1)
                pe.wait_ge(wo_in, 32 + START)

                def project_out(s):
                    pe.wait_ge(gated_s, i * SUBS + s + 1 + START)
                    if s:
                        pe.wait_ge(residual, i * SUBS + s + START)
                    for m in range(KD):
                        for c in range(HC):
                            mm = pe.matmul(ps[:, 6, m * P:(m + 1) * P], w_o[:, c, m * P:(m + 1) * P],
                                           gated[:, c, :], start=(c == 0), stop=(c == HC - 1))
                    mm.then_inc(out_summed, 1)

                for s in range(SUBS):
                    pe.wait_ge(spread_dve, i * 2 * SUBS + 2 * s + 2 + START)
                    pe.wait_ge(spread_act, i * 2 * SUBS + 2 * s + 2 + START)
                    if s:
                        pe.wait_ge(o_kept, i * SUBS + s + START)
                    for h in range(HEADS):
                        c, e = divmod(h, 2)
                        mm = pe.matmul(ps[e * DH:(e + 1) * DH, c // 4, (c % 4) * P:(c % 4 + 1) * P],
                                       v_rows[:, s, h * DH:(h + 1) * DH], spread[s % 2][:, h, :],
                                       start=True, stop=True)
                    mm.then_inc(o_summed, 1)
                    if s:
                        pe.wait_ge(g_kept, i * SUBS + s + START)
                    for c in range(HC):
                        for k in range(KD):
                            mm = pe.matmul(ps[:, 2 + c // 4, (c % 4) * P:(c % 4 + 1) * P],
                                           w_g[:, k, c * P:(c + 1) * P], xn[:, k, s * P:(s + 1) * P],
                                           start=(k == 0), stop=(k == KD - 1))
                    mm.then_inc(g_summed, 1)
                    pe.wait_ge(o_squared, i * SUBS + s + 1 + START)
                    if s:
                        pe.wait_ge(o_rooted, i * SUBS + s + START)
                    for c in range(2):
                        mm = pe.matmul(ps[:, 4 + c, :], cst["head_mean"], o_sq[:, 4 * c:4 * c + 4, :],
                                       start=True, stop=True)
                    mm.then_inc(o_var, 1)
                    if s:
                        project_out(s - 1)
                project_out(SUBS - 1)

        @block.scalar
        def _(act):
            with act.Fori(0, HALVES) as i:
                for a in range(HT):
                    act.wait_ge(centred_s, i * HT + a + 1 + START)
                    if a:
                        act.wait_ge(summed_var, i * HT + a + START)
                    act.activation(squared, centred, ACT.Square).then_inc(squared_s, 1)
                    act.wait_ge(summed_var, i * HT + a + 1 + START)
                    act.wait_ge(inverted, i * HT + a + START)
                    act.activation(deviation, ps[:, 5, :], ACT.Sqrt, bias=cst["eps5"]).then_inc(rooted, 1)
                act.wait_ge(pads_clear, i + 1 + START)

                def raw(n, kind):
                    c = n % HC
                    act.wait_ge(projected, i * 3 * UNITS + 3 * n + kind + 1 + START)
                    if n:
                        act.wait_ge(conv_step[kind], i * 3 * UNITS + 3 * n + START)
                        act.wait_ge(acted_s[kind], i * UNITS + n + START)
                    act.activation(padded[kind][:, :, CONV - 1:], b(ps[:, kind, :]), ACT.Copy)
                    w = cols["conv"] + (kind * HC + c) * (CONV + 1)
                    act.activation(conv[kind], ps[:, kind, :], ACT.Identity, bias=vec[:, w + CONV:w + CONV + 1],
                                   scale=vec[:, w + CONV - 1:w + CONV]).then_inc(raw_copied, 1)

                def silu(n, kind):
                    act.wait_ge(conv_step[kind], i * 3 * UNITS + 3 * n + 3 + START)
                    if kind == 2:
                        if n >= 3:
                            act.wait_ge(v_turned, i * UNITS + n - 2 + START)
                    elif n >= 3:
                        act.wait_ge(kq_ready, i * 2 * UNITS + 2 * (n - 2) + START)
                        if kind == 0:
                            act.wait_ge(q_squared, i * UNITS + n - 2 + START)
                    act.activation(acted[n % 3][kind], conv[kind], ACT.Silu).then_inc(acted_s[kind], 1)

                def keep(n):
                    a, c = divmod(n, HC)
                    subs = slice(a * (TILE // P), (a + 1) * (TILE // P))
                    act.wait_ge(v_turned, i * UNITS + n + 1 + START)
                    act.activation(v_rows[:, subs, c * P:(c + 1) * P],
                                   ps[:, 5, :].rearrange("p (s c) -> p s c", c=P), ACT.Copy).then_inc(v_kept, 1)
                    for e in range(2):
                        act.wait_ge(scored, i * 2 * UNITS + 2 * n + e + 1 + START)
                        act.activation(scores[:, :, subs, 2 * c + e].rearrange("p r s -> p s r"),
                                       ps[:, 3 + e, 0:256].rearrange("p (s r) -> p s r", r=2 * L),
                                       ACT.Copy).then_inc(score_kept, 1)

                for n in range(UNITS + 2):
                    if n < UNITS:
                        for kind in range(3):
                            raw(n, kind)
                        for kind in range(3):
                            silu(n, kind)
                    if n >= 2:
                        keep(n - 2)

                base = i * ACT_GATE + START
                act.wait_ge(gates_kept, i + 1 + START)
                act.activation(g_small[:, 1, :], gates[:, 0, :], ACT.Sigmoid,
                               bias=vec[:, cols["bb"]:cols["bb"] + 1]).then_inc(act_gate, 1)
                act.wait_ge(dve_gate, i * DVE_GATE + 1 + START)
                act.activation(g_small[:, 2, :], g_small[:, 3, :], ACT.Abs).then_inc(act_gate, 1)
                act.wait_ge(act_gate, base + 2)
                act.activation(g_small[:, 4, :], g_small[:, 2, :], ACT.Exp, scale=-1.0).then_inc(act_gate, 1)
                act.wait_ge(act_gate, base + 3)
                act.activation(g_small[:, 5, :], g_small[:, 4, :], ACT.Ln, bias=cst["one"]).then_inc(act_gate, 1)
                act.activation(nega[:, 0:1], vec[:, cols["A_log"]:cols["A_log"] + 1], ACT.Exp).then_inc(act_gate, 1)
                act.activation(g_small[:, 6, :], gates[:, 2, :], ACT.Sqrt, bias=cst["eps6"]).then_inc(act_gate, 1)
                act.wait_ge(dve_gate, i * DVE_GATE + 3 + START)
                act.activation(g_small[:, 0, :], g_small[:, 7, :], ACT.Exp).then_inc(act_gate, 1)
                for g in range(0, ROW_GROUPS, 2):
                    act.wait_ge(rows_turned, i * ROW_GROUPS + g + 1 + START)
                    act.activation(kq_rows[:, 4 * g:4 * g + 4, :].rearrange("p a b -> p (a b)"), ps[:, g % 4, :],
                                   ACT.Copy).then_inc(rows_kept_act, 1)
                act.wait_ge(diag_step, i * 2 * SPB + SPB + START)
                act.activation(g_small[:, 8, :], g_small[:, 9, :], ACT.Sqrt,
                               bias=cst["eps6"]).then_inc(key_rooted, 1)
                for g in range(0, TURNS, 2):
                    act.wait_ge(table_turned, i * TURNS + g + 1 + START)
                    act.activation(table_rows[:, 4 * g:4 * g + 4].rearrange("p a b c -> p (a b c)"), ps[:, g % 4, :],
                                   ACT.Copy).then_inc(table_kept_act, 1)

                def spread_block(s):
                    if s == 0:
                        act.wait_ge(table_kept_act, i * TURNS // 2 + TURNS // 2 + START)
                        act.wait_ge(table_kept_dve, i * TURNS // 2 + TURNS // 2 + START)
                        act.wait_ge(spread_clear, i * 2 + 2 + START)
                    if s >= 2:
                        act.wait_ge(o_summed, i * SUBS + s - 1 + START)
                    for j in range(2, SPB):
                        q = slice(j * L, j * L + L)
                        act.activation(spread[s % 2][q, :, q], table_rows[q, :, s, :].rearrange("p t h -> p h t"),
                                       ACT.Copy).then_inc(spread_act, 1)

                spread_block(0)
                for s in range(SUBS):
                    act.wait_ge(o_kept, i * SUBS + s + 1 + START)
                    act.activation(o_sq, o_sb, ACT.Square).then_inc(o_squared, 1)
                    act.wait_ge(g_summed, i * SUBS + s + 1 + START)
                    if s >= 2:
                        act.wait_ge(gated_s, i * SUBS + s - 1 + START)
                    act.activation(gate[s % 2].rearrange("p a b -> p (a b)"),
                                   ps[:, 2:4, :].rearrange("p a b -> p (a b)"), ACT.Copy).then_inc(g_kept, 1)
                    act.wait_ge(o_var, i * SUBS + s + 1 + START)
                    if s:
                        act.wait_ge(o_inverted, i * SUBS + s + START)
                    act.activation(o_sd.rearrange("p a b -> p (a b)"), ps[:, 4:6, :].rearrange("p a b -> p (a b)"),
                                   ACT.Sqrt, bias=cst["eps6"]).then_inc(o_rooted, 1)
                    if s + 1 < SUBS:
                        spread_block(s + 1)
                    act.wait_ge(o_normed, i * SUBS + s + 1 + START)
                    act.activation(o_act, o_norm, ACT.Silu).then_inc(o_acted, 1)

        @block.vector
        def _(dve):
            with dve.Fori(0, HALVES) as i:
                for a in range(HT):
                    src = bass.ds(i * HALF + a * TILE, TILE)
                    dve.wait_ge(summed_mean, i * HT + a + 1 + START)
                    if a:
                        dve.wait_ge(normed, i * HT + a + START)
                    dve.tensor_tensor(centred, hT[:, :, src], ps[:, 6:7, :].broadcast_to([P, KD, TILE]),
                                      ALU.subtract).then_inc(centred_s, 1)
                    dve.wait_ge(rooted, i * HT + a + 1 + START)
                    dve.reciprocal(inverse, deviation).then_inc(inverted, 1)
                    dve.wait_ge(inverted, i * HT + a + 1 + START)
                    dve.tensor_tensor(xn[:, :, a * TILE:(a + 1) * TILE], centred,
                                      inverse.unsqueeze(1).broadcast_to([P, KD, TILE]), ALU.mult).then_inc(normed, 1)
                for kind in range(3):
                    ins = dve.memset(padded[kind][:, :, 0:CONV - 1], 0.0)
                ins.then_inc(pads_clear, 1)
                dve.wait_ge(ab_summed, i + 1 + START)
                dve.tensor_copy(ab[:, 0:2].rearrange("p k s h -> p s k h"),
                                ps[:, 6, 0:256].rearrange("p (s k h) -> p s k h", k=2, h=HEADS)
                                ).then_inc(ab_kept, 1)

                def tap(n, kind, j):
                    c = n % HC
                    if j == 0:
                        dve.wait_ge(raw_copied, i * 3 * UNITS + 3 * n + kind + 1 + START)
                    else:
                        dve.wait_ge(conv_step[kind], i * 3 * UNITS + 3 * n + j + START)
                    w = cols["conv"] + (kind * HC + c) * (CONV + 1) + j
                    dve.scalar_tensor_tensor(b(conv[kind]), padded[kind][:, :, j:j + L], vec[:, w:w + 1],
                                             b(conv[kind]), ALU.mult, ALU.add).then_inc(conv_step[kind], 1)

                def rotate(n):
                    for kind in range(2):
                        s = acted[n % 3][kind]
                        dve.wait_ge(acted_s[kind], i * UNITS + n + 1 + START)
                        if n:
                            dve.wait_ge(kq_ready, i * 2 * UNITS + 2 * (n - 1) + kind + 1 + START)
                        dve.tensor_tensor(b(cosine[kind]), b(s), cst["cos"].unsqueeze(1).broadcast_to([P, SEQ, L]),
                                          ALU.mult).then_inc(cosined, 1)
                        dve.stream_shuffle(swapped[kind], s, [q ^ 1 for q in range(32)]).then_inc(shuffled, 1)

                def add_rotated(n):
                    if n >= 2:
                        dve.wait_ge(scored, i * 2 * UNITS + 2 * (n - 1) + START)
                    for kind in range(2):
                        dve.wait_ge(cosined, i * 2 * UNITS + 2 * n + kind + 1 + START)
                        dve.wait_ge(sined, i * 2 * UNITS + 2 * n + kind + 1 + START)
                        dve.tensor_tensor(kq[n % 2][:, 1 - kind, :], cosine[kind], sine[kind],
                                          ALU.add).then_inc(kq_ready, 1)

                for n in range(UNITS + 1):
                    if n < UNITS:
                        for j in range(CONV - 1):
                            for kind in range(2):
                                tap(n, kind, j)
                    if n >= 1:
                        rotate(n - 1)
                    if n < UNITS:
                        for j in range(CONV - 1):
                            tap(n, 2, j)
                    if n >= 1:
                        add_rotated(n - 1)

                dve.wait_ge(lengths_summed, (i + 1) * UNITS + START)
                dve.tensor_copy(ab[:, 2].rearrange("p a b -> p (a b)"), ps[:, 7, 0:P]).then_inc(ab_kept, 1)
                dve.wait_ge(gates_turned, i + 1 + START)
                dve.tensor_copy(gates.rearrange("p a b -> p (a b)"), ps[:, 6, 0:3 * P]).then_inc(gates_kept, 1)
                dve.wait_ge(gates_kept, i + 1 + START)
                base = i * DVE_GATE + START
                c = cols["dt"]
                dve.tensor_scalar(g_small[:, 3, :], gates[:, 1, :], vec[:, c:c + 1], vec[:, c + 1:c + 2],
                                  ALU.add, ALU.add).then_inc(dve_gate, 1)
                dve.wait_ge(dve_gate, base + 1)
                dve.wait_ge(act_gate, i * ACT_GATE + 5 + START)
                dve.scalar_tensor_tensor(g_small[:, 5, :], g_small[:, 3, :], 0.0, g_small[:, 5, :],
                                         ALU.max, ALU.add).then_inc(dve_gate, 1)
                dve.wait_ge(dve_gate, base + 2)
                dve.tensor_scalar(g_small[:, 7, :], g_small[:, 5, :], nega[:, 0:1], -1.0,
                                  ALU.mult, ALU.mult).then_inc(dve_gate, 1)
                dve.wait_ge(act_gate, i * ACT_GATE + 6 + START)
                dve.reciprocal(g_small[:, 6, :], g_small[:, 6, :]).then_inc(dve_gate, 1)
                for g in range(1, ROW_GROUPS, 2):
                    dve.wait_ge(rows_turned, i * ROW_GROUPS + g + 1 + START)
                    dve.tensor_copy(kq_rows[:, 4 * g:4 * g + 4, :].rearrange("p a b -> p (a b)"),
                                    ps[:, g % 4, :]).then_inc(rows_kept_dve, 1)
                dve.wait_ge(rows_kept_act, (i + 1) * (ROW_GROUPS // 2) + START)
                dve.wait_ge(rows_kept_dve, (i + 1) * (ROW_GROUPS // 2) + START)
                for j in range(SPB):
                    dve.tensor_copy(g_small[:, 9, j * L:(j + 1) * L], diagonal(k_flat, j)).then_inc(diag_step, 1)
                for j in range(SPB):
                    dve.tensor_copy(g_small[:, 10, j * L:(j + 1) * L], diagonal(q_flat, j)).then_inc(diag_step, 1)
                dve.wait_ge(key_rooted, i + 1 + START)
                dve.reciprocal(g_small[:, 8, :], g_small[:, 8, :]).then_inc(dve_gate, 1)
                dve.wait_ge(dve_gate, base + 5)
                dve.tensor_tensor(g_small[:, 11, :], g_small[:, 1, :], g_small[:, 8, :],
                                  ALU.mult).then_inc(dve_gate, 1)
                dve.wait_ge(dve_gate, base + 6)
                dve.tensor_tensor(g_small[:, 2, :], g_small[:, 11, :], g_small[:, 8, :],
                                  ALU.mult).then_inc(dve_gate, 1)
                dve.wait_ge(diag_step, i * 2 * SPB + 2 * SPB + START)
                dve.scalar_tensor_tensor(g_small[:, 10, :], g_small[:, 10, :], vec[:, cols["Dp"]:cols["Dp"] + 1],
                                         g_small[:, 8, :], ALU.mult, ALU.mult).then_inc(dve_gate, 1)
                dve.wait_ge(dve_gate, base + 8)
                dve.tensor_tensor(g_small[:, 10, :], g_small[:, 10, :], g_small[:, 6, :],
                                  ALU.mult).then_inc(dve_gate, 1)
                dve.wait_ge(decay_ready, (i + 1) * (L - 1) + SPB + 1 + START)
                d3 = decay.rearrange("p a b c -> p a (b c)")

                def by_row(x):
                    return x.rearrange("p (j t) -> p t j", j=SPB)

                dve.tensor_tensor(a_rows, a_rows, d3, ALU.mult).then_inc(dve_gate, 1)
                dve.tensor_tensor(g_rows[:, 1:L, :], g_rows[:, 1:L, :], d3[:, 0:L - 1, :], ALU.mult)
                dve.memset(g_rows[:, 0, :], 0.0).then_inc(dve_gate, 1)
                dve.wait_ge(dve_gate, base + 11)
                dve.tensor_tensor(a4, a4, by_row(g_small[:, 2, :]).unsqueeze(3).broadcast_to([P, L, SPB, L]), ALU.mult)
                dve.tensor_tensor(g4, g4, by_row(g_small[:, 6, :]).unsqueeze(3).broadcast_to([P, L, SPB, L]),
                                  ALU.mult).then_inc(tables_ready, 1)
                dve.wait_ge(tables_ready, i + 1 + START)
                tmp = product[:, 0:768]
                k = 0
                for t in range(L - 2, 0, -1):
                    j, r = slice(0, DVE_SEQ), L - 1 - t
                    out = tmp[:, 0:r * DVE_SEQ * t].rearrange("p (r j s) -> p r j s", r=r, j=DVE_SEQ)
                    if k:
                        dve.wait_ge(solved_dve, i * SOLVE + k + START)
                    dve.tensor_tensor(out, g4[:, t + 1:L, j, t:t + 1].broadcast_to([P, r, DVE_SEQ, t]),
                                      a4[:, t:t + 1, j, 0:t].broadcast_to([P, r, DVE_SEQ, t]),
                                      ALU.mult).then_inc(solved_dve, 1)
                    dve.wait_ge(solved_dve, i * SOLVE + k + 1 + START)
                    dve.tensor_tensor(g4[:, t + 1:L, j, 0:t], g4[:, t + 1:L, j, 0:t], out,
                                      ALU.subtract).then_inc(solved_dve, 1)
                    k += 2
                dve.wait_ge(solved_dve, i * SOLVE + SOLVE + START)
                dve.wait_ge(solved_pool, i * SOLVE + SOLVE + START)
                dve.tensor_tensor(g_rows, g_rows, g_small[:, 11:12, :].broadcast_to([P, L, P]),
                                  ALU.mult).then_inc(table_scaled, 1)
                dve.wait_ge(table_scaled, i * (1 + SPB) + 1 + START)
                for j in range(SPB):
                    dve.tensor_copy(diagonal(q_flat, j), g_small[:, 10, j * L:(j + 1) * L]).then_inc(table_scaled, 1)
                for g in range(1, TURNS, 2):
                    dve.wait_ge(table_turned, i * TURNS + g + 1 + START)
                    dve.tensor_copy(table_rows[:, 4 * g:4 * g + 4].rearrange("p a b c -> p (a b c)"),
                                    ps[:, g % 4, :]).then_inc(table_kept_dve, 1)

                def spread_block(s):
                    if s == 0:
                        dve.wait_ge(table_kept_act, i * TURNS // 2 + TURNS // 2 + START)
                        dve.wait_ge(table_kept_dve, i * TURNS // 2 + TURNS // 2 + START)
                        dve.wait_ge(spread_clear, i * 2 + 2 + START)
                    if s >= 2:
                        dve.wait_ge(o_summed, i * SUBS + s - 1 + START)
                    for j in range(2):
                        q = slice(j * L, j * L + L)
                        dve.tensor_copy(spread[s % 2][q, :, q],
                                        table_rows[q, :, s, :].rearrange("p t h -> p h t")).then_inc(spread_dve, 1)

                def add_residual(s):
                    dve.wait_ge(out_summed, i * SUBS + s + 1 + START)
                    dst = hT[:, :, bass.ds(i * HALF + s * P, P)]
                    dve.tensor_tensor(dst, dst, ps[:, 6, 0:KD * P].rearrange("p (a b) -> p a b", a=KD),
                                      ALU.add).then_inc(residual, 1)

                spread_block(0)
                for s in range(SUBS):
                    dve.wait_ge(o_summed, i * SUBS + s + 1 + START)
                    if s:
                        dve.wait_ge(o_squared, i * SUBS + s + START)
                        dve.wait_ge(o_normed, i * SUBS + s + START)
                    dve.tensor_copy(o_sb.rearrange("p a b -> p (a b)"),
                                    ps[:, 0:2, :].rearrange("p a b -> p (a b)")).then_inc(o_kept, 1)
                    if s + 1 < SUBS:
                        spread_block(s + 1)
                    dve.wait_ge(o_rooted, i * SUBS + s + 1 + START)
                    dve.reciprocal(o_inv, o_sd).then_inc(o_inverted, 1)
                    dve.wait_ge(o_inverted, i * SUBS + s + 1 + START)
                    if s:
                        dve.wait_ge(o_acted, i * SUBS + s + START)
                    dve.scalar_tensor_tensor(o_norm, o_sb, vec[:, cols["onorm"]:cols["onorm"] + 1], o_inv,
                                             ALU.mult, ALU.mult).then_inc(o_normed, 1)
                    if s:
                        add_residual(s - 1)
                    dve.wait_ge(o_acted, i * SUBS + s + 1 + START)
                    dve.tensor_tensor(gated, o_act, gate[s % 2], ALU.mult).then_inc(gated_s, 1)
                add_residual(SUBS - 1)


class Norm:

    def __init__(self, nc, mem, ps, mean_bank, var_bank):
        self.mem, self.ps, self.mean_bank, self.var_bank = mem, ps, mean_bank, var_bank
        self.centred, self.squared = mem.part([P, KD, TILE]), mem.part([P, KD, TILE])
        self.root = mem.part([P, TILE])
        self.xn = mem.part([P, KD, TILE])
        if mem.norm_sems is None:
            mem.norm_sems = named(nc, mem.ctx, "mean_summed norm_centred norm_squared var_summed norm_rooted "
                                  "norm_inverted norm_normed")
            self.opened = mem.norm_sems
        else:
            self.opened = []
        (self.mean_summed, self.is_centred, self.is_squared, self.var_summed, self.is_rooted, self.is_inverted,
         self.is_normed) = mem.norm_sems
        self.base = START + TILES * mem.norms
        mem.norms += 1

    def mean(self, pe, i):
        for k in range(KD):
            mm = pe.matmul(self.ps[:, self.mean_bank, :], self.mem.cst["mean"],
                           self.mem.hT[:, k, bass.ds(i * TILE, TILE)], start=(k == 0), stop=(k == KD - 1))
        mm.then_inc(self.mean_summed, 1)

    def variance(self, pe, i):
        pe.wait_ge(self.is_squared, i + 1 + self.base)
        for k in range(KD):
            mm = pe.matmul(self.ps[:, self.var_bank, :], self.mem.cst["mean"], self.squared[:, k, :],
                           start=(k == 0), stop=(k == KD - 1))
        mm.then_inc(self.var_summed, 1)

    def centre(self, dve, i):
        dve.wait_ge(self.mean_summed, i + 1 + self.base)
        dve.tensor_tensor(self.centred, self.mem.hT[:, :, bass.ds(i * TILE, TILE)],
                          self.ps[:, self.mean_bank:self.mean_bank + 1, :].broadcast_to([P, KD, TILE]),
                          ALU.subtract).then_inc(self.is_centred, 1)

    def scale(self, dve, i):
        dve.wait_ge(self.is_rooted, i + 1 + self.base)
        dve.reciprocal(self.root, self.root).then_inc(self.is_inverted, 1)
        dve.wait_ge(self.is_inverted, i + 1 + self.base)
        dve.tensor_tensor(self.xn, self.centred, self.root.unsqueeze(1).broadcast_to([P, KD, TILE]),
                          ALU.mult).then_inc(self.is_normed, 1)

    def square(self, act, i):
        act.wait_ge(self.is_centred, i + 1 + self.base)
        act.activation(self.squared, self.centred, ACT.Square).then_inc(self.is_squared, 1)

    def take_root(self, act, i):
        act.wait_ge(self.var_summed, i + 1 + self.base)
        act.activation(self.root, self.ps[:, self.var_bank, :], ACT.Sqrt,
                       bias=self.mem.cst["eps5"]).then_inc(self.is_rooted, 1)


EXPERTS, RANK, FFN = 8, 64, 512
PAIRS = EXPERTS // 2
FC = FFN // P


def phase_experts(nc, mem, dram):
    hT, cst = mem.hT, mem.cst
    part = mem.part
    w_a = part([P, KD, EXPERTS * RANK])
    w_b = part([P, PAIRS, FFN])
    w_up = part([P, EXPERTS, KD, FFN])
    w_down = part([P, EXPERTS, FC, D])
    ghid = part([P, PAIRS, TILE])
    ghid_sq = part([P, PAIRS, TILE])
    silus = [part([P, TILE]) for _ in range(2)]
    acts = [part([P, TILE]) for _ in range(2)]
    weighted = [part([P, KD, TILE]) for _ in range(2)]
    SUBT = TILE // P
    score = part([P, SUBT, EXPERTS])
    score2, place = part([P, SUBT, EXPERTS]), part([P, SUBT, EXPERTS])
    top = part([P, SUBT, 2])
    first = part([P, SUBT, 1])
    gap, one_plus, share1, share2 = (part([P, SUBT, 1]) for _ in range(4))
    hot1, hot2 = part([P, SUBT, EXPERTS]), part([P, SUBT, EXPERTS])
    share = part([P, SUBT, EXPERTS])
    shareT = part([EXPERTS, TILE])
    one_row = part([EXPERTS, EXPERTS, P])
    with ExitStack() as ctx:
        ps = ctx.enter_context(nc.psum_tensor("ps_experts", [P, 8, 512], F32))
        norm = Norm(nc, mem, ps, 6, 7)
        sems = (wa_in, hid_summed, hid_kept, hid_squared, score_summed, score_rooted, route, gap_exp, share_ready,
                share_turned, shareT_ready, share_spread, x_weighted, gate_summed, up_summed, silu_ready,
                act_ready, down_step, rows_made, residual) = named(nc, mem.ctx, (
                    "wa_in moe_hid_summed moe_hid_kept moe_hid_squared score_summed score_rooted route gap_exp "
                    "share_ready share_turned shareT_ready share_spread x_weighted gate_summed up_summed silu_ready "
                    "act_ready down_step moe_rows_made moe_residual"))
        expert_in = named(nc, mem.ctx, " ".join(f"expert_in_{e}" for e in range(EXPERTS)))
        block = ctx.enter_context(nc.Block())
        STEPS = EXPERTS * FC
        ROUTE = 17

        @block.sync
        def _(sp):
            open_phase(sp, [*sems, *expert_in, *norm.opened])
            sp.dma_start(w_a, dram["W_A"]).then_inc(wa_in, 16)
            sp.dma_start(w_b, dram["W_B"]).then_inc(wa_in, 16)
            for e in range(EXPERTS):
                sp.dma_start(w_up[:, e], dram["W_up"][:, e]).then_inc(expert_in[e], 16)
                sp.dma_start(w_down[:, e], dram["W_down"][:, e]).then_inc(expert_in[e], 16)

        @block.gpsimd
        def _(pool):
            pool.tensor_copy(one_row, cst["ident"][0:EXPERTS, 0:EXPERTS].unsqueeze(2).broadcast_to(
                [EXPERTS, EXPERTS, P])).then_inc(rows_made, 1)

        @block.tensor
        def _(pe):
            pe.wait_ge(wa_in, 32 + START)
            pe.wait_ge(rows_made, 1 + START)
            with pe.Fori(0, TILES) as i:
                norm.mean(pe, i)
                norm.variance(pe, i)
                pe.wait_ge(norm.is_normed, i + 1 + norm.base)
                for g in range(PAIRS):
                    for k in range(KD):
                        mm = pe.matmul(ps[:, g, :], w_a[:, k, g * P:(g + 1) * P], norm.xn[:, k, :],
                                       start=(k == 0), stop=(k == KD - 1))
                    mm.then_inc(hid_summed, 1)
                pe.wait_ge(hid_squared, i + 1 + START)
                for s in range(SUBT):
                    for g in range(PAIRS):
                        mm = pe.matmul(ps[:, 6, s * EXPERTS:(s + 1) * EXPERTS], ghid_sq[:, g, s * P:(s + 1) * P],
                                       cst["expert_of"][:, g * EXPERTS:(g + 1) * EXPERTS],
                                       start=(g == 0), stop=(g == PAIRS - 1))
                mm.then_inc(score_summed, 1)
                pe.wait_ge(share_ready, i + 1 + START)
                for s in range(SUBT):
                    mm = pe.transpose(ps[0:EXPERTS, 7, s * P:(s + 1) * P], share[:, s, :], cst["ident"])
                mm.then_inc(share_turned, 1)

                def spread(e):
                    if e:
                        pe.wait_ge(x_weighted, i * EXPERTS + e + START)
                    pe.matmul(ps[:, 7, :], one_row[:, e, :], shareT,
                              start=True, stop=True).then_inc(share_spread, 1)

                def up(q):
                    e, m = divmod(q, FC)
                    h = slice((e % 2) * RANK, (e % 2) * RANK + RANK)
                    if q >= 2:
                        pe.wait_ge(silu_ready, i * STEPS + q - 1 + START)
                    pe.matmul(ps[:, q % 2, :], w_b[h, e // 2, m * P:(m + 1) * P], ghid[h, e // 2, :],
                              start=True, stop=True).then_inc(gate_summed, 1)
                    if q >= 2:
                        pe.wait_ge(act_ready, i * STEPS + q - 1 + START)
                    if m == 0:
                        pe.wait_ge(x_weighted, i * EXPERTS + e + 1 + START)
                        pe.wait_ge(expert_in[e], 32 + START)
                    for k in range(KD):
                        mm = pe.matmul(ps[:, 2 + q % 2, :], w_up[:, e, k, m * P:(m + 1) * P],
                                       weighted[e % 2][:, k, :], start=(k == 0), stop=(k == KD - 1))
                    mm.then_inc(up_summed, 1)

                def down(q):
                    e, m = divmod(q, FC)
                    pe.wait_ge(act_ready, i * STEPS + q + 1 + START)
                    for c in range(KD):
                        mm = pe.matmul(ps[:, 4 + c, :], w_down[:, e, m, c * P:(c + 1) * P], acts[q % 2],
                                       start=(q == 0), stop=(q == STEPS - 1))
                    mm.then_inc(down_step, 1)

                pe.wait_ge(shareT_ready, i + 1 + START)
                spread(0)
                for q in range(STEPS + 1):
                    if q < STEPS:
                        up(q)
                        if q % FC == 1 and q // FC + 1 < EXPERTS:
                            spread(q // FC + 1)
                    if q == 1:
                        pe.wait_ge(residual, i + START)
                    if q:
                        down(q - 1)

        @block.scalar
        def _(act):
            with act.Fori(0, TILES) as i:
                norm.square(act, i)
                norm.take_root(act, i)
                for g in range(PAIRS):
                    act.wait_ge(hid_summed, i * PAIRS + g + 1 + START)
                    act.activation(ghid[:, g, :], ps[:, g, :], ACT.Copy).then_inc(hid_kept, 1)
                act.wait_ge(hid_kept, (i + 1) * PAIRS + START)
                act.activation(ghid_sq, ghid, ACT.Square).then_inc(hid_squared, 1)
                act.wait_ge(score_summed, i + 1 + START)
                act.activation(score.rearrange("p a b -> p (a b)"), ps[:, 6, 0:SUBT * EXPERTS],
                               ACT.Sqrt).then_inc(score_rooted, 1)
                act.wait_ge(route, i * ROUTE + 12 + START)
                act.activation(share2, gap, ACT.Exp).then_inc(gap_exp, 1)
                for q in range(STEPS):
                    act.wait_ge(gate_summed, i * STEPS + q + 1 + START)
                    if q >= 2:
                        act.wait_ge(act_ready, i * STEPS + q - 1 + START)
                    act.activation(silus[q % 2], ps[:, q % 2, :], ACT.Silu).then_inc(silu_ready, 1)

        @block.vector
        def _(dve):
            with dve.Fori(0, TILES) as i:
                norm.centre(dve, i)
                norm.scale(dve, i)
                dve.wait_ge(score_rooted, i + 1 + START)
                step = i * ROUTE + START
                number = cst["number"].unsqueeze(1).broadcast_to([P, SUBT, EXPERTS])
                wide = [P, SUBT, EXPERTS]
                k = 0
                for j, (left, hot) in enumerate(((score, hot1), (score2, hot2))):
                    dve.tensor_reduce(top[:, :, j:j + 1], left, AX.X, ALU.max).then_inc(route, 1)
                    dve.wait_ge(route, step + k + 1)
                    dve.tensor_tensor(hot, left, top[:, :, j:j + 1].broadcast_to(wide), ALU.is_equal).then_inc(route, 1)
                    dve.wait_ge(route, step + k + 2)
                    dve.tensor_tensor(place, hot, number, ALU.mult).then_inc(route, 1)
                    dve.wait_ge(route, step + k + 3)
                    dve.tensor_reduce(first, place, AX.X, ALU.min).then_inc(route, 1)
                    dve.wait_ge(route, step + k + 4)
                    dve.tensor_tensor(hot, number, first.broadcast_to(wide), ALU.is_equal).then_inc(route, 1)
                    if j == 0:
                        dve.wait_ge(route, step + k + 5)
                        dve.scalar_tensor_tensor(score2, hot1, -1e38, score, ALU.mult, ALU.add).then_inc(route, 1)
                        dve.wait_ge(route, step + k + 6)
                        k += 6
                dve.tensor_tensor(gap, top[:, :, 1:2], top[:, :, 0:1], ALU.subtract).then_inc(route, 1)
                dve.wait_ge(gap_exp, i + 1 + START)
                dve.tensor_scalar(one_plus, share2, 1.0, None, ALU.add).then_inc(route, 1)
                dve.wait_ge(route, step + 13)
                dve.reciprocal(share1, one_plus).then_inc(route, 1)
                dve.wait_ge(route, step + 14)
                dve.tensor_tensor(share2, share2, share1, ALU.mult).then_inc(route, 1)
                dve.tensor_tensor(hot1, hot1, share1.broadcast_to(wide), ALU.mult).then_inc(route, 1)
                dve.wait_ge(route, step + 16)
                dve.tensor_tensor(hot2, hot2, share2.broadcast_to(wide), ALU.mult).then_inc(route, 1)
                dve.wait_ge(route, step + 17)
                dve.tensor_tensor(share, hot1, hot2, ALU.add).then_inc(share_ready, 1)
                dve.wait_ge(share_turned, i + 1 + START)
                dve.tensor_copy(shareT, ps[0:EXPERTS, 7, :]).then_inc(shareT_ready, 1)

                def weight(e):
                    dve.wait_ge(share_spread, i * EXPERTS + e + 1 + START)
                    if e >= 2:
                        dve.wait_ge(up_summed, i * STEPS + (e - 1) * FC + START)
                    dve.tensor_tensor(weighted[e % 2], norm.xn, ps[:, 7:8, :].broadcast_to([P, KD, TILE]),
                                      ALU.mult).then_inc(x_weighted, 1)

                weight(0)
                for q in range(STEPS):
                    dve.wait_ge(silu_ready, i * STEPS + q + 1 + START)
                    dve.wait_ge(up_summed, i * STEPS + q + 1 + START)
                    if q >= 2:
                        dve.wait_ge(down_step, i * STEPS + q - 1 + START)
                    dve.tensor_tensor(acts[q % 2], silus[q % 2], ps[:, 2 + q % 2, :], ALU.mult).then_inc(act_ready, 1)
                    if q % FC == 1 and q // FC + 1 < EXPERTS:
                        weight(q // FC + 1)
                dve.wait_ge(down_step, (i + 1) * STEPS + START)
                dst = hT[:, :, bass.ds(i * TILE, TILE)]
                dve.tensor_tensor(dst, dst, ps[:, 4:6, :], ALU.add).then_inc(residual, 1)


INNER1, STATES, DT_RANK = 512, 16, 16
IC = INNER1 // P
DBC = DT_RANK + 2 * STATES


def phase_state_space(nc, mem, dram):
    hT, vec, cols, cst = mem.hT, mem.vec, mem.cols, mem.cst
    part = mem.part
    w_in = part([P, KD, 2 * INNER1])
    w_x = part([P, IC, DBC])
    w_dt = part([DT_RANK, INNER1])
    w_out = part([P, IC, D])
    one_row = part([DBC, 2 * STATES, P])
    neg_a = part([P, IC * STATES])
    padded = part([P, IC * SEQ, L + CONV - 1])
    u = part([P, IC, TILE])
    conv = part([P, IC, TILE])
    gate = part([P, IC, TILE])
    dbc = part([DBC, TILE])
    z = part([P, IC, TILE])
    soft = part([P, IC, TILE])
    delta_u = part([P, IC, TILE])
    factor = [part([P, IC, TILE]) for _ in range(2)]
    state = [part([P, IC, TILE]) for _ in range(2)]
    c_rows = [part([P, TILE]) for _ in range(2)]
    read = [part([P, IC, TILE]) for _ in range(2)]
    y = conv

    def b(x):
        return x.rearrange("p (a b) -> p a b", b=L)

    with ExitStack() as ctx:
        ps = ctx.enter_context(nc.psum_tensor("ps_state_space", [P, 8, 512], F32))
        norm = Norm(nc, mem, ps, 6, 7)
        sems = (weights_in, a_exp, a_neg, rows_made, pads_clear, x_summed, x_copied, conv_step, u_ready, gate_summed,
                gate_ready, dbc_summed, dbc_ready, dt_summed, z_ready, abs_ready, exp_ready, ln_ready, delta_ready,
                du_ready, starts_cut, b_spread, c_spread, c_kept, factor_ready, input_ready, state_ready,
                read_ready, y_summed, y_added, y_gated, out_summed, residual) = named(nc, mem.ctx, (
                    "ssm_weights_in a_exp a_neg rows_made ssm_pads_clear x_summed x_copied ssm_conv_step u_ready "
                    "ssm_gate_summed ssm_gate_ready dbc_summed dbc_ready dt_summed z_ready abs_ready exp_ready "
                    "ln_ready delta_ready du_ready starts_cut b_spread c_spread c_kept factor_ready input_ready "
                    "state_ready read_ready y_summed y_added y_gated ssm_out_summed ssm_residual"))
        block = ctx.enter_context(nc.Block())
        TAPS = (CONV - 1) * IC

        @block.sync
        def _(sp):
            open_phase(sp, [*sems, *norm.opened])
            sp.dma_start(w_in, dram["W_in"]).then_inc(weights_in, 16)
            sp.dma_start(w_x, dram["W_x"]).then_inc(weights_in, 16)
            sp.dma_start(w_dt, dram["W_dt"]).then_inc(weights_in, 16)
            sp.dma_start(w_out, dram["W_out"]).then_inc(weights_in, 16)

        @block.gpsimd
        def _(pool):
            pool.memset(padded[:, :, 0:CONV - 1], 0.0).then_inc(pads_clear, 1)
            pool.tensor_copy(one_row, cst["ident"][0:DBC, DT_RANK:DBC].unsqueeze(2).broadcast_to(
                [DBC, 2 * STATES, P])).then_inc(rows_made, 1)
            with pool.Fori(0, TILES) as i:
                for n in range(STATES):
                    pool.wait_ge(c_kept, i * STATES + n + 1 + START)
                    pool.wait_ge(state_ready, i * STATES + n + 1 + START)
                    if n >= 2:
                        pool.wait_ge(y_summed, i * STATES + n - 1 + START)
                    pool.tensor_tensor(read[n % 2], state[n % 2], c_rows[n % 2].unsqueeze(1).broadcast_to(
                        [P, IC, TILE]), ALU.mult).then_inc(read_ready, 1)

        @block.tensor
        def _(pe):
            pe.wait_ge(weights_in, 64 + START)
            pe.wait_ge(rows_made, 1 + START)
            with pe.Fori(0, TILES) as i:
                norm.mean(pe, i)
                norm.variance(pe, i)
                pe.wait_ge(norm.is_normed, i + 1 + norm.base)
                pe.wait_ge(y_added, i * IC + START)
                for m in range(2 * IC):
                    if m >= IC:
                        pe.wait_ge(x_copied, i * IC + m - IC + 1 + START)
                    for k in range(KD):
                        mm = pe.matmul(ps[:, m % IC, :], w_in[:, k, m * P:(m + 1) * P], norm.xn[:, k, :],
                                       start=(k == 0), stop=(k == KD - 1))
                    mm.then_inc(x_summed if m < IC else gate_summed, 1)
                pe.wait_ge(u_ready, (i + 1) * IC + START)
                pe.wait_ge(residual, i + START)
                for k in range(IC):
                    mm = pe.matmul(ps[0:DBC, 4, :], w_x[:, k, :], u[:, k, :], start=(k == 0), stop=(k == IC - 1))
                mm.then_inc(dbc_summed, 1)
                pe.wait_ge(gate_ready, (i + 1) * IC + START)
                pe.wait_ge(dbc_ready, i + 1 + START)
                for m in range(IC):
                    pe.matmul(ps[:, m, :], w_dt[:, m * P:(m + 1) * P], dbc[0:DT_RANK, :],
                              start=True, stop=True).then_inc(dt_summed, 1)

                def spread(n):
                    if n:
                        pe.wait_ge(input_ready, i * STATES + n + START)
                    pe.matmul(ps[:, 4, :], one_row[:, n, :], dbc, start=True, stop=True).then_inc(b_spread, 1)
                    if n:
                        pe.wait_ge(c_kept, i * STATES + n + START)
                    pe.matmul(ps[:, 5, :], one_row[:, STATES + n, :], dbc, start=True, stop=True).then_inc(c_spread, 1)

                def gather(n):
                    pe.wait_ge(read_ready, i * STATES + n + 1 + START)
                    if n == 0:
                        pe.wait_ge(z_ready, (i + 1) * IC + START)
                    for c in range(IC):
                        mm = pe.matmul(ps[:, c, :], cst["ident"], read[n % 2][:, c, :],
                                       start=(n == 0), stop=(n == STATES - 1))
                    mm.then_inc(y_summed, 1)

                for n in range(STATES + 1):
                    if n < STATES:
                        spread(n)
                    if n:
                        gather(n - 1)
                pe.wait_ge(y_gated, i + 1 + START)
                for m in range(KD):
                    for k in range(IC):
                        mm = pe.matmul(ps[:, 4 + m, :], w_out[:, k, m * P:(m + 1) * P], y[:, k, :],
                                       start=(k == 0), stop=(k == IC - 1))
                mm.then_inc(out_summed, 1)

        @block.scalar
        def _(act):
            c = cols["ssm_A_log"]
            act.activation(neg_a, vec[:, c:c + IC * STATES], ACT.Exp).then_inc(a_exp, 1)
            act.wait_ge(pads_clear, 1 + START)
            with act.Fori(0, TILES) as i:
                norm.square(act, i)
                norm.take_root(act, i)
                for c in range(IC):
                    act.wait_ge(x_summed, i * IC + c + 1 + START)
                    if c == 0:
                        act.wait_ge(out_summed, i + START)
                    w = cols["ssm_conv"] + c * (CONV + 1)
                    act.activation(padded[:, c * SEQ:(c + 1) * SEQ, CONV - 1:], b(ps[:, c, :]), ACT.Copy)
                    act.activation(conv[:, c, :], ps[:, c, :], ACT.Identity, bias=vec[:, w + CONV:w + CONV + 1],
                                   scale=vec[:, w + CONV - 1:w + CONV]).then_inc(x_copied, 1)
                for c in range(IC):
                    act.wait_ge(gate_summed, i * IC + c + 1 + START)
                    act.activation(gate[:, c, :], ps[:, c, :], ACT.Silu).then_inc(gate_ready, 1)
                for c in range(IC):
                    act.wait_ge(conv_step, i * TAPS + (CONV - 2) * IC + c + 1 + START)
                    act.activation(u[:, c, :], conv[:, c, :], ACT.Silu).then_inc(u_ready, 1)
                act.wait_ge(dbc_summed, i + 1 + START)
                act.activation(dbc, ps[0:DBC, 4, :], ACT.Copy).then_inc(dbc_ready, 1)
                for c in range(IC):
                    act.wait_ge(dt_summed, i * IC + c + 1 + START)
                    w = cols["ssm_b_dt"] + c
                    act.activation(z[:, c, :], ps[:, c, :], ACT.Identity, bias=vec[:, w:w + 1]).then_inc(z_ready, 1)
                act.wait_ge(z_ready, (i + 1) * IC + START)
                act.activation(soft, z, ACT.Abs).then_inc(abs_ready, 1)
                act.wait_ge(abs_ready, i + 1 + START)
                act.activation(soft, soft, ACT.Exp, scale=-1.0).then_inc(exp_ready, 1)
                act.wait_ge(exp_ready, i + 1 + START)
                act.activation(soft, soft, ACT.Ln, bias=cst["one"]).then_inc(ln_ready, 1)
                act.wait_ge(a_neg, 1 + START)
                for n in range(STATES):
                    if n == 0:
                        act.wait_ge(starts_cut, i + 1 + START)
                    if n >= 2:
                        act.wait_ge(state_ready, i * STATES + n - 1 + START)
                    for c in range(IC):
                        w = c * STATES + n
                        act.activation(factor[n % 2][:, c, :], z[:, c, :], ACT.Exp,
                                       scale=neg_a[:, w:w + 1]).then_inc(factor_ready, 1)
                    act.wait_ge(c_spread, i * STATES + n + 1 + START)
                    if n >= 2:
                        act.wait_ge(read_ready, i * STATES + n - 1 + START)
                    act.activation(c_rows[n % 2], ps[:, 5, :], ACT.Copy).then_inc(c_kept, 1)

        @block.vector
        def _(dve):
            dve.wait_ge(a_exp, 1 + START)
            dve.tensor_scalar(neg_a, neg_a, -1.0, None, ALU.mult).then_inc(a_neg, 1)
            with dve.Fori(0, TILES) as i:
                norm.centre(dve, i)
                norm.scale(dve, i)
                for j in range(CONV - 1):
                    for c in range(IC):
                        if j == 0:
                            dve.wait_ge(x_copied, i * IC + c + 1 + START)
                        else:
                            dve.wait_ge(conv_step, i * TAPS + (j - 1) * IC + c + 1 + START)
                        w = cols["ssm_conv"] + c * (CONV + 1) + j
                        dve.scalar_tensor_tensor(b(conv[:, c, :]), padded[:, c * SEQ:(c + 1) * SEQ, j:j + L],
                                                 vec[:, w:w + 1], b(conv[:, c, :]), ALU.mult,
                                                 ALU.add).then_inc(conv_step, 1)
                dve.wait_ge(ln_ready, i + 1 + START)
                dve.scalar_tensor_tensor(z, z, 0.0, soft, ALU.max, ALU.add).then_inc(delta_ready, 1)
                dve.wait_ge(delta_ready, i + 1 + START)
                dve.tensor_tensor(delta_u, z, u, ALU.mult).then_inc(du_ready, 1)
                dve.wait_ge(du_ready, i + 1 + START)
                dve.memset(z.rearrange("p c (q t) -> p (c q) t", t=L)[:, :, 0:1], 1e30).then_inc(starts_cut, 1)
                for n in range(STATES):
                    dve.wait_ge(b_spread, i * STATES + n + 1 + START)
                    if n >= 2:
                        dve.wait_ge(read_ready, i * STATES + n - 1 + START)
                    dve.tensor_tensor(state[n % 2], delta_u, ps[:, 4:5, :].broadcast_to([P, IC, TILE]),
                                      ALU.mult).then_inc(input_ready, 1)
                    dve.wait_ge(input_ready, i * STATES + n + 1 + START)
                    dve.wait_ge(factor_ready, i * STATES * IC + (n + 1) * IC + START)
                    s = state[n % 2].rearrange("p a b -> p (a b)")
                    dve.tensor_tensor_scan(s, factor[n % 2].rearrange("p a b -> p (a b)"), s, 0.0, ALU.mult,
                                           ALU.add).then_inc(state_ready, 1)
                dve.wait_ge(y_summed, (i + 1) * STATES + START)
                for c in range(IC):
                    w = cols["ssm_D"] + c
                    dve.scalar_tensor_tensor(y[:, c, :], u[:, c, :], vec[:, w:w + 1], ps[:, c, :], ALU.mult,
                                             ALU.add).then_inc(y_added, 1)
                dve.wait_ge(y_added, (i + 1) * IC + START)
                dve.tensor_tensor(y, y, gate, ALU.mult).then_inc(y_gated, 1)
                dve.wait_ge(out_summed, i + 1 + START)
                dst = hT[:, :, bass.ds(i * TILE, TILE)]
                dve.tensor_tensor(dst, dst, ps[:, 4:6, :], ALU.add).then_inc(residual, 1)


def phase_last(nc, mem, dram, out):
    hT, vec, cols, cst = mem.hT, mem.vec, mem.cols, mem.cst
    part = mem.part
    wT, a1, a2, first, whole = (part([P, KD, D]) for _ in range(5))
    tanh = part([P, KD, TILE])
    h_out = part([P, KD, TILE])
    rows = part([P, TILE // P, D])
    with ExitStack() as ctx:
        ps = ctx.enter_context(nc.psum_tensor("ps_last", [P, 8, 512], F32))
        norm = Norm(nc, mem, ps, 6, 7)
        sems = (weights_in, first_summed, first_kept, whole_summed, whole_kept, lin_summed, tanh_ready, h_ready,
                turned, rows_ready, written) = named(nc, mem.ctx, (
                    "last_weights_in first_summed first_kept whole_summed whole_kept lin_summed tanh_ready h_ready "
                    "turned rows_ready written"))
        block = ctx.enter_context(nc.Block())

        @block.sync
        def _(sp):
            open_phase(sp, [*sems, *norm.opened])
            for w, name in ((wT, "ffn_wT"), (a1, "ffn_a1"), (a2, "ffn_a2")):
                sp.dma_start(w, dram[name]).then_inc(weights_in, 16)
            with sp.Fori(0, TILES) as i:
                sp.wait_ge(rows_ready, i + 1 + START)
                sp.dma_start(out[bass.ds(i * (TILE // P), TILE // P)].rearrange("s p d -> p s d"),
                             rows).then_inc(written, 16)
            sp.wait_ge(written, 16 * TILES + START)

        @block.tensor
        def _(pe):
            pe.wait_ge(weights_in, 48 + START)
            for m in range(KD):
                for k in range(KD):
                    mm = pe.matmul(ps[:, m, 0:D], a1[:, k, m * P:(m + 1) * P], wT[:, k, :],
                                   start=(k == 0), stop=(k == KD - 1))
            mm.then_inc(first_summed, 1)
            pe.wait_ge(first_kept, 1 + START)
            for m in range(KD):
                for k in range(KD):
                    mm = pe.matmul(ps[:, 2 + m, 0:D], first[:, k, m * P:(m + 1) * P], a2[:, k, :],
                                   start=(k == 0), stop=(k == KD - 1))
            mm.then_inc(whole_summed, 1)
            pe.wait_ge(whole_kept, 1 + START)
            with pe.Fori(0, TILES) as i:
                norm.mean(pe, i)
                norm.variance(pe, i)
                pe.wait_ge(norm.is_normed, i + 1 + norm.base)
                for m in range(KD):
                    for k in range(KD):
                        mm = pe.matmul(ps[:, m, :], whole[:, k, m * P:(m + 1) * P], norm.xn[:, k, :],
                                       start=(k == 0), stop=(k == KD - 1))
                mm.then_inc(lin_summed, 1)
                pe.wait_ge(h_ready, i + 1 + START)
                for s in range(TILE // P):
                    for k in range(KD):
                        mm = pe.transpose(ps[:, 2 + s // 2, (s % 2) * D + k * P:(s % 2) * D + (k + 1) * P],
                                          h_out[:, k, s * P:(s + 1) * P], cst["ident"])
                mm.then_inc(turned, 1)

        @block.scalar
        def _(act):
            with act.Fori(0, TILES) as i:
                norm.square(act, i)
                norm.take_root(act, i)
                act.wait_ge(lin_summed, i + 1 + START)
                for m in range(KD):
                    c = cols["ffn_bias"] + m
                    act.activation(tanh[:, m, :], ps[:, m, :], ACT.Tanh,
                                   bias=vec[:, c:c + 1]).then_inc(tanh_ready, 1)

        @block.vector
        def _(dve):
            dve.wait_ge(first_summed, 1 + START)
            dve.tensor_copy(first, ps[:, 0:KD, 0:D]).then_inc(first_kept, 1)
            dve.wait_ge(whole_summed, 1 + START)
            dve.tensor_copy(whole, ps[:, 2:2 + KD, 0:D]).then_inc(whole_kept, 1)
            with dve.Fori(0, TILES) as i:
                norm.centre(dve, i)
                norm.scale(dve, i)
                dve.wait_ge(tanh_ready, (i + 1) * KD + START)
                dve.tensor_tensor(h_out, tanh, hT[:, :, bass.ds(i * TILE, TILE)], ALU.add).then_inc(h_ready, 1)
                dve.wait_ge(turned, i + 1 + START)
                dve.wait_ge(written, i * 16 + START)
                dve.tensor_copy(rows.rearrange("p a b -> p (a b)"),
                                ps[:, 2:4, :].rearrange("p a b -> p (a b)")).then_inc(rows_ready, 1)


def phase_out(nc, mem, dram, out):
    hT, ident = mem.hT, mem.ident
    h_tile = mem.part([P, KD, TILE])
    rows = mem.part([P, TILE // P, D])
    with ExitStack() as ctx:
        ps = ctx.enter_context(nc.psum_tensor("ps_rows", [P, TILE // P, D], F32))
        tile_copied, turned, rows_ready, written = (
            mem.ctx.enter_context(nc.semaphore(n)) for n in
            ("tile_copied", "turned", "rows_ready", "written"))
        block = ctx.enter_context(nc.Block())

        @block.gpsimd
        def _(pool):
            with pool.Fori(0, TILES) as i:
                pool.wait_ge(turned, i + START)
                pool.tensor_copy(h_tile[:], hT[:, :, bass.ds(i * TILE, TILE)]).then_inc(tile_copied, 1)

        @block.tensor
        def _(pe):
            with pe.Fori(0, TILES) as i:
                pe.wait_ge(tile_copied, i + 1 + START)
                pe.wait_ge(rows_ready, i + START)
                for s in range(TILE // P):
                    for k in range(KD):
                        mm = pe.transpose(ps[:, s, k * P:(k + 1) * P], h_tile[:, k, s * P:(s + 1) * P], ident)
                mm.then_inc(turned, 1)

        @block.vector
        def _(dve):
            with dve.Fori(0, TILES) as i:
                dve.wait_ge(turned, i + 1 + START)
                dve.wait_ge(written, i * 16 + START)
                dve.tensor_copy(rows[:], ps[:]).then_inc(rows_ready, 1)

        @block.sync
        def _(sp):
            open_phase(sp, [tile_copied, turned, rows_ready, written])
            with sp.Fori(0, TILES) as i:
                sp.wait_ge(rows_ready, i + 1 + START)
                sp.dma_start(out[bass.ds(i * (TILE // P), TILE // P)].rearrange("s p d -> p s d"),
                             rows[:]).then_inc(written, 16)
            sp.wait_ge(written, 16 * TILES + START)


class Memory:

    def __init__(self, nc, ctx, cols, cst, n_vec, n_const):
        def sb(name, shape):
            return ctx.enter_context(nc.sbuf_tensor(name, shape, F32))
        self.cols = cols
        self.norm_sems, self.norms = None, 0
        self.ctx = ctx
        self.hT = sb("hT", [P, KD, N])
        self.vec = sb("vec", [P, n_vec])
        self.const = sb("const", [P, n_const])
        self.ident = self.const[:, 0:P]
        self.words = (nc.sbuf_bytes_remaining() if callable(nc.sbuf_bytes_remaining) else nc.sbuf_bytes_remaining) // 4 - 64
        self.region = sb("region", [P, self.words])
        self.used = 0
        self.cst = {name: self.const[:, a:b] for name, (a, b) in cst.items()}

    def part(self, shape, at=None):
        n = int(np.prod(shape[1:]))
        if at is None:
            at = self.used
            self.used += n
        assert at + n <= self.words, (at + n, self.words)
        flat = self.region[0:shape[0], at:at + n]
        if len(shape) == 3:
            return flat.rearrange("p (a b) -> p a b", a=shape[1])
        if len(shape) == 4:
            return flat.rearrange("p (a b c) -> p a b c", a=shape[1], b=shape[2])
        if len(shape) == 5:
            return flat.rearrange("p (a b c d) -> p a b c d", a=shape[1], b=shape[2], c=shape[3])
        return flat


def program(nc, dram, out, cols, cst, n_vec, n_const):
    with ExitStack() as ctx:
        mem = Memory(nc, ctx, cols, cst, n_vec, n_const)
        phase_tokens(nc, mem, dram, None)
        mem.used = 0
        if LAST_PHASE >= 2:
            phase_attention(nc, mem, dram)
            mem.used = 0
        if LAST_PHASE >= 3:
            phase_experts(nc, mem, dram)
            mem.used = 0
        if LAST_PHASE >= 4:
            phase_state_space(nc, mem, dram)
            mem.used = 0
        if LAST_PHASE >= 5:
            phase_last(nc, mem, dram, out)
            return
        phase_out(nc, mem, dram, out)


def chunks(a, p=P):
    a = np.asarray(a)
    return a.reshape(a.shape[0] // p, p, *a.shape[1:]).swapaxes(0, 1)


def flat(a):
    return np.ascontiguousarray(a.reshape(a.shape[0], -1))


def constants():
    f = np.float32
    e = np.arange(P) // DH
    inv_freq = 1.0 / f(10000.0) ** (np.arange(0, DH, 2, dtype=f) / f(DH))
    angle = np.outer(np.arange(L, dtype=f), inv_freq).astype(f)
    of = (2 * ((np.arange(P) % DH) // 2)) % (DH // 2)
    sign = np.where(np.arange(P) % 2 == 0, f(-1), f(1))[:, None]
    tables = {
        "ident": np.eye(P, dtype=f),
        "mean": np.full((P, P), 1.0 / D, f),
        "head_mean": (e[:, None] == e[None, :]).astype(f) / f(DH),
        "pick2": (e[:, None] == np.arange(2)[None, :]).astype(f),
        "cos": np.cos(angle).T[of],
        "sin": np.sin(angle).T[of] * sign,
        "eps5": np.full((P, 1), 1e-5, f),
        "eps6": np.full((P, 1), 1e-6, f),
        "one": np.ones((P, 1), f),
        "expert_of": flat((2 * np.arange(PAIRS)[None, :, None] + e[:, None, None]
                           == np.arange(EXPERTS)[None, None, :]).astype(f)),
        "number": np.tile(np.arange(EXPERTS, dtype=f) - EXPERTS, (P, 1)),
    }
    at, where = 0, {}
    for name, a in tables.items():
        where[name] = (at, at + a.shape[1])
        at += a.shape[1]
    return np.concatenate([a.astype(f) for a in tables.values()], axis=1), where


def kernel(**inputs):
    import concourse.bacc as bacc
    from concourse.bass_utils import run_bass_kernel_spmd

    t = {k: np.asarray(v) for k, v in inputs.items()}
    f = np.float32
    vec = Columns()
    for name, key in (("b1", "L0_tok_b1"), ("b2", "L0_tok_b2")):
        vec.add(name, chunks(t[key]))
    convs = [np.concatenate([chunks(t[f"L0_attn_{q}cw"][:, 0]), chunks(t[f"L0_attn_{q}cb"])[..., None]], axis=2)
             for q in "qkv"]
    vec.add("conv", flat(np.stack(convs, axis=1)))
    for name, key in (("bb", "bb"), ("dt", "gkb"), ("dt_bias", "dt_bias"), ("A_log", "A_log"), ("Dp", "D_param")):
        vec.add(name, np.tile(t["L0_attn_" + key], P // HEADS)[:, None])
    vec.add("onorm", np.tile(t["L0_attn_onorm_w"], P // DH)[:, None])
    vec.add("ssm_conv", flat(np.concatenate([chunks(t["L1_attn_conv_w"][:, 0]), chunks(t["L1_attn_conv_b"])[..., None]],
                                            axis=2)))
    vec.add("ssm_b_dt", chunks(t["L1_attn_b_dt"]))
    vec.add("ssm_A_log", flat(chunks(t["L1_attn_A_log"])))
    vec.add("ssm_D", chunks(t["L1_attn_D"]))
    vec.add("ffn_bias", chunks(t["L1_ffn_bias"]))
    vecs = np.ascontiguousarray(np.concatenate(vec.parts, axis=1))

    const, cst = constants()

    arrays = {
        "x": t["x"],
        "W1": t["L0_tok_W1"].reshape(V, 2, PATCH // 2, D).transpose(1, 0, 2, 3).reshape(P, PATCH // 2, D),
        "W2": chunks(t["L0_tok_W2"]),
        "Wqkv": np.stack([chunks(t["L0_attn_W" + q]) for q in "qkv"], axis=1),
        "Wg": chunks(t["L0_attn_Wg"]),
        "Wo": chunks(t["L0_attn_Wo"]),
        "Wab": np.concatenate([chunks(t["L0_attn_bw"]), chunks(t["L0_attn_gkw"])], axis=2),
        "W_A": chunks(t["L0_ffn_W_A"].reshape(EXPERTS * RANK, D).T),
        "W_B": t["L0_ffn_W_B"].reshape(PAIRS, 2, FFN, RANK).transpose(1, 3, 0, 2).reshape(P, PAIRS, FFN),
        "W_up": t["L0_ffn_W_up"].reshape(EXPERTS, FFN, KD, P).transpose(3, 0, 2, 1),
        "W_down": t["L0_ffn_W_down"].reshape(EXPERTS, D, FC, P).transpose(3, 0, 2, 1),
        "W_in": chunks(t["L1_attn_W_in"]),
        "W_x": chunks(t["L1_attn_W_x"]),
        "W_dt": t["L1_attn_W_dt"],
        "W_out": chunks(t["L1_attn_W_out"]),
        "ffn_wT": chunks(t["L1_ffn_weight"].T),
        "ffn_a1": chunks(t["L1_ffn_aux_weight1"]),
        "ffn_a2": chunks(t["L1_ffn_aux_weight2"]),
        "vec": vecs,
        "const": const,
    }
    arrays = {k: np.ascontiguousarray(a) for k, a in arrays.items()}
    nc = bacc.Bacc("TRN2", target_bir_lowering=False, num_devices=1)
    dram = {k: nc.dram_tensor(f"in_{k}", a.shape, F32, kind="ExternalInput").ap() for k, a in arrays.items()}
    out = nc.dram_tensor("out_h", (N // P, P, D), F32, kind="ExternalOutput").ap()
    program(nc, dram, out, vec.at, cst, vecs.shape[1], const.shape[1])
    r = run_bass_kernel_spmd(nc, [{f"in_{k}": a for k, a in arrays.items()}], core_ids=[0])
    return r.results[0]["out_h"].reshape(B, L, D)
```

```python
from contextlib import ExitStack

import numpy as np

import concourse.bass as bass
from concourse import mybir

F32 = mybir.dt.float32
BF16 = mybir.dt.bfloat16
ALU = mybir.AluOpType
ACT = mybir.ActivationFunctionType
AX = mybir.AxisListType

P = 128
B, V, T, D = 64, 64, 256, 256
PATCH, STRIDE = 16, 8
L = (T + STRIDE - PATCH) // STRIDE + 1
N = B * L
TILE = 512
TILES = N // TILE
SEQ = TILE // L
KD = D // P


class Columns:

    def __init__(self):
        self.at, self.parts, self.n = {}, [], 0

    def add(self, name, a):
        self.at[name] = self.n
        self.parts.append(a)
        self.n += a.shape[1]


def phase_tokens(nc, mem, dram):
    hT, vec, cols = mem.hT, mem.vec, mem.cols
    x = mem.part([P, B, T])
    w1 = mem.part([P, PATCH // 2, D])
    w2 = mem.part([P, KD, D])
    hid = mem.part([P, KD, TILE])
    with ExitStack() as ctx:
        ps_hid = ctx.enter_context(nc.psum_tensor("ps_hid", [P, KD, TILE], F32))
        ps_out = ctx.enter_context(nc.psum_tensor("ps_out", [P, KD, TILE], F32))
        weights_in, x_in, x_padded, hid_summed, hid_ready, out_summed, out_added = (
            mem.ctx.enter_context(nc.semaphore(n)) for n in
            ("tok_weights_in", "x_in", "x_padded", "hid_summed", "hid_ready", "tok_summed", "tok_added"))
        block = ctx.enter_context(nc.Block())
        xv = dram["x"].rearrange("b v t -> v b t")

        @block.sync
        def _(sp):
            open_phase(sp, [weights_in, x_in, x_padded, hid_summed, hid_ready, out_summed, out_added])
            sp.dma_start(w1[:], dram["W1"]).then_inc(weights_in, 16)
            sp.dma_start(w2[:], dram["W2"]).then_inc(weights_in, 16)
            sp.dma_start(vec[:], dram["vec"]).then_inc(weights_in, 16)
            sp.dma_start(mem.const[:], dram["const"]).then_inc(weights_in, 16)
            with sp.Fori(0, TILES) as i:
                sp.wait_ge(x_in, i * 32 + START)
                sp.dma_start(x[0:V, bass.ds(i * SEQ, SEQ), :], xv[:, bass.ds(i * SEQ, SEQ), :]).then_inc(x_in, 16)
                sp.dma_start(x[V:P, bass.ds(i * SEQ, SEQ), 0:T - STRIDE],
                             xv[:, bass.ds(i * SEQ, SEQ), STRIDE:T]).then_inc(x_in, 16)

        @block.gpsimd
        def _(pool):
            with pool.Fori(0, TILES) as i:
                pool.wait_ge(x_in, i * 32 + 32 + START)
                s = bass.ds(i * SEQ, SEQ)
                pool.tensor_copy(x[V:P, s, T - STRIDE:T],
                                 x[V:P, s, T - STRIDE - 1:T - STRIDE].broadcast_to([V, SEQ, STRIDE])
                                 ).then_inc(x_padded, 1)

        @block.tensor
        def _(pe):
            pe.wait_ge(weights_in, 64 + START)
            with pe.Fori(0, TILES) as i:
                pe.wait_ge(x_padded, i + 1 + START)
                pe.wait_ge(hid_ready, i * KD + START)
                for m in range(KD):
                    for p in range(PATCH // 2):
                        mm = pe.matmul(ps_hid[:, m, :], w1[:, p, m * P:(m + 1) * P],
                                       x[:, bass.ds(i * SEQ, SEQ), p:T:STRIDE],
                                       start=(p == 0), stop=(p == PATCH // 2 - 1))
                    mm.then_inc(hid_summed, 1)
                pe.wait_ge(hid_ready, i * KD + KD + START)
                pe.wait_ge(out_added, i * KD + START)
                for m in range(KD):
                    for k in range(KD):
                        mm = pe.matmul(ps_out[:, m, :], w2[:, k, m * P:(m + 1) * P], hid[:, k, :],
                                       start=(k == 0), stop=(k == KD - 1))
                    mm.then_inc(out_summed, 1)

        @block.scalar
        def _(act):
            act.wait_ge(weights_in, 64 + START)
            with act.Fori(0, TILES) as i:
                act.wait_ge(out_summed, i * KD + START)
                for m in range(KD):
                    act.wait_ge(hid_summed, i * KD + m + 1 + START)
                    c = cols["b1"] + m
                    act.activation(hid[:, m, :], ps_hid[:, m, :], ACT.Relu,
                                   bias=vec[:, c:c + 1]).then_inc(hid_ready, 1)

        @block.vector
        def _(dve):
            dve.wait_ge(weights_in, 64 + START)
            with dve.Fori(0, TILES) as i:
                for m in range(KD):
                    dve.wait_ge(out_summed, i * KD + m + 1 + START)
                    c = cols["b2"] + m
                    dve.tensor_scalar(hT[:, m, bass.ds(i * TILE, TILE)], ps_out[:, m, :],
                                      vec[:, c:c + 1], None, ALU.add).then_inc(out_added, 1)


HEADS, DH, CONV = 16, 64, 4
INNER = HEADS * DH
HC = INNER // P
HALVES = 2
HALF = N // HALVES
HT = HALF // TILE
SUBS = HALF // P
SPB = P // L
UNITS = HT * HC
START = 2


def open_phase(eng, sems):
    for s in sems:
        eng.sem_inc(s, START)


def named(nc, ctx, names):
    return [ctx.enter_context(nc.semaphore(n)) for n in names.split()]


def diagonal(rows, seq):
    return rows[:, seq * L:seq * L + (L - 1) * (P + 1) + 1:P + 1]


def phase_attention(nc, mem, dram):
    hT, vec, cols, cst = mem.hT, mem.vec, mem.cols, mem.cst
    part = mem.part
    w_qkv = part([P, 3, KD, INNER])
    w_g = part([P, KD, INNER])
    w_o = part([P, HC, D])
    w_ab = part([P, KD, 2 * HEADS])
    xn = part([P, KD, HALF])
    at_v = mem.used
    v_rows = part([P, SUBS, INNER])
    at_scores = mem.used
    scores = part([P, 2 * L, SUBS, HEADS])
    table_rows = part([P, L, SUBS, HEADS], at_scores)
    spread = [part([P, HEADS, P], at_scores + 4096 + b * 2048) for b in range(2)]
    decay = part([P, L, SPB, L])
    ab = part([P, 3, SUBS, HEADS])
    gates = part([P, 3, P])
    g_small = part([P, 12, P])
    nega = part([P, 2])
    work = mem.used
    kq_rows = part([P, 2 * L, P])
    k_flat = kq_rows[:, 0:L, :].rearrange("p a b -> p (a b)")
    q_flat = kq_rows[:, L:2 * L, :].rearrange("p a b -> p (a b)")
    a_rows = kq_rows[:, 0:L, :]
    g_rows = kq_rows[:, L:2 * L, :]
    a4 = a_rows.rearrange("p t (j s) -> p t j s", j=SPB)
    g4 = g_rows.rearrange("p t (j s) -> p t j s", j=SPB)
    product = part([P, 1024])
    end = mem.used
    mem.used = work
    padded = [part([P, SEQ, L + CONV - 1]) for _ in range(3)]
    conv = [part([P, TILE]) for _ in range(3)]
    acted = [[part([P, TILE]) for _ in range(3)] for _ in range(3)]
    swapped = [part([P, TILE]) for _ in range(2)]
    cosine = [part([P, TILE]) for _ in range(2)]
    sine = swapped
    kq = [part([P, 2, TILE]) for _ in range(2)]
    q_square = part([P, TILE])
    end = max(end, mem.used)
    mem.used = end
    centred = part([P, KD, TILE], at_v)
    squared = part([P, KD, TILE], at_v + 1024)
    deviation = part([P, TILE], at_v + 2048)
    inverse = part([P, TILE], at_v + 2560)
    o_sb = [part([P, HC, P], work), part([P, HC, P], work + 9216)]
    o_sq = part([P, HC, P], work + 1024)
    o_sd = part([P, HC, P], work + 2048)
    o_inv = part([P, HC, P], work + 3072)
    o_norm = part([P, HC, P], work + 4096)
    o_act = part([P, HC, P], work + 5120)
    gate = [part([P, HC, P], work + 6144 + b * 1024) for b in range(2)]
    gated = part([P, HC, P], work + 8192)

    with ExitStack() as ctx:
        ps = ctx.enter_context(nc.psum_tensor("ps_attention", [P, 8, 512], F32))
        (w_in, wo_in, summed_mean, centred_s, squared_s, summed_var, rooted, inverted, normed,
         pads_clear, projected, raw_copied, shuffled, cosined, sined, kq_ready, q_squared,
         scored, v_turned, score_kept, v_kept, lengths_summed) = named(nc, mem.ctx, (
            "w_in wo_in summed_mean centred squared summed_var rooted inverted normed "
            "pads_clear projected raw_copied shuffled cosined sined kq_ready q_squared "
            "scored v_turned score_kept v_kept lengths_summed"))
        conv_step = named(nc, mem.ctx, "conv_q conv_k conv_v")
        acted_s = named(nc, mem.ctx, "acted_q acted_k acted_v")
        (ab_summed, ab_kept, gates_turned, gates_kept, act_gate, dve_gate, decay_ready, rows_turned, rows_kept_act,
         rows_kept_dve, key_rooted, tables_ready, solved_dve, solved_pool, diag_step, table_scaled, table_turned,
         table_kept_act, table_kept_dve, spread_clear, spread_dve, spread_act, o_summed, o_kept, o_squared,
         o_var, o_rooted, o_inverted, o_normed, o_acted, g_summed, g_kept, gated_s, out_summed,
         residual) = named(nc, mem.ctx, (
            "ab_summed ab_kept gates_turned gates_kept act_gate dve_gate decay_ready rows_turned rows_kept_act "
            "rows_kept_dve key_rooted tables_ready solved_dve solved_pool diag_step table_scaled table_turned "
            "table_kept_act table_kept_dve spread_clear spread_dve spread_act o_summed o_kept o_squared "
            "o_var o_rooted o_inverted o_normed o_acted g_summed g_kept gated out_summed residual"))
        block = ctx.enter_context(nc.Block())
        ACT_GATE, DVE_GATE = 7, 11
        ROW_GROUPS = 2 * L // 4
        TURNS = L // 4
        SOLVE = 2 * (L - 2)
        SOLVE_POOL = 4 + SOLVE + 1
        POOL_SEQ = 1
        DVE_SEQ = SPB - POOL_SEQ

        def b(x):
            return x.rearrange("p (a b) -> p a b", b=L)

        every = [w_in, wo_in, summed_mean, centred_s, squared_s, summed_var, rooted, inverted, normed,
                 pads_clear, projected, raw_copied, shuffled, cosined, sined, kq_ready, q_squared,
                 scored, v_turned, score_kept, v_kept, lengths_summed, *conv_step, *acted_s,
                 ab_summed, ab_kept, gates_turned, gates_kept, act_gate, dve_gate, decay_ready, rows_turned,
                 rows_kept_act, rows_kept_dve, key_rooted, tables_ready, solved_dve, solved_pool, diag_step, table_scaled,
                 table_turned, table_kept_act, table_kept_dve, spread_clear, spread_dve, spread_act, o_summed,
                 o_kept, o_squared, o_var, o_rooted, o_inverted, o_normed, o_acted, g_summed, g_kept, gated_s,
                 out_summed, residual]

        @block.sync
        def _(sp):
            open_phase(sp, every)
            sp.dma_start(w_qkv, dram["Wqkv"]).then_inc(w_in, 16)
            sp.dma_start(w_ab, dram["Wab"]).then_inc(w_in, 16)
            sp.dma_start(w_g, dram["Wg"]).then_inc(wo_in, 16)
            sp.dma_start(w_o, dram["Wo"]).then_inc(wo_in, 16)

        @block.gpsimd
        def _(pool):
            pool.memset(decay[:], 0.0).then_inc(decay_ready, 1)
            pool.wait_ge(decay_ready, 1 + START)
            dflat = decay.rearrange("p a b c -> p (a b c)")
            for j in range(SPB):
                pool.memset(diagonal(dflat, j), 1.0).then_inc(decay_ready, 1)
            with pool.Fori(0, HALVES) as i:
                for n in range(UNITS):
                    for kind in range(2):
                        pool.wait_ge(shuffled, i * 2 * UNITS + 2 * n + kind + 1 + START)
                        pool.tensor_tensor(b(sine[kind]), b(swapped[kind]),
                                           cst["sin"].unsqueeze(1).broadcast_to([P, SEQ, L]),
                                           ALU.mult).then_inc(sined, 1)
                    pool.wait_ge(lengths_summed, i * UNITS + n + START)
                    s = acted[n % 3][0]
                    pool.tensor_tensor(q_square, s, s, ALU.mult).then_inc(q_squared, 1)
                pool.wait_ge(act_gate, i * ACT_GATE + 6 + START)
                for t in range(1, L):
                    pool.wait_ge(decay_ready, i * (L - 1) + SPB + t + START)
                    pool.tensor_tensor(decay[:, t, :, 0:t], decay[:, t - 1, :, 0:t],
                                       g_small[:, 0, :].rearrange("p (j t) -> p j t", j=SPB)[:, :, t:t + 1]
                                       .broadcast_to([P, SPB, t]), ALU.mult).then_inc(decay_ready, 1)
                own = slice(DVE_SEQ, SPB)

                def by_row(x):
                    return x.rearrange("p (j t) -> p t j", j=SPB)[:, :, own].unsqueeze(3).broadcast_to(
                        [P, L, POOL_SEQ, L])

                step = i * SOLVE_POOL + START
                pool.wait_ge(decay_ready, (i + 1) * (L - 1) + SPB + 1 + START)
                pool.wait_ge(dve_gate, i * DVE_GATE + 9 + START)
                pool.tensor_tensor(a4[:, :, own], a4[:, :, own], decay[:, :, own], ALU.mult).then_inc(solved_pool, 1)
                pool.tensor_tensor(g4[:, 1:L, own], g4[:, 1:L, own], decay[:, 0:L - 1, own], ALU.mult)
                pool.memset(g4[:, 0:1, own], 0.0).then_inc(solved_pool, 1)
                pool.wait_ge(solved_pool, step + 2)
                pool.tensor_tensor(a4[:, :, own], a4[:, :, own], by_row(g_small[:, 2, :]),
                                   ALU.mult).then_inc(solved_pool, 1)
                pool.tensor_tensor(g4[:, :, own], g4[:, :, own], by_row(g_small[:, 6, :]),
                                   ALU.mult).then_inc(solved_pool, 1)
                pool.wait_ge(solved_pool, step + 4)
                tmp = product[:, 768:1024]
                k = 4
                for t in range(L - 2, 0, -1):
                    j, r = slice(DVE_SEQ, SPB), L - 1 - t
                    out = tmp[:, 0:r * POOL_SEQ * t].rearrange("p (r j s) -> p r j s", r=r, j=POOL_SEQ)
                    pool.wait_ge(solved_pool, step + k)
                    pool.tensor_tensor(out, g4[:, t + 1:L, j, t:t + 1].broadcast_to([P, r, POOL_SEQ, t]),
                                       a4[:, t:t + 1, j, 0:t].broadcast_to([P, r, POOL_SEQ, t]),
                                       ALU.mult).then_inc(solved_pool, 1)
                    if k == 4:
                        for s in range(2):
                            pool.memset(spread[s], 0.0).then_inc(spread_clear, 1)
                    pool.wait_ge(solved_pool, step + k + 1)
                    pool.tensor_tensor(g4[:, t + 1:L, j, 0:t], g4[:, t + 1:L, j, 0:t], out,
                                       ALU.subtract).then_inc(solved_pool, 1)
                    k += 2
                pool.wait_ge(solved_pool, step + k)
                scale = g_small[:, 11:12, :].rearrange("p o (j s) -> p o j s", j=SPB)[:, :, own]
                pool.tensor_tensor(g4[:, :, own], g4[:, :, own], scale.broadcast_to([P, L, POOL_SEQ, L]),
                                   ALU.mult).then_inc(solved_pool, 1)

        @block.tensor
        def _(pe):
            with pe.Fori(0, HALVES) as i:
                def mean(a):
                    src = bass.ds(i * HALF + a * TILE, TILE)
                    if a == 0:
                        pe.wait_ge(residual, i * SUBS + START)
                    else:
                        pe.wait_ge(centred_s, i * HT + a + START)
                    for k in range(KD):
                        mm = pe.matmul(ps[:, 6, :], cst["mean"], hT[:, k, src], start=(k == 0), stop=(k == KD - 1))
                    mm.then_inc(summed_mean, 1)

                def variance(a):
                    pe.wait_ge(squared_s, i * HT + a + 1 + START)
                    if a:
                        pe.wait_ge(rooted, i * HT + a + START)
                    for k in range(KD):
                        mm = pe.matmul(ps[:, 5, :], cst["mean"], squared[:, k, :], start=(k == 0), stop=(k == KD - 1))
                    mm.then_inc(summed_var, 1)

                def turn_gates(first, last):
                    pe.wait_ge(ab_kept, i * 2 + last - 1 + START)
                    for g in range(first, last):
                        mm = pe.transpose(ps[:, 6, g * P:(g + 1) * P], ab[:, g].rearrange("p a b -> p (a b)"),
                                          cst["ident"])
                    mm.then_inc(gates_turned, 1)

                def gate_inputs(s):
                    if s == 0:
                        pe.wait_ge(normed, i * HT + HT + START)
                    for k in range(KD):
                        mm = pe.matmul(ps[:, 6, s * 32:s * 32 + 32], xn[:, k, s * P:(s + 1) * P], w_ab[:, k, :],
                                       start=(k == 0), stop=(k == KD - 1))
                    mm.then_inc(ab_summed, 1)

                def project(n):
                    a, c = divmod(n, HC)
                    if n == HC:
                        pe.wait_ge(normed, i * HT + HT + START)
                    for kind in range(3):
                        if n:
                            pe.wait_ge(raw_copied, i * 3 * UNITS + 3 * (n - 1) + kind + 1 + START)
                        for k in range(KD):
                            mm = pe.matmul(ps[:, kind, :], w_qkv[:, kind, k, c * P:(c + 1) * P],
                                           xn[:, k, a * TILE:(a + 1) * TILE], start=(k == 0), stop=(k == KD - 1))
                        mm.then_inc(projected, 1)

                def compare(n):
                    a, c = divmod(n, HC)
                    pe.wait_ge(q_squared, i * UNITS + n + 1 + START)
                    for s in range(TILE // P):
                        sub = a * (TILE // P) + s
                        mm = pe.matmul(ps[:, 7, sub * HEADS + 2 * c:sub * HEADS + 2 * c + 2],
                                       q_square[:, s * P:(s + 1) * P], cst["pick2"], start=True, stop=True)
                    mm.then_inc(lengths_summed, 1)
                    pe.wait_ge(kq_ready, i * 2 * UNITS + 2 * n + 2 + START)
                    if n:
                        pe.wait_ge(score_kept, i * 2 * UNITS + 2 * n + START)
                        pe.wait_ge(v_kept, i * UNITS + n + START)
                    pe.wait_ge(acted_s[2], i * UNITS + n + 1 + START)
                    for s in range(TILE // P):
                        mm = pe.transpose(ps[:, 5, s * P:(s + 1) * P], acted[n % 3][2][:, s * P:(s + 1) * P],
                                          cst["ident"])
                    mm.then_inc(v_turned, 1)
                    for e in range(2):
                        h = slice(e * DH, e * DH + DH)
                        for q in range(SEQ):
                            sub, j = divmod(q, SPB)
                            mm = pe.matmul(ps[j * L:j * L + L, 3 + e, sub * 2 * L:(sub + 1) * 2 * L],
                                           kq[n % 2][h, 0, q * L:(q + 1) * L],
                                           kq[n % 2][h, :, q * L:(q + 1) * L], start=True, stop=True)
                        mm.then_inc(scored, 1)

                mean(0)
                variance(0)
                mean(1)
                pe.wait_ge(w_in, 32 + START)
                pe.wait_ge(normed, i * HT + 1 + START)
                project(0)
                variance(1)
                for n in range(1, UNITS + 2):
                    if n < UNITS:
                        project(n)
                    if n >= 2:
                        compare(n - 2)
                    if 2 <= n < 2 + SUBS:
                        gate_inputs(n - 2)
                    if n == 3 + SUBS:
                        turn_gates(0, 2)
                turn_gates(2, 3)
                pe.wait_ge(score_kept, (i + 1) * 2 * UNITS + START)
                for g in range(ROW_GROUPS):
                    if g >= 4:
                        which = rows_kept_dve if g % 2 else rows_kept_act
                        pe.wait_ge(which, i * (ROW_GROUPS // 2) + (g - 4) // 2 + 1 + START)
                    for r in range(4):
                        mm = pe.transpose(ps[:, g % 4, r * P:(r + 1) * P],
                                          scores[:, 4 * g + r].rearrange("p a b -> p (a b)"), cst["ident"])
                    mm.then_inc(rows_turned, 1)
                pe.wait_ge(table_scaled, i * (1 + SPB) + 1 + SPB + START)
                for g in range(TURNS):
                    if g >= 4:
                        which = table_kept_dve if g % 2 else table_kept_act
                        pe.wait_ge(which, i * (TURNS // 2) + (g - 4) // 2 + 1 + START)
                    for r in range(4):
                        mm = pe.transpose(ps[:, g % 4, r * P:(r + 1) * P], g_rows[:, 4 * g + r, :], cst["ident"])
                    mm.then_inc(table_turned, 1)
                pe.wait_ge(wo_in, 32 + START)

                def project_out(s):
                    pe.wait_ge(gated_s, i * SUBS + s + 1 + START)
                    if s:
                        pe.wait_ge(residual, i * SUBS + s + START)
                    for m in range(KD):
                        for c in range(HC):
                            mm = pe.matmul(ps[:, 6, m * P:(m + 1) * P], w_o[:, c, m * P:(m + 1) * P],
                                           gated[:, c, :], start=(c == 0), stop=(c == HC - 1))
                    mm.then_inc(out_summed, 1)

                for s in range(SUBS):
                    pe.wait_ge(spread_dve, i * 2 * SUBS + 2 * s + 2 + START)
                    pe.wait_ge(spread_act, i * 2 * SUBS + 2 * s + 2 + START)
                    if s:
                        pe.wait_ge(o_kept, i * SUBS + s + START)
                    for h in range(HEADS):
                        c, e = divmod(h, 2)
                        mm = pe.matmul(ps[e * DH:(e + 1) * DH, c // 4, (c % 4) * P:(c % 4 + 1) * P],
                                       v_rows[:, s, h * DH:(h + 1) * DH], spread[s % 2][:, h, :],
                                       start=True, stop=True)
                    mm.then_inc(o_summed, 1)
                    if s:
                        pe.wait_ge(g_kept, i * SUBS + s + START)
                    for c in range(HC):
                        for k in range(KD):
                            mm = pe.matmul(ps[:, 2 + c // 4, (c % 4) * P:(c % 4 + 1) * P],
                                           w_g[:, k, c * P:(c + 1) * P], xn[:, k, s * P:(s + 1) * P],
                                           start=(k == 0), stop=(k == KD - 1))
                    mm.then_inc(g_summed, 1)
                    pe.wait_ge(o_squared, i * SUBS + s + 1 + START)
                    if s:
                        pe.wait_ge(o_rooted, i * SUBS + s + START)
                    for c in range(2):
                        mm = pe.matmul(ps[:, 4 + c, :], cst["head_mean"], o_sq[:, 4 * c:4 * c + 4, :],
                                       start=True, stop=True)
                    mm.then_inc(o_var, 1)
                    if s:
                        project_out(s - 1)
                project_out(SUBS - 1)

        @block.scalar
        def _(act):
            with act.Fori(0, HALVES) as i:
                def square(a):
                    act.wait_ge(centred_s, i * HT + a + 1 + START)
                    if a:
                        act.wait_ge(summed_var, i * HT + a + START)
                    act.activation(squared, centred, ACT.Square).then_inc(squared_s, 1)

                def root(a):
                    act.wait_ge(summed_var, i * HT + a + 1 + START)
                    act.wait_ge(inverted, i * HT + a + START)
                    act.activation(deviation, ps[:, 5, :], ACT.Sqrt, bias=cst["eps5"]).then_inc(rooted, 1)

                def raw(n, kind):
                    c = n % HC
                    act.wait_ge(projected, i * 3 * UNITS + 3 * n + kind + 1 + START)
                    if n:
                        act.wait_ge(conv_step[kind], i * 3 * UNITS + 3 * n + START)
                        act.wait_ge(acted_s[kind], i * UNITS + n + START)
                    act.activation(padded[kind][:, :, CONV - 1:], b(ps[:, kind, :]), ACT.Copy)
                    w = cols["conv"] + (kind * HC + c) * (CONV + 1)
                    act.activation(conv[kind], ps[:, kind, :], ACT.Identity, bias=vec[:, w + CONV:w + CONV + 1],
                                   scale=vec[:, w + CONV - 1:w + CONV]).then_inc(raw_copied, 1)

                def silu(n, kind):
                    act.wait_ge(conv_step[kind], i * 3 * UNITS + 3 * n + 3 + START)
                    if kind == 2:
                        if n >= 3:
                            act.wait_ge(v_turned, i * UNITS + n - 2 + START)
                    elif n >= 3:
                        act.wait_ge(kq_ready, i * 2 * UNITS + 2 * (n - 2) + START)
                        if kind == 0:
                            act.wait_ge(q_squared, i * UNITS + n - 2 + START)
                    act.activation(acted[n % 3][kind], conv[kind], ACT.Silu).then_inc(acted_s[kind], 1)

                def keep(n):
                    a, c = divmod(n, HC)
                    subs = slice(a * (TILE // P), (a + 1) * (TILE // P))
                    act.wait_ge(v_turned, i * UNITS + n + 1 + START)
                    act.activation(v_rows[:, subs, c * P:(c + 1) * P],
                                   ps[:, 5, :].rearrange("p (s c) -> p s c", c=P), ACT.Copy).then_inc(v_kept, 1)
                    for e in range(2):
                        act.wait_ge(scored, i * 2 * UNITS + 2 * n + e + 1 + START)
                        act.activation(scores[:, :, subs, 2 * c + e].rearrange("p r s -> p s r"),
                                       ps[:, 3 + e, 0:256].rearrange("p (s r) -> p s r", r=2 * L),
                                       ACT.Copy).then_inc(score_kept, 1)

                def gate_step(k):
                    base = i * ACT_GATE + START
                    if k == 0:
                        act.wait_ge(gates_kept, i * 2 + 1 + START)
                        act.activation(g_small[:, 1, :], gates[:, 0, :], ACT.Sigmoid,
                                       bias=vec[:, cols["bb"]:cols["bb"] + 1]).then_inc(act_gate, 1)
                        act.wait_ge(dve_gate, i * DVE_GATE + 1 + START)
                        act.activation(g_small[:, 2, :], g_small[:, 3, :], ACT.Abs).then_inc(act_gate, 1)
                    if k == 1:
                        act.wait_ge(act_gate, base + 2)
                        act.activation(g_small[:, 4, :], g_small[:, 2, :], ACT.Exp,
                                       scale=-1.0).then_inc(act_gate, 1)
                        act.activation(nega[:, 0:1], vec[:, cols["A_log"]:cols["A_log"] + 1],
                                       ACT.Exp).then_inc(act_gate, 1)
                    if k == 2:
                        act.wait_ge(act_gate, base + 3)
                        act.activation(g_small[:, 5, :], g_small[:, 4, :], ACT.Ln,
                                       bias=cst["one"]).then_inc(act_gate, 1)
                    if k == 3:
                        act.wait_ge(dve_gate, i * DVE_GATE + 3 + START)
                        act.activation(g_small[:, 0, :], g_small[:, 7, :], ACT.Exp).then_inc(act_gate, 1)

                square(0)
                root(0)
                square(1)
                act.wait_ge(pads_clear, i + 1 + START)
                for kind in range(3):
                    raw(0, kind)
                root(1)
                for n in range(UNITS + 2):
                    if n < UNITS:
                        silu(n, 0)
                        silu(n, 1)
                    if n >= 2:
                        keep(n - 2)
                    if n + 1 < UNITS:
                        raw(n + 1, 0)
                        raw(n + 1, 1)
                    if n < UNITS:
                        silu(n, 2)
                    if n + 1 < UNITS:
                        raw(n + 1, 2)
                    if n >= UNITS - 3:
                        gate_step(n - (UNITS - 3))

                act.wait_ge(gates_kept, i * 2 + 2 + START)
                act.activation(g_small[:, 6, :], gates[:, 2, :], ACT.Sqrt, bias=cst["eps6"]).then_inc(act_gate, 1)
                for g in range(0, ROW_GROUPS, 2):
                    act.wait_ge(rows_turned, i * ROW_GROUPS + g + 1 + START)
                    act.activation(kq_rows[:, 4 * g:4 * g + 4, :].rearrange("p a b -> p (a b)"), ps[:, g % 4, :],
                                   ACT.Copy).then_inc(rows_kept_act, 1)
                act.wait_ge(diag_step, i * 2 * SPB + SPB + START)
                act.activation(g_small[:, 8, :], g_small[:, 9, :], ACT.Sqrt,
                               bias=cst["eps6"]).then_inc(key_rooted, 1)
                for g in range(0, TURNS, 2):
                    act.wait_ge(table_turned, i * TURNS + g + 1 + START)
                    act.activation(table_rows[:, 4 * g:4 * g + 4].rearrange("p a b c -> p (a b c)"), ps[:, g % 4, :],
                                   ACT.Copy).then_inc(table_kept_act, 1)

                def spread_block(s):
                    if s == 0:
                        act.wait_ge(table_kept_act, i * TURNS // 2 + TURNS // 2 + START)
                        act.wait_ge(table_kept_dve, i * TURNS // 2 + TURNS // 2 + START)
                        act.wait_ge(spread_clear, i * 2 + 2 + START)
                    if s >= 2:
                        act.wait_ge(o_summed, i * SUBS + s - 1 + START)
                    for j in range(2, SPB):
                        q = slice(j * L, j * L + L)
                        act.activation(spread[s % 2][q, :, q], table_rows[q, :, s, :].rearrange("p t h -> p h t"),
                                       ACT.Copy).then_inc(spread_act, 1)

                def act_silu(s):
                    act.wait_ge(o_normed, i * SUBS + s + 1 + START)
                    if s:
                        act.wait_ge(gated_s, i * SUBS + s + START)
                    act.activation(o_act, o_norm, ACT.Silu).then_inc(o_acted, 1)

                spread_block(0)
                for s in range(SUBS):
                    if s + 1 < SUBS:
                        spread_block(s + 1)
                    act.wait_ge(o_kept, i * SUBS + s + 1 + START)
                    if s:
                        act.wait_ge(o_var, i * SUBS + s + START)
                    act.activation(o_sq, o_sb[s % 2], ACT.Square).then_inc(o_squared, 1)
                    if s:
                        act_silu(s - 1)
                    act.wait_ge(g_summed, i * SUBS + s + 1 + START)
                    if s >= 2:
                        act.wait_ge(gated_s, i * SUBS + s - 1 + START)
                    act.activation(gate[s % 2].rearrange("p a b -> p (a b)"),
                                   ps[:, 2:4, :].rearrange("p a b -> p (a b)"), ACT.Copy).then_inc(g_kept, 1)
                    act.wait_ge(o_var, i * SUBS + s + 1 + START)
                    if s:
                        act.wait_ge(o_inverted, i * SUBS + s + START)
                    act.activation(o_sd.rearrange("p a b -> p (a b)"), ps[:, 4:6, :].rearrange("p a b -> p (a b)"),
                                   ACT.Ln, bias=cst["eps6"]).then_inc(o_rooted, 1)
                    act.wait_ge(o_rooted, i * SUBS + s + 1 + START)
                    if s:
                        act.wait_ge(o_normed, i * SUBS + s + START)
                    act.activation(o_inv, o_sd, ACT.Exp, scale=-0.5).then_inc(o_inverted, 1)
                act_silu(SUBS - 1)

        @block.vector
        def _(dve):
            with dve.Fori(0, HALVES) as i:
                def centre(a):
                    src = bass.ds(i * HALF + a * TILE, TILE)
                    dve.wait_ge(summed_mean, i * HT + a + 1 + START)
                    if a:
                        dve.wait_ge(normed, i * HT + a + START)
                    dve.tensor_tensor(centred, hT[:, :, src], ps[:, 6:7, :].broadcast_to([P, KD, TILE]),
                                      ALU.subtract).then_inc(centred_s, 1)

                def scale(a):
                    dve.wait_ge(rooted, i * HT + a + 1 + START)
                    dve.reciprocal(inverse, deviation).then_inc(inverted, 1)
                    dve.wait_ge(inverted, i * HT + a + 1 + START)
                    dve.tensor_tensor(xn[:, :, a * TILE:(a + 1) * TILE], centred,
                                      inverse.unsqueeze(1).broadcast_to([P, KD, TILE]), ALU.mult).then_inc(normed, 1)

                def keep_gate_inputs():
                    dve.wait_ge(ab_summed, (i + 1) * SUBS + START)
                    dve.tensor_copy(ab[:, 0:2].rearrange("p k s h -> p s k h"),
                                    ps[:, 6, 0:256].rearrange("p (s k h) -> p s k h", k=2, h=HEADS)
                                    ).then_inc(ab_kept, 1)

                def tap(n, kind, j):
                    c = n % HC
                    if j == 0:
                        dve.wait_ge(raw_copied, i * 3 * UNITS + 3 * n + kind + 1 + START)
                    else:
                        dve.wait_ge(conv_step[kind], i * 3 * UNITS + 3 * n + j + START)
                    w = cols["conv"] + (kind * HC + c) * (CONV + 1) + j
                    dve.scalar_tensor_tensor(b(conv[kind]), padded[kind][:, :, j:j + L], vec[:, w:w + 1],
                                             b(conv[kind]), ALU.mult, ALU.add).then_inc(conv_step[kind], 1)

                def rotate(n):
                    for kind in range(2):
                        s = acted[n % 3][kind]
                        dve.wait_ge(acted_s[kind], i * UNITS + n + 1 + START)
                        if n:
                            dve.wait_ge(kq_ready, i * 2 * UNITS + 2 * (n - 1) + kind + 1 + START)
                        dve.tensor_tensor(b(cosine[kind]), b(s), cst["cos"].unsqueeze(1).broadcast_to([P, SEQ, L]),
                                          ALU.mult).then_inc(cosined, 1)
                        dve.stream_shuffle(swapped[kind], s, [q ^ 1 for q in range(32)]).then_inc(shuffled, 1)

                def add_rotated(n):
                    if n >= 2:
                        dve.wait_ge(scored, i * 2 * UNITS + 2 * (n - 1) + START)
                    for kind in range(2):
                        dve.wait_ge(cosined, i * 2 * UNITS + 2 * n + kind + 1 + START)
                        dve.wait_ge(sined, i * 2 * UNITS + 2 * n + kind + 1 + START)
                        dve.tensor_tensor(kq[n % 2][:, 1 - kind, :], cosine[kind], sine[kind],
                                          ALU.add).then_inc(kq_ready, 1)

                base = i * DVE_GATE + START

                def gate_step(k):
                    if k == 0:
                        dve.wait_ge(gates_turned, i * 2 + 1 + START)
                        dve.tensor_copy(gates[:, 0:2].rearrange("p a b -> p (a b)"),
                                        ps[:, 6, 0:2 * P]).then_inc(gates_kept, 1)
                        dve.wait_ge(gates_kept, i * 2 + 1 + START)
                        c = cols["dt"]
                        dve.tensor_scalar(g_small[:, 3, :], gates[:, 1, :], vec[:, c:c + 1], vec[:, c + 1:c + 2],
                                          ALU.add, ALU.add).then_inc(dve_gate, 1)
                    if k == 1:
                        dve.wait_ge(act_gate, i * ACT_GATE + 5 + START)
                        dve.scalar_tensor_tensor(g_small[:, 5, :], g_small[:, 3, :], 0.0, g_small[:, 5, :],
                                                 ALU.max, ALU.add).then_inc(dve_gate, 1)
                        dve.wait_ge(dve_gate, base + 2)
                        dve.tensor_scalar(g_small[:, 7, :], g_small[:, 5, :], nega[:, 0:1], -1.0,
                                          ALU.mult, ALU.mult).then_inc(dve_gate, 1)

                centre(0)
                scale(0)
                centre(1)
                for kind in range(3):
                    ins = dve.memset(padded[kind][:, :, 0:CONV - 1], 0.0)
                ins.then_inc(pads_clear, 1)
                for n in range(UNITS + 1):
                    if n < UNITS:
                        for j in range(CONV - 1):
                            for kind in range(2):
                                tap(n, kind, j)
                    if n >= 1:
                        rotate(n - 1)
                    if n < UNITS:
                        for j in range(CONV - 1):
                            tap(n, 2, j)
                    if n == 0:
                        scale(1)
                    if n >= 1:
                        add_rotated(n - 1)
                    if n == 2 + SUBS:
                        keep_gate_inputs()
                    if n == 4 + SUBS:
                        gate_step(0)
                    if n == UNITS:
                        gate_step(1)

                dve.wait_ge(lengths_summed, (i + 1) * UNITS + START)
                dve.tensor_copy(ab[:, 2].rearrange("p a b -> p (a b)"), ps[:, 7, 0:P]).then_inc(ab_kept, 1)
                dve.wait_ge(gates_turned, i * 2 + 2 + START)
                dve.tensor_copy(gates[:, 2, :], ps[:, 6, 2 * P:3 * P]).then_inc(gates_kept, 1)
                for g in range(1, ROW_GROUPS, 2):
                    dve.wait_ge(rows_turned, i * ROW_GROUPS + g + 1 + START)
                    dve.tensor_copy(kq_rows[:, 4 * g:4 * g + 4, :].rearrange("p a b -> p (a b)"),
                                    ps[:, g % 4, :]).then_inc(rows_kept_dve, 1)
                dve.wait_ge(rows_kept_act, (i + 1) * (ROW_GROUPS // 2) + START)
                dve.wait_ge(rows_kept_dve, (i + 1) * (ROW_GROUPS // 2) + START)
                for j in range(SPB):
                    dve.tensor_copy(g_small[:, 9, j * L:(j + 1) * L], diagonal(k_flat, j)).then_inc(diag_step, 1)
                for j in range(SPB):
                    dve.tensor_copy(g_small[:, 10, j * L:(j + 1) * L], diagonal(q_flat, j)).then_inc(diag_step, 1)
                dve.wait_ge(act_gate, i * ACT_GATE + 7 + START)
                dve.reciprocal(g_small[:, 6, :], g_small[:, 6, :]).then_inc(dve_gate, 1)
                dve.wait_ge(key_rooted, i + 1 + START)
                dve.reciprocal(g_small[:, 8, :], g_small[:, 8, :]).then_inc(dve_gate, 1)
                dve.wait_ge(dve_gate, base + 5)
                dve.tensor_tensor(g_small[:, 11, :], g_small[:, 1, :], g_small[:, 8, :],
                                  ALU.mult).then_inc(dve_gate, 1)
                dve.wait_ge(dve_gate, base + 6)
                dve.tensor_tensor(g_small[:, 2, :], g_small[:, 11, :], g_small[:, 8, :],
                                  ALU.mult).then_inc(dve_gate, 1)
                dve.wait_ge(diag_step, i * 2 * SPB + 2 * SPB + START)
                dve.scalar_tensor_tensor(g_small[:, 10, :], g_small[:, 10, :], vec[:, cols["Dp"]:cols["Dp"] + 1],
                                         g_small[:, 8, :], ALU.mult, ALU.mult).then_inc(dve_gate, 1)
                dve.wait_ge(dve_gate, base + 8)
                dve.tensor_tensor(g_small[:, 10, :], g_small[:, 10, :], g_small[:, 6, :],
                                  ALU.mult).then_inc(dve_gate, 1)
                dve.wait_ge(decay_ready, (i + 1) * (L - 1) + SPB + 1 + START)
                own = slice(0, DVE_SEQ)

                def by_row(x):
                    return x.rearrange("p (j t) -> p t j", j=SPB)[:, :, own].unsqueeze(3).broadcast_to(
                        [P, L, DVE_SEQ, L])

                dve.tensor_tensor(a4[:, :, own], a4[:, :, own], decay[:, :, own], ALU.mult).then_inc(dve_gate, 1)
                dve.tensor_tensor(g4[:, 1:L, own], g4[:, 1:L, own], decay[:, 0:L - 1, own], ALU.mult)
                dve.memset(g4[:, 0:1, own], 0.0).then_inc(dve_gate, 1)
                dve.wait_ge(dve_gate, base + 11)
                dve.tensor_tensor(a4[:, :, own], a4[:, :, own], by_row(g_small[:, 2, :]), ALU.mult)
                dve.tensor_tensor(g4[:, :, own], g4[:, :, own], by_row(g_small[:, 6, :]),
                                  ALU.mult).then_inc(tables_ready, 1)
                dve.wait_ge(tables_ready, i + 1 + START)
                tmp = product[:, 0:768]
                k = 0
                for t in range(L - 2, 0, -1):
                    j, r = slice(0, DVE_SEQ), L - 1 - t
                    out = tmp[:, 0:r * DVE_SEQ * t].rearrange("p (r j s) -> p r j s", r=r, j=DVE_SEQ)
                    if k:
                        dve.wait_ge(solved_dve, i * SOLVE + k + START)
                    dve.tensor_tensor(out, g4[:, t + 1:L, j, t:t + 1].broadcast_to([P, r, DVE_SEQ, t]),
                                      a4[:, t:t + 1, j, 0:t].broadcast_to([P, r, DVE_SEQ, t]),
                                      ALU.mult).then_inc(solved_dve, 1)
                    dve.wait_ge(solved_dve, i * SOLVE + k + 1 + START)
                    dve.tensor_tensor(g4[:, t + 1:L, j, 0:t], g4[:, t + 1:L, j, 0:t], out,
                                      ALU.subtract).then_inc(solved_dve, 1)
                    k += 2
                dve.wait_ge(solved_dve, i * SOLVE + SOLVE + START)
                scale = g_small[:, 11:12, :].rearrange("p o (j s) -> p o j s", j=SPB)[:, :, own]
                dve.tensor_tensor(g4[:, :, own], g4[:, :, own], scale.broadcast_to([P, L, DVE_SEQ, L]),
                                  ALU.mult).then_inc(table_scaled, 1)
                dve.wait_ge(solved_pool, (i + 1) * SOLVE_POOL + START)
                dve.wait_ge(table_scaled, i * (1 + SPB) + 1 + START)
                for j in range(SPB):
                    dve.tensor_copy(diagonal(q_flat, j), g_small[:, 10, j * L:(j + 1) * L]).then_inc(table_scaled, 1)
                for g in range(1, TURNS, 2):
                    dve.wait_ge(table_turned, i * TURNS + g + 1 + START)
                    dve.tensor_copy(table_rows[:, 4 * g:4 * g + 4].rearrange("p a b c -> p (a b c)"),
                                    ps[:, g % 4, :]).then_inc(table_kept_dve, 1)

                def spread_block(s):
                    if s == 0:
                        dve.wait_ge(table_kept_act, i * TURNS // 2 + TURNS // 2 + START)
                        dve.wait_ge(table_kept_dve, i * TURNS // 2 + TURNS // 2 + START)
                        dve.wait_ge(spread_clear, i * 2 + 2 + START)
                    if s >= 2:
                        dve.wait_ge(o_summed, i * SUBS + s - 1 + START)
                    for j in range(2):
                        q = slice(j * L, j * L + L)
                        dve.tensor_copy(spread[s % 2][q, :, q],
                                        table_rows[q, :, s, :].rearrange("p t h -> p h t")).then_inc(spread_dve, 1)

                def add_residual(s):
                    dve.wait_ge(out_summed, i * SUBS + s + 1 + START)
                    dst = hT[:, :, bass.ds(i * HALF + s * P, P)]
                    dve.tensor_tensor(dst, dst, ps[:, 6, 0:KD * P].rearrange("p (a b) -> p a b", a=KD),
                                      ALU.add).then_inc(residual, 1)

                spread_block(0)
                for s in range(SUBS + 1):
                    if s + 1 < SUBS:
                        spread_block(s + 1)
                    if s < SUBS:
                        dve.wait_ge(o_summed, i * SUBS + s + 1 + START)
                        if s >= 2:
                            dve.wait_ge(o_squared, i * SUBS + s - 1 + START)
                            dve.wait_ge(o_normed, i * SUBS + s - 1 + START)
                        dve.tensor_copy(o_sb[s % 2].rearrange("p a b -> p (a b)"),
                                        ps[:, 0:2, :].rearrange("p a b -> p (a b)")).then_inc(o_kept, 1)
                    if s:
                        dve.wait_ge(o_inverted, i * SUBS + s + START)
                        if s >= 2:
                            dve.wait_ge(o_acted, i * SUBS + s - 1 + START)
                        dve.scalar_tensor_tensor(o_norm, o_sb[(s - 1) % 2],
                                                 vec[:, cols["onorm"]:cols["onorm"] + 1], o_inv,
                                                 ALU.mult, ALU.mult).then_inc(o_normed, 1)
                    if s >= 2:
                        add_residual(s - 2)
                    if s:
                        dve.wait_ge(o_acted, i * SUBS + s + START)
                        dve.tensor_tensor(gated, o_act, gate[(s - 1) % 2], ALU.mult).then_inc(gated_s, 1)
                add_residual(SUBS - 1)


class Norm:

    def __init__(self, nc, mem, ps, mean_bank, var_bank, by_ln=False):
        self.by_ln = by_ln
        self.mem, self.ps, self.mean_bank, self.var_bank = mem, ps, mean_bank, var_bank
        self.centred, self.squared = mem.part([P, KD, TILE]), mem.part([P, KD, TILE])
        self.root = mem.part([P, TILE])
        self.xn = mem.part([P, KD, TILE])
        if mem.norm_sems is None:
            mem.norm_sems = named(nc, mem.ctx, "mean_summed norm_centred norm_squared var_summed norm_rooted "
                                  "norm_inverted norm_normed")
            self.opened = mem.norm_sems
        else:
            self.opened = []
        (self.mean_summed, self.is_centred, self.is_squared, self.var_summed, self.is_rooted, self.is_inverted,
         self.is_normed) = mem.norm_sems
        self.base = START + TILES * mem.norms
        mem.norms += 1

    def mean(self, pe, i):
        for k in range(KD):
            mm = pe.matmul(self.ps[:, self.mean_bank, :], self.mem.cst["mean"],
                           self.mem.hT[:, k, bass.ds(i * TILE, TILE)], start=(k == 0), stop=(k == KD - 1))
        mm.then_inc(self.mean_summed, 1)

    def variance(self, pe, i):
        pe.wait_ge(self.is_squared, i + 1 + self.base)
        for k in range(KD):
            mm = pe.matmul(self.ps[:, self.var_bank, :], self.mem.cst["mean"], self.squared[:, k, :],
                           start=(k == 0), stop=(k == KD - 1))
        mm.then_inc(self.var_summed, 1)

    def centre(self, dve, i):
        dve.wait_ge(self.mean_summed, i + 1 + self.base)
        dve.tensor_tensor(self.centred, self.mem.hT[:, :, bass.ds(i * TILE, TILE)],
                          self.ps[:, self.mean_bank:self.mean_bank + 1, :].broadcast_to([P, KD, TILE]),
                          ALU.subtract).then_inc(self.is_centred, 1)

    def scale(self, dve, i):
        if not self.by_ln:
            dve.wait_ge(self.is_rooted, i + 1 + self.base)
            dve.reciprocal(self.root, self.root).then_inc(self.is_inverted, 1)
        dve.wait_ge(self.is_inverted, i + 1 + self.base)
        dve.tensor_tensor(self.xn, self.centred, self.root.unsqueeze(1).broadcast_to([P, KD, TILE]),
                          ALU.mult).then_inc(self.is_normed, 1)

    def square(self, act, i):
        act.wait_ge(self.is_centred, i + 1 + self.base)
        act.activation(self.squared, self.centred, ACT.Square).then_inc(self.is_squared, 1)

    def take_root(self, act, i):
        act.wait_ge(self.var_summed, i + 1 + self.base)
        act.activation(self.root, self.ps[:, self.var_bank, :], ACT.Ln if self.by_ln else ACT.Sqrt,
                       bias=self.mem.cst["eps5"]).then_inc(self.is_rooted, 1)
        if self.by_ln:
            act.wait_ge(self.is_rooted, i + 1 + self.base)
            act.activation(self.root, self.root, ACT.Exp, scale=-0.5).then_inc(self.is_inverted, 1)


EXPERTS, RANK, FFN = 8, 64, 512
PAIRS = EXPERTS // 2
FC = FFN // P


def phase_experts(nc, mem, dram):
    hT, cst = mem.hT, mem.cst
    part = mem.part
    w_a = part([P, KD, EXPERTS * RANK])
    w_b = part([P, PAIRS, FFN])
    w_up = part([P, EXPERTS, KD, FFN])
    w_down = part([P, EXPERTS, FC, D])
    xn = part([P, KD, TILE])
    ghid = part([P, PAIRS, TILE])
    ghid_next = part([P, PAIRS, TILE])
    ghid_sq = part([P, PAIRS, TILE])
    silus = [part([P, TILE]) for _ in range(2)]
    acts = [part([P, TILE]) for _ in range(2)]
    weighted = [part([P, KD, TILE]) for _ in range(2)]
    SUBT = TILE // P
    score = part([P, SUBT, EXPERTS])
    score2, place = part([P, SUBT, EXPERTS]), part([P, SUBT, EXPERTS])
    top = part([P, SUBT, 2])
    first = part([P, SUBT, 1])
    gap, one_plus, share1, share2 = (part([P, SUBT, 1]) for _ in range(4))
    hot1, hot2 = part([P, SUBT, EXPERTS]), part([P, SUBT, EXPERTS])
    share = part([P, SUBT, EXPERTS])
    shareT = part([EXPERTS, TILE])
    one_row = part([EXPERTS, EXPERTS, P])
    with ExitStack() as ctx:
        ps = ctx.enter_context(nc.psum_tensor("ps_experts", [P, 8, 512], F32))
        norm = Norm(nc, mem, ps, 6, 6)
        sems = (wa_in, hid_summed, hid_squared, xn_kept, ghid_ready, score_summed, score_rooted, route, gap_exp, share_ready,
                share_turned, shareT_ready, share_spread, x_weighted, gate_summed, up_summed, silu_ready,
                act_ready, down_step, rows_made, residual) = named(nc, mem.ctx, (
                    "wa_in moe_hid_summed moe_hid_squared xn_kept ghid_ready score_summed score_rooted route gap_exp "
                    "share_ready share_turned shareT_ready share_spread x_weighted gate_summed up_summed silu_ready "
                    "act_ready down_step moe_rows_made moe_residual"))
        expert_in = named(nc, mem.ctx, " ".join(f"expert_in_{e}" for e in range(EXPERTS)))
        block = ctx.enter_context(nc.Block())
        STEPS = EXPERTS * FC
        ROUTE = 17

        @block.sync
        def _(sp):
            open_phase(sp, [*sems, *expert_in, *norm.opened])
            sp.dma_start(w_a, dram["W_A"]).then_inc(wa_in, 16)
            sp.dma_start(w_b, dram["W_B"]).then_inc(wa_in, 16)
            for e in range(EXPERTS):
                sp.dma_start(w_up[:, e], dram["W_up"][:, e]).then_inc(expert_in[e], 16)
                sp.dma_start(w_down[:, e], dram["W_down"][:, e]).then_inc(expert_in[e], 16)

        @block.gpsimd
        def _(pool):
            pool.tensor_copy(one_row, cst["ident"][0:EXPERTS, 0:EXPERTS].unsqueeze(2).broadcast_to(
                [EXPERTS, EXPERTS, P])).then_inc(rows_made, 1)

        @block.tensor
        def _(pe):
            def hidden(t, g):
                if g:
                    pe.wait_ge(hid_squared, t * PAIRS + g + START)
                else:
                    pe.wait_ge(norm.is_normed, t + 1 + norm.base)
                for k in range(KD):
                    mm = pe.matmul(ps[:, 6, :], w_a[:, k, g * P:(g + 1) * P], norm.xn[:, k, :],
                                   start=(k == 0), stop=(k == KD - 1))
                mm.then_inc(hid_summed, 1)

            def spread(i, e):
                if e == 0:
                    pe.wait_ge(shareT_ready, i + 1 + START)
                pe.wait_ge(x_weighted, i * EXPERTS + e + START)
                pe.matmul(ps[:, 7, :], one_row[:, e, :], shareT, start=True, stop=True).then_inc(share_spread, 1)

            def prologue(t, q):
                if q == 2:
                    pe.wait_ge(shareT_ready, t + START)
                    norm.mean(pe, t)
                if q == 5:
                    norm.variance(pe, t)
                if q in (9, 11, 13, 15):
                    hidden(t, (q - 9) // 2)
                if q == 18:
                    pe.wait_ge(hid_squared, (t + 1) * PAIRS + START)
                    for s in range(SUBT):
                        for g in range(PAIRS):
                            mm = pe.matmul(ps[:, 6, s * EXPERTS:(s + 1) * EXPERTS], ghid_sq[:, g, s * P:(s + 1) * P],
                                           cst["expert_of"][:, g * EXPERTS:(g + 1) * EXPERTS],
                                           start=(g == 0), stop=(g == PAIRS - 1))
                    mm.then_inc(score_summed, 1)
                if q == 25:
                    pe.wait_ge(share_ready, t + 1 + START)
                    for s in range(SUBT):
                        mm = pe.transpose(ps[0:EXPERTS, 6, s * P:(s + 1) * P], share[:, s, :], cst["ident"])
                    mm.then_inc(share_turned, 1)
                if q == 28:
                    spread(t, 0)

            def up(i, q):
                e, m = divmod(q, FC)
                h = slice((e % 2) * RANK, (e % 2) * RANK + RANK)
                if q >= 2:
                    pe.wait_ge(silu_ready, i * STEPS + q - 1 + START)
                if q % (2 * FC) == 0:
                    pe.wait_ge(ghid_ready, i * PAIRS + e // 2 + 1 + START)
                pe.matmul(ps[:, q % 2, :], w_b[h, e // 2, m * P:(m + 1) * P], ghid[h, e // 2, :],
                          start=True, stop=True).then_inc(gate_summed, 1)
                if q >= 2:
                    pe.wait_ge(act_ready, i * STEPS + q - 1 + START)
                if m == 0:
                    pe.wait_ge(x_weighted, i * EXPERTS + e + 1 + START)
                    pe.wait_ge(expert_in[e], 32 + START)
                for k in range(KD):
                    mm = pe.matmul(ps[:, 2 + q % 2, :], w_up[:, e, k, m * P:(m + 1) * P],
                                   weighted[e % 2][:, k, :], start=(k == 0), stop=(k == KD - 1))
                mm.then_inc(up_summed, 1)

            def down(i, q):
                e, m = divmod(q, FC)
                pe.wait_ge(act_ready, i * STEPS + q + 1 + START)
                for c in range(KD):
                    mm = pe.matmul(ps[:, 4 + c, :], w_down[:, e, m, c * P:(c + 1) * P], acts[q % 2],
                                   start=(q == 0), stop=(q == STEPS - 1))
                mm.then_inc(down_step, 1)

            def tile(i, more):
                for q in range(STEPS + 1):
                    if q < STEPS:
                        up(i, q)
                        if q % FC == 1 and q // FC + 1 < EXPERTS:
                            spread(i, q // FC + 1)
                        if more:
                            prologue(i + 1, q)
                    if q == 1:
                        pe.wait_ge(residual, i + START)
                    if q:
                        down(i, q - 1)

            norm.mean(pe, 0)
            norm.variance(pe, 0)
            pe.wait_ge(wa_in, 32 + START)
            pe.wait_ge(rows_made, 1 + START)
            for q in range(9, STEPS):
                prologue(0, q)
            with pe.Fori(0, TILES - 1) as i:
                tile(i, True)
            tile(TILES - 1, False)

        @block.scalar
        def _(act):
            def prologue(t, q):
                if q == 4:
                    norm.square(act, t)
                if q == 6:
                    norm.take_root(act, t)
                if q in (10, 12, 14, 16):
                    g = (q - 10) // 2
                    act.wait_ge(hid_summed, t * PAIRS + g + 1 + START)
                    if g == 0:
                        act.wait_ge(ghid_ready, t * PAIRS + START)
                    act.activation(ghid_next[:, g, :], ps[:, 6, :], ACT.Copy)
                    act.activation(ghid_sq[:, g, :], ps[:, 6, :], ACT.Square).then_inc(hid_squared, 1)
                if q == 19:
                    act.wait_ge(score_summed, t + 1 + START)
                    act.activation(score.rearrange("p a b -> p (a b)"), ps[:, 6, 0:SUBT * EXPERTS],
                                   ACT.Sqrt).then_inc(score_rooted, 1)
                if q == 22:
                    act.wait_ge(route, t * ROUTE + 12 + START)
                    act.activation(share2, gap, ACT.Exp).then_inc(gap_exp, 1)
                if q == 27:
                    act.wait_ge(norm.is_normed, t + 1 + norm.base)
                    act.wait_ge(x_weighted, t * EXPERTS + START)
                    act.activation(xn, norm.xn, ACT.Copy).then_inc(xn_kept, 1)

            def keep_hidden(t):
                act.wait_ge(hid_squared, (t + 1) * PAIRS + START)
                for g in range(PAIRS):
                    act.activation(ghid[:, g, :], ghid_next[:, g, :], ACT.Copy).then_inc(ghid_ready, 1)

            def tile(i, more):
                for q in range(STEPS):
                    act.wait_ge(gate_summed, i * STEPS + q + 1 + START)
                    if q >= 2:
                        act.wait_ge(act_ready, i * STEPS + q - 1 + START)
                    act.activation(silus[q % 2], ps[:, q % 2, :], ACT.Silu).then_inc(silu_ready, 1)
                    if more:
                        prologue(i + 1, q)
                if more:
                    keep_hidden(i + 1)

            for q in range(STEPS):
                prologue(0, q)
            keep_hidden(0)
            with act.Fori(0, TILES - 1) as i:
                tile(i, True)
            tile(TILES - 1, False)

        @block.vector
        def _(dve):
            number = cst["number"].unsqueeze(1).broadcast_to([P, SUBT, EXPERTS])
            wide = [P, SUBT, EXPERTS]

            def choose(t):
                dve.wait_ge(score_rooted, t + 1 + START)
                step = t * ROUTE + START
                k = 0
                for j, (left, hot) in enumerate(((score, hot1), (score2, hot2))):
                    dve.tensor_reduce(top[:, :, j:j + 1], left, AX.X, ALU.max).then_inc(route, 1)
                    dve.wait_ge(route, step + k + 1)
                    dve.tensor_tensor(hot, left, top[:, :, j:j + 1].broadcast_to(wide), ALU.is_equal).then_inc(route, 1)
                    dve.wait_ge(route, step + k + 2)
                    dve.tensor_tensor(place, hot, number, ALU.mult).then_inc(route, 1)
                    dve.wait_ge(route, step + k + 3)
                    dve.tensor_reduce(first, place, AX.X, ALU.min).then_inc(route, 1)
                    dve.wait_ge(route, step + k + 4)
                    dve.tensor_tensor(hot, number, first.broadcast_to(wide), ALU.is_equal).then_inc(route, 1)
                    if j == 0:
                        dve.wait_ge(route, step + k + 5)
                        dve.scalar_tensor_tensor(score2, hot1, -1e38, score, ALU.mult, ALU.add).then_inc(route, 1)
                        dve.wait_ge(route, step + k + 6)
                        k += 6
                dve.tensor_tensor(gap, top[:, :, 1:2], top[:, :, 0:1], ALU.subtract).then_inc(route, 1)

            def shares(t):
                step = t * ROUTE + START
                dve.wait_ge(gap_exp, t + 1 + START)
                dve.tensor_scalar(one_plus, share2, 1.0, None, ALU.add).then_inc(route, 1)
                dve.wait_ge(route, step + 13)
                dve.reciprocal(share1, one_plus).then_inc(route, 1)
                dve.wait_ge(route, step + 14)
                dve.tensor_tensor(share2, share2, share1, ALU.mult).then_inc(route, 1)
                dve.tensor_tensor(hot1, hot1, share1.broadcast_to(wide), ALU.mult).then_inc(route, 1)
                dve.wait_ge(route, step + 16)
                dve.tensor_tensor(hot2, hot2, share2.broadcast_to(wide), ALU.mult).then_inc(route, 1)
                dve.wait_ge(route, step + 17)
                dve.tensor_tensor(share, hot1, hot2, ALU.add).then_inc(share_ready, 1)

            def weight(i, e, first=False):
                dve.wait_ge(share_spread, i * EXPERTS + e + 1 + START)
                if e == 0:
                    dve.wait_ge(xn_kept, i + 1 + START)
                if not first:
                    dve.wait_ge(up_summed, i * STEPS + (e - 1) * FC + START)
                dve.tensor_tensor(weighted[e % 2], xn, ps[:, 7:8, :].broadcast_to([P, KD, TILE]),
                                  ALU.mult).then_inc(x_weighted, 1)

            def prologue(t, q, first=False):
                if q == 2:
                    norm.centre(dve, t)
                if q == 7:
                    dve.wait_ge(xn_kept, t + START)
                    norm.scale(dve, t)
                if q == 20:
                    choose(t)
                if q == 23:
                    shares(t)
                if q == 26:
                    dve.wait_ge(share_turned, t + 1 + START)
                    dve.wait_ge(share_spread, t * EXPERTS + START)
                    dve.tensor_copy(shareT, ps[0:EXPERTS, 6, :]).then_inc(shareT_ready, 1)
                if q == 29:
                    weight(t, 0, first)

            def tile(i, more):
                for q in range(STEPS):
                    dve.wait_ge(silu_ready, i * STEPS + q + 1 + START)
                    dve.wait_ge(up_summed, i * STEPS + q + 1 + START)
                    if q >= 2:
                        dve.wait_ge(down_step, i * STEPS + q - 1 + START)
                    dve.tensor_tensor(acts[q % 2], silus[q % 2], ps[:, 2 + q % 2, :], ALU.mult).then_inc(act_ready, 1)
                    if q % FC == 1 and q // FC + 1 < EXPERTS:
                        weight(i, q // FC + 1)
                    if more:
                        prologue(i + 1, q)
                dve.wait_ge(down_step, (i + 1) * STEPS + START)
                dst = hT[:, :, bass.ds(i * TILE, TILE)]
                dve.tensor_tensor(dst, dst, ps[:, 4:6, :], ALU.add).then_inc(residual, 1)

            for q in range(STEPS):
                prologue(0, q, first=True)
            with dve.Fori(0, TILES - 1) as i:
                tile(i, True)
            tile(TILES - 1, False)


INNER1, STATES, DT_RANK = 512, 16, 16
IC = INNER1 // P
BC = 2 * STATES


def phase_state_space(nc, mem, dram):
    hT, vec, cols, cst = mem.hT, mem.vec, mem.cols, mem.cst
    part = mem.part
    w_in = part([P, KD, 2 * INNER1])
    w_x = part([P, IC, 3 * BC + DT_RANK])
    w_dt = part([DT_RANK, INNER1])
    w_out = part([P, IC, D])
    one_row = part([3 * BC, BC * P // 2]).bitcast(BF16).rearrange("p (a b) -> p a b", b=P)
    neg_a = part([P, IC * STATES])
    padded = part([P, IC * SEQ, L + CONV - 1])
    u = part([P, IC, TILE])
    skip = part([P, IC, TILE])
    conv = part([P, IC, TILE])
    gate = part([P, IC, TILE])
    gate_next = part([P, IC, TILE])
    dbc = part([3 * BC, TILE])
    dt_in = part([DT_RANK, TILE])
    high = part([3 * BC, TILE // 2]).bitcast(BF16)
    middle = part([3 * BC, TILE // 2]).bitcast(BF16)
    rest = part([3 * BC, TILE])
    pieces = part([3 * BC, TILE // 2]).bitcast(BF16)
    z_raw = part([P, IC, TILE])
    z = part([P, IC, TILE])
    soft = part([P, IC, TILE])
    delta_u = part([P, IC, TILE])
    factor = [part([P, IC, TILE]) for _ in range(2)]
    state = [part([P, IC, TILE]) for _ in range(2)]
    c_rows = [part([P, TILE]) for _ in range(2)]
    read = [part([P, IC, TILE]) for _ in range(2)]
    y = soft

    def b(x):
        return x.rearrange("p (a b) -> p a b", b=L)

    with ExitStack() as ctx:
        ps = ctx.enter_context(nc.psum_tensor("ps_state_space", [P, 8, 512], F32))
        norm = Norm(nc, mem, ps, 6, 7, by_ln=True)
        sems = (weights_in, a_exp, a_neg, rows_made, pads_clear, proj_summed, proj_read, conv_step, u_ready,
                skip_ready, gate_ready, high_ready, rest_ready, middle_ready, pieces_ready, soft_step, delta_ready,
                du_ready, starts_cut, b_spread, c_spread, c_kept, factor_ready, input_ready, state_ready,
                read_ready, y_summed, y_added, y_gated, out_summed, residual) = named(nc, mem.ctx, (
                    "ssm_weights_in a_exp a_neg rows_made ssm_pads_clear proj_summed proj_read ssm_conv_step "
                    "ssm_u_ready skip_ready ssm_gate_ready high_ready rest_ready middle_ready pieces_ready "
                    "soft_step delta_ready du_ready starts_cut b_spread c_spread c_kept factor_ready input_ready "
                    "state_ready read_ready y_summed y_added y_gated ssm_out_summed ssm_residual"))
        block = ctx.enter_context(nc.Block())
        TAPS = (CONV - 1) * IC
        GATE, DBC_AT, LAST_GATE, DT = IC, 2 * IC - 1, 2 * IC, 2 * IC + 1
        PROJ = 3 * IC + 1

        def proj_bank(t, j):
            return 6 + j % 2

        @block.sync
        def _(sp):
            open_phase(sp, [*sems, *norm.opened])
            sp.dma_start(w_in, dram["W_in"]).then_inc(weights_in, 16)
            sp.dma_start(w_x, dram["W_x"]).then_inc(weights_in, 16)
            sp.dma_start(w_dt, dram["W_dt"]).then_inc(weights_in, 16)
            sp.dma_start(w_out, dram["W_out"]).then_inc(weights_in, 16)

        @block.gpsimd
        def _(pool):
            pool.memset(padded[:, :, 0:CONV - 1], 0.0).then_inc(pads_clear, 1)
            with pool.Fori(0, TILES) as i:
                for n in range(STATES):
                    pool.wait_ge(c_kept, i * STATES + n + 1 + START)
                    pool.wait_ge(state_ready, i * STATES + n + 1 + START)
                    pool.wait_ge(y_summed, i * STATES + n - 1 + START)
                    pool.tensor_tensor(read[n % 2], state[n % 2], c_rows[n % 2].unsqueeze(1).broadcast_to(
                        [P, IC, TILE]), ALU.mult).then_inc(read_ready, 1)

        @block.tensor
        def _(pe):
            def project(t, j):
                if j >= 2:
                    pe.wait_ge(proj_read, t * PROJ + j - 2 + 1 + START)
                bank = proj_bank(t, j)
                if j < DBC_AT or j == LAST_GATE:
                    m = min(j, 2 * IC - 1)
                    for k in range(KD):
                        mm = pe.matmul(ps[:, bank, :], w_in[:, k, m * P:(m + 1) * P], norm.xn[:, k, :],
                                       start=(k == 0), stop=(k == KD - 1))
                elif j == DBC_AT:
                    pe.wait_ge(u_ready, t + 1 + START)
                    for k in range(IC):
                        mm = pe.matmul(ps[0:3 * BC + DT_RANK, bank, :], w_x[:, k, :], u[:, k, :],
                                       start=(k == 0), stop=(k == IC - 1))
                else:
                    pe.wait_ge(proj_read, t * PROJ + DBC_AT + 1 + START)
                    m = j - DT
                    mm = pe.matmul(ps[:, bank, :], w_dt[:, m * P:(m + 1) * P], dt_in, start=True, stop=True)
                mm.then_inc(proj_summed, 1)

            def prologue(t, slot):
                if slot == 2:
                    pe.wait_ge(residual, t - 1 + START)
                    norm.mean(pe, t)
                if slot == 4:
                    norm.variance(pe, t)
                if slot == 5:
                    pe.wait_ge(norm.is_normed, t + 1 + norm.base)
                for j in PE_SLOTS.get(slot, ()):
                    project(t, j)

            def spread(i, n):
                if n == 0:
                    pe.wait_ge(pieces_ready, (i + 1) * 3 + START)
                pe.wait_ge(input_ready, i * STATES + n + START)
                pe.matmul(ps[:, 4, :], one_row[:, n, :], pieces, start=True, stop=True).then_inc(b_spread, 1)
                pe.wait_ge(c_kept, i * STATES + n + START)
                pe.matmul(ps[:, 5, :], one_row[:, STATES + n, :], pieces, start=True,
                          stop=True).then_inc(c_spread, 1)

            def gather(i, n):
                pe.wait_ge(read_ready, i * STATES + n + 1 + START)
                if n == 0:
                    pe.wait_ge(y_added, i * IC + START)
                for c in range(IC):
                    mm = pe.matmul(ps[:, c, :], cst["ident"], read[n % 2][:, c, :],
                                   start=(n == 0), stop=(n == STATES - 1))
                mm.then_inc(y_summed, 1)

            def tile(i, more):
                for n in range(2, STATES):
                    spread(i, n)
                    if more:
                        prologue(i + 1, n)
                    gather(i, n - 2)
                if more:
                    prologue(i + 1, STATES)
                    spread(i + 1, 0)
                gather(i, STATES - 2)
                gather(i, STATES - 1)
                if more:
                    spread(i + 1, 1)
                if more:
                    pe.wait_ge(proj_read, (i + 2) * PROJ + START)
                for k in range(IC):
                    pe.wait_ge(y_gated, i * IC + k + 1 + START)
                    for m in range(KD):
                        mm = pe.matmul(ps[:, 6 + m, :], w_out[:, k, m * P:(m + 1) * P], y[:, k, :],
                                       start=(k == 0), stop=(k == IC - 1))
                mm.then_inc(out_summed, 1)

            PE_SLOTS = {5: (0,), 6: (1, 2), 7: (3,), 8: (4,), 9: (5,), 10: (6,), 11: (7,), 12: (8,), 13: (9, 10),
                        14: (11, 12)}
            norm.mean(pe, 0)
            norm.variance(pe, 0)
            pe.wait_ge(weights_in, 64 + START)
            for slot in range(5, STATES):
                prologue(0, slot)
            pe.wait_ge(rows_made, 3 + START)
            spread(0, 0)
            spread(0, 1)
            with pe.Fori(0, TILES - 1) as i:
                tile(i, True)
            tile(TILES - 1, False)

        @block.scalar
        def _(act):
            def take(t, j):
                act.wait_ge(proj_summed, t * PROJ + j + 1 + START)
                bank = proj_bank(t, j)
                if j < GATE:
                    if j == 0:
                        act.wait_ge(u_ready, t + START)
                    w = cols["ssm_conv"] + j * (CONV + 1)
                    act.activation(padded[:, j * SEQ:(j + 1) * SEQ, CONV - 1:], b(ps[:, bank, :]), ACT.Copy)
                    act.activation(conv[:, j, :], ps[:, bank, :], ACT.Identity, bias=vec[:, w + CONV:w + CONV + 1],
                                   scale=vec[:, w + CONV - 1:w + CONV]).then_inc(proj_read, 1)
                elif j < DBC_AT or j == LAST_GATE:
                    if j == GATE:
                        act.wait_ge(gate_ready, t + START)
                    act.activation(gate_next[:, min(j, LAST_GATE - 1) - GATE, :], ps[:, bank, :], ACT.Copy).then_inc(proj_read, 1)
                elif j == DBC_AT:
                    act.activation(dbc, ps[0:3 * BC, bank, :], ACT.Copy).then_inc(high_ready, 1)
                    act.activation(dt_in, ps[3 * BC:3 * BC + DT_RANK, bank, :], ACT.Copy).then_inc(proj_read, 1)
                else:
                    if j == DT:
                        act.wait_ge(delta_ready, t + START)
                    w = cols["ssm_b_dt"] + j - DT
                    if j == DT:
                        act.wait_ge(out_summed, t - 1 + START)
                    act.activation(z_raw[:, j - DT, :], ps[:, bank, :], ACT.Identity, bias=vec[:, w:w + 1])
                    act.activation(soft[:, j - DT, :], ps[:, bank, :], ACT.Abs,
                                   bias=vec[:, w:w + 1]).then_inc(proj_read, 1)

            def prologue(t, slot):
                if slot == 3:
                    norm.square(act, t)
                if slot == 4:
                    norm.take_root(act, t)
                for j in ACT_SLOTS.get(slot, ()):
                    take(t, j)
                if slot == 10:
                    act.wait_ge(conv_step, (t + 1) * TAPS + START)
                    act.wait_ge(skip_ready, t * IC + START)
                    act.activation(u, conv, ACT.Silu).then_inc(u_ready, 1)
                if slot == 12:
                    act.wait_ge(high_ready, t * 2 + 1 + START)
                    act.wait_ge(pieces_ready, t * 3 + START)
                    act.activation(high, dbc, ACT.Copy).then_inc(high_ready, 1)
                if slot == 13:
                    act.wait_ge(rest_ready, t * 2 + 1 + START)
                    act.activation(middle, rest, ACT.Copy).then_inc(middle_ready, 1)
                if slot == 15:
                    act.wait_ge(proj_read, (t + 1) * PROJ + START)
                    act.activation(soft, soft, ACT.Exp, scale=-1.0).then_inc(soft_step, 1)
                    act.wait_ge(soft_step, t * 2 + 1 + START)
                    act.activation(soft, soft, ACT.Ln, bias=cst["one"]).then_inc(soft_step, 1)
                if slot == STATES:
                    act.wait_ge(c_spread, t * STATES + START)
                    act.wait_ge(rest_ready, (t + 1) * 2 + START)
                    for piece, source in enumerate((high, middle, rest)):
                        rows = slice(piece * BC, (piece + 1) * BC)
                        act.activation(pieces[rows], source[rows], ACT.Copy).then_inc(pieces_ready, 1)

            def factors(i, n):
                if n == 0:
                    act.wait_ge(starts_cut, i + 1 + START)
                act.wait_ge(state_ready, i * STATES + n - 1 + START)
                for c in range(IC):
                    w = c * STATES + n
                    act.activation(factor[n % 2][:, c, :], z[:, c, :], ACT.Exp,
                                   scale=neg_a[:, w:w + 1]).then_inc(factor_ready, 1)

            def keep_c(i, n):
                act.wait_ge(c_spread, i * STATES + n + 1 + START)
                act.wait_ge(read_ready, i * STATES + n - 1 + START)
                act.activation(c_rows[n % 2], ps[:, 5, :], ACT.Copy).then_inc(c_kept, 1)

            def first_states(i):
                for n in range(2):
                    factors(i, n)
                    keep_c(i, n)
                act.wait_ge(proj_read, (i + 1) * PROJ + START)
                act.wait_ge(y_gated, i * IC + START)
                act.wait_ge(u_ready, i + 1 + START)
                act.activation(gate, gate_next, ACT.Silu).then_inc(gate_ready, 1)
                for c in range(IC):
                    w = cols["ssm_D"] + c
                    act.activation(skip[:, c, :], u[:, c, :], ACT.Identity, bias=cst["zero"],
                                   scale=vec[:, w:w + 1]).then_inc(skip_ready, 1)

            def tile(i, more):
                for n in range(2, STATES):
                    factors(i, n)
                    if more:
                        prologue(i + 1, n)
                    keep_c(i, n)
                if more:
                    prologue(i + 1, STATES)
                    first_states(i + 1)

            ACT_SLOTS = {6: (0,), 7: (1, 2), 8: (3,), 9: (4,), 10: (5,), 11: (6,), 12: (7,), 13: (8,), 14: (9, 10),
                         15: (11, 12)}
            c = cols["ssm_A_log"]
            act.activation(neg_a, vec[:, c:c + IC * STATES], ACT.Exp).then_inc(a_exp, 1)
            norm.square(act, 0)
            norm.take_root(act, 0)
            act.wait_ge(pads_clear, 1 + START)
            for slot in range(6, STATES + 1):
                prologue(0, slot)
            act.wait_ge(a_neg, 1 + START)
            first_states(0)
            with act.Fori(0, TILES - 1) as i:
                tile(i, True)
            tile(TILES - 1, False)

        @block.vector
        def _(dve):
            def taps(t, c):
                for j in range(CONV - 1):
                    if j == 0:
                        dve.wait_ge(proj_read, t * PROJ + c + 1 + START)
                    else:
                        dve.wait_ge(conv_step, t * TAPS + c * (CONV - 1) + j + START)
                    w = cols["ssm_conv"] + c * (CONV + 1) + j
                    dve.scalar_tensor_tensor(b(conv[:, c, :]), padded[:, c * SEQ:(c + 1) * SEQ, j:j + L],
                                             vec[:, w:w + 1], b(conv[:, c, :]), ALU.mult,
                                             ALU.add).then_inc(conv_step, 1)

            def prologue(t, slot):
                if slot == 2:
                    norm.centre(dve, t)
                if slot == 4:
                    norm.scale(dve, t)
                if 6 <= slot < 6 + IC:
                    taps(t, slot - 6)
                if slot == 12:
                    dve.wait_ge(high_ready, (t + 1) * 2 + START)
                    dve.wait_ge(pieces_ready, t * 3 + START)
                    dve.tensor_tensor(rest, dbc, high, ALU.subtract).then_inc(rest_ready, 1)
                if slot == 13:
                    dve.wait_ge(middle_ready, t + 1 + START)
                    dve.tensor_tensor(rest, rest, middle, ALU.subtract).then_inc(rest_ready, 1)
                if slot == STATES:
                    dve.wait_ge(soft_step, (t + 1) * 2 + START)
                    dve.wait_ge(factor_ready, t * STATES * IC + START)
                    dve.scalar_tensor_tensor(z, z_raw, 0.0, soft, ALU.max, ALU.add).then_inc(delta_ready, 1)
                    dve.wait_ge(delta_ready, t + 1 + START)
                    dve.wait_ge(input_ready, t * STATES + START)
                    dve.tensor_tensor(delta_u, z, u, ALU.mult).then_inc(du_ready, 1)
                    dve.wait_ge(du_ready, t + 1 + START)
                    dve.memset(z.rearrange("p c (q t) -> p (c q) t", t=L)[:, :, 0:1], 1e30).then_inc(starts_cut, 1)

            def scan(i, n):
                dve.wait_ge(b_spread, i * STATES + n + 1 + START)
                dve.wait_ge(read_ready, i * STATES + n - 1 + START)
                dve.tensor_tensor(state[n % 2], delta_u, ps[:, 4:5, :].broadcast_to([P, IC, TILE]),
                                  ALU.mult).then_inc(input_ready, 1)
                dve.wait_ge(input_ready, i * STATES + n + 1 + START)
                dve.wait_ge(factor_ready, i * STATES * IC + (n + 1) * IC + START)
                s = state[n % 2].rearrange("p a b -> p (a b)")
                dve.tensor_tensor_scan(s, factor[n % 2].rearrange("p a b -> p (a b)"), s, 0.0, ALU.mult,
                                       ALU.add).then_inc(state_ready, 1)

            def tile(i, more):
                for n in range(2, STATES):
                    scan(i, n)
                    if more:
                        prologue(i + 1, n)
                if more:
                    prologue(i + 1, STATES)
                    scan(i + 1, 0)
                dve.wait_ge(y_summed, (i + 1) * STATES + START)
                dve.wait_ge(skip_ready, (i + 1) * IC + START)
                dve.wait_ge(gate_ready, i + 1 + START)
                for c in range(IC + 1):
                    if c < IC:
                        dve.tensor_tensor(y[:, c, :], skip[:, c, :], ps[:, c, :], ALU.add).then_inc(y_added, 1)
                    if c:
                        dve.wait_ge(y_added, i * IC + c + START)
                        dve.tensor_tensor(y[:, c - 1, :], y[:, c - 1, :], gate[:, c - 1, :],
                                          ALU.mult).then_inc(y_gated, 1)
                if more:
                    scan(i + 1, 1)
                dve.wait_ge(out_summed, i + 1 + START)
                dst = hT[:, :, bass.ds(i * TILE, TILE)]
                dve.tensor_tensor(dst, dst, ps[:, 6:8, :], ALU.add).then_inc(residual, 1)

            dve.wait_ge(a_exp, 1 + START)
            dve.tensor_scalar(neg_a, neg_a, -1.0, None, ALU.mult).then_inc(a_neg, 1)
            norm.centre(dve, 0)
            norm.scale(dve, 0)
            for piece in range(3):
                rows = slice(piece * BC, (piece + 1) * BC)
                dve.tensor_copy(one_row[rows], cst["ident"][rows, rows].unsqueeze(2).broadcast_to(
                    [BC, BC, P])).then_inc(rows_made, 1)
            for slot in range(6, STATES + 1):
                prologue(0, slot)
            scan(0, 0)
            scan(0, 1)
            with dve.Fori(0, TILES - 1) as i:
                tile(i, True)
            tile(TILES - 1, False)


def phase_last(nc, mem, dram, out):
    hT, vec, cols, cst = mem.hT, mem.vec, mem.cols, mem.cst
    part = mem.part
    wT, a1, a2, first, whole = (part([P, KD, D]) for _ in range(5))
    tanh = part([P, KD, TILE])
    h_out = part([P, KD, TILE])
    rows = part([P, TILE // P, D])
    with ExitStack() as ctx:
        ps = ctx.enter_context(nc.psum_tensor("ps_last", [P, 8, 512], F32))
        norm = Norm(nc, mem, ps, 6, 7)
        sems = (weights_in, first_summed, first_kept, whole_summed, whole_kept, lin_summed, tanh_ready, h_ready,
                turned, rows_ready, written) = named(nc, mem.ctx, (
                    "last_weights_in first_summed first_kept whole_summed whole_kept lin_summed tanh_ready h_ready "
                    "turned rows_ready written"))
        block = ctx.enter_context(nc.Block())

        @block.sync
        def _(sp):
            open_phase(sp, [*sems, *norm.opened])
            for w, name in ((wT, "ffn_wT"), (a1, "ffn_a1"), (a2, "ffn_a2")):
                sp.dma_start(w, dram[name]).then_inc(weights_in, 16)
            with sp.Fori(0, TILES) as i:
                sp.wait_ge(rows_ready, i + 1 + START)
                sp.dma_start(out[bass.ds(i * (TILE // P), TILE // P)].rearrange("s p d -> p s d"),
                             rows).then_inc(written, 16)
            sp.wait_ge(written, 16 * TILES + START)

        @block.tensor
        def _(pe):
            norm.mean(pe, 0)
            norm.variance(pe, 0)
            pe.wait_ge(weights_in, 48 + START)
            for m in range(KD):
                for k in range(KD):
                    mm = pe.matmul(ps[:, m, 0:D], a1[:, k, m * P:(m + 1) * P], wT[:, k, :],
                                   start=(k == 0), stop=(k == KD - 1))
            mm.then_inc(first_summed, 1)
            pe.wait_ge(first_kept, 1 + START)
            for m in range(KD):
                for k in range(KD):
                    mm = pe.matmul(ps[:, 2 + m, 0:D], first[:, k, m * P:(m + 1) * P], a2[:, k, :],
                                   start=(k == 0), stop=(k == KD - 1))
            mm.then_inc(whole_summed, 1)
            pe.wait_ge(whole_kept, 1 + START)

            def tile(i, more):
                pe.wait_ge(norm.is_normed, i + 1 + norm.base)
                pe.wait_ge(tanh_ready, i * KD + START)
                for m in range(KD):
                    for k in range(KD):
                        mm = pe.matmul(ps[:, m, :], whole[:, k, m * P:(m + 1) * P], norm.xn[:, k, :],
                                       start=(k == 0), stop=(k == KD - 1))
                mm.then_inc(lin_summed, 1)
                if more:
                    norm.mean(pe, i + 1)
                    norm.variance(pe, i + 1)
                pe.wait_ge(h_ready, i + 1 + START)
                pe.wait_ge(rows_ready, i + START)
                for s in range(TILE // P):
                    for k in range(KD):
                        mm = pe.transpose(ps[:, 2 + s // 2, (s % 2) * D + k * P:(s % 2) * D + (k + 1) * P],
                                          h_out[:, k, s * P:(s + 1) * P], cst["ident"])
                mm.then_inc(turned, 1)

            with pe.Fori(0, TILES - 1) as i:
                tile(i, True)
            tile(TILES - 1, False)

        @block.scalar
        def _(act):
            def tile(i, more):
                act.wait_ge(lin_summed, i + 1 + START)
                act.wait_ge(h_ready, i + START)
                for m in range(KD):
                    c = cols["ffn_bias"] + m
                    act.activation(tanh[:, m, :], ps[:, m, :], ACT.Tanh,
                                   bias=vec[:, c:c + 1]).then_inc(tanh_ready, 1)
                if more:
                    norm.square(act, i + 1)
                    norm.take_root(act, i + 1)

            norm.square(act, 0)
            norm.take_root(act, 0)
            with act.Fori(0, TILES - 1) as i:
                tile(i, True)
            tile(TILES - 1, False)

        @block.vector
        def _(dve):
            norm.centre(dve, 0)
            dve.wait_ge(first_summed, 1 + START)
            dve.tensor_copy(first, ps[:, 0:KD, 0:D]).then_inc(first_kept, 1)
            dve.wait_ge(whole_summed, 1 + START)
            dve.tensor_copy(whole, ps[:, 2:2 + KD, 0:D]).then_inc(whole_kept, 1)
            norm.scale(dve, 0)

            def tile(i, more):
                if more:
                    norm.centre(dve, i + 1)
                dve.wait_ge(tanh_ready, (i + 1) * KD + START)
                dve.wait_ge(turned, i + START)
                dve.tensor_tensor(h_out, tanh, hT[:, :, bass.ds(i * TILE, TILE)], ALU.add).then_inc(h_ready, 1)
                if more:
                    norm.scale(dve, i + 1)
                dve.wait_ge(turned, i + 1 + START)
                dve.wait_ge(written, i * 16 + START)
                dve.tensor_copy(rows.rearrange("p a b -> p (a b)"),
                                ps[:, 2:4, :].rearrange("p a b -> p (a b)")).then_inc(rows_ready, 1)

            with dve.Fori(0, TILES - 1) as i:
                tile(i, True)
            tile(TILES - 1, False)


class Memory:

    def __init__(self, nc, ctx, cols, cst, n_vec, n_const):
        def sb(name, shape):
            return ctx.enter_context(nc.sbuf_tensor(name, shape, F32))
        self.cols = cols
        self.norm_sems, self.norms = None, 0
        self.ctx = ctx
        self.hT = sb("hT", [P, KD, N])
        self.vec = sb("vec", [P, n_vec])
        self.const = sb("const", [P, n_const])
        self.ident = self.const[:, 0:P]
        self.words = nc.sbuf_bytes_remaining // 4 - 64
        self.region = sb("region", [P, self.words])
        self.used = 0
        self.cst = {name: self.const[:, a:b] for name, (a, b) in cst.items()}

    def part(self, shape, at=None):
        n = int(np.prod(shape[1:]))
        if at is None:
            at = self.used
            self.used += n
        assert at + n <= self.words, (at + n, self.words)
        flat = self.region[0:shape[0], at:at + n]
        if len(shape) == 3:
            return flat.rearrange("p (a b) -> p a b", a=shape[1])
        if len(shape) == 4:
            return flat.rearrange("p (a b c) -> p a b c", a=shape[1], b=shape[2])
        if len(shape) == 5:
            return flat.rearrange("p (a b c d) -> p a b c d", a=shape[1], b=shape[2], c=shape[3])
        return flat


def program(nc, dram, out, cols, cst, n_vec, n_const):
    with ExitStack() as ctx:
        mem = Memory(nc, ctx, cols, cst, n_vec, n_const)
        phase_tokens(nc, mem, dram)
        mem.used = 0
        phase_attention(nc, mem, dram)
        mem.used = 0
        phase_experts(nc, mem, dram)
        mem.used = 0
        phase_state_space(nc, mem, dram)
        mem.used = 0
        phase_last(nc, mem, dram, out)


def chunks(a, p=P):
    a = np.asarray(a)
    return a.reshape(a.shape[0] // p, p, *a.shape[1:]).swapaxes(0, 1)


def flat(a):
    return np.ascontiguousarray(a.reshape(a.shape[0], -1))


def constants():
    f = np.float32
    e = np.arange(P) // DH
    inv_freq = 1.0 / f(10000.0) ** (np.arange(0, DH, 2, dtype=f) / f(DH))
    angle = np.outer(np.arange(L, dtype=f), inv_freq).astype(f)
    of = (2 * ((np.arange(P) % DH) // 2)) % (DH // 2)
    sign = np.where(np.arange(P) % 2 == 0, f(-1), f(1))[:, None]
    tables = {
        "ident": np.eye(P, dtype=f),
        "mean": np.full((P, P), 1.0 / D, f),
        "head_mean": (e[:, None] == e[None, :]).astype(f) / f(DH),
        "pick2": (e[:, None] == np.arange(2)[None, :]).astype(f),
        "cos": np.cos(angle).T[of],
        "sin": np.sin(angle).T[of] * sign,
        "eps5": np.full((P, 1), 1e-5, f),
        "eps6": np.full((P, 1), 1e-6, f),
        "one": np.ones((P, 1), f),
        "zero": np.zeros((P, 1), f),
        "expert_of": flat((2 * np.arange(PAIRS)[None, :, None] + e[:, None, None]
                           == np.arange(EXPERTS)[None, None, :]).astype(f)),
        "number": np.tile(np.arange(EXPERTS, dtype=f) - EXPERTS, (P, 1)),
    }
    at, where = 0, {}
    for name, a in tables.items():
        where[name] = (at, at + a.shape[1])
        at += a.shape[1]
    return np.concatenate([a.astype(f) for a in tables.values()], axis=1), where


def kernel(**inputs):
    import concourse.bacc as bacc
    from concourse.bass_utils import run_bass_kernel_spmd

    t = {k: np.asarray(v) for k, v in inputs.items()}
    f = np.float32
    vec = Columns()
    for name, key in (("b1", "L0_tok_b1"), ("b2", "L0_tok_b2")):
        vec.add(name, chunks(t[key]))
    convs = [np.concatenate([chunks(t[f"L0_attn_{q}cw"][:, 0]), chunks(t[f"L0_attn_{q}cb"])[..., None]], axis=2)
             for q in "qkv"]
    vec.add("conv", flat(np.stack(convs, axis=1)))
    for name, key in (("bb", "bb"), ("dt", "gkb"), ("dt_bias", "dt_bias"), ("A_log", "A_log"), ("Dp", "D_param")):
        vec.add(name, np.tile(t["L0_attn_" + key], P // HEADS)[:, None])
    vec.add("onorm", np.tile(t["L0_attn_onorm_w"], P // DH)[:, None])
    vec.add("ssm_conv", flat(np.concatenate([chunks(t["L1_attn_conv_w"][:, 0]), chunks(t["L1_attn_conv_b"])[..., None]],
                                            axis=2)))
    vec.add("ssm_b_dt", chunks(t["L1_attn_b_dt"]))
    vec.add("ssm_A_log", flat(chunks(t["L1_attn_A_log"])))
    vec.add("ssm_D", chunks(t["L1_attn_D"]))
    vec.add("ffn_bias", chunks(t["L1_ffn_bias"]))
    vecs = np.ascontiguousarray(np.concatenate(vec.parts, axis=1))

    const, cst = constants()

    arrays = {
        "x": t["x"],
        "W1": t["L0_tok_W1"].reshape(V, 2, PATCH // 2, D).transpose(1, 0, 2, 3).reshape(P, PATCH // 2, D),
        "W2": chunks(t["L0_tok_W2"]),
        "Wqkv": np.stack([chunks(t["L0_attn_W" + q]) for q in "qkv"], axis=1),
        "Wg": chunks(t["L0_attn_Wg"]),
        "Wo": chunks(t["L0_attn_Wo"]),
        "Wab": np.concatenate([chunks(t["L0_attn_bw"]), chunks(t["L0_attn_gkw"])], axis=2),
        "W_A": chunks(t["L0_ffn_W_A"].reshape(EXPERTS * RANK, D).T),
        "W_B": t["L0_ffn_W_B"].reshape(PAIRS, 2, FFN, RANK).transpose(1, 3, 0, 2).reshape(P, PAIRS, FFN),
        "W_up": t["L0_ffn_W_up"].reshape(EXPERTS, FFN, KD, P).transpose(3, 0, 2, 1),
        "W_down": t["L0_ffn_W_down"].reshape(EXPERTS, D, FC, P).transpose(3, 0, 2, 1),
        "W_in": chunks(t["L1_attn_W_in"]),
        "W_x": chunks(np.concatenate([t["L1_attn_W_x"][:, DT_RANK:]] * 3 + [t["L1_attn_W_x"][:, :DT_RANK]], axis=1)),
        "W_dt": t["L1_attn_W_dt"],
        "W_out": chunks(t["L1_attn_W_out"]),
        "ffn_wT": chunks(t["L1_ffn_weight"].T),
        "ffn_a1": chunks(t["L1_ffn_aux_weight1"]),
        "ffn_a2": chunks(t["L1_ffn_aux_weight2"]),
        "vec": vecs,
        "const": const,
    }
    arrays = {k: np.ascontiguousarray(a) for k, a in arrays.items()}
    nc = bacc.Bacc("TRN2", target_bir_lowering=False, num_devices=1)
    dram = {k: nc.dram_tensor(f"in_{k}", a.shape, F32, kind="ExternalInput").ap() for k, a in arrays.items()}
    out = nc.dram_tensor("out_h", (N // P, P, D), F32, kind="ExternalOutput").ap()
    program(nc, dram, out, vec.at, cst, vecs.shape[1], const.shape[1])
    r = run_bass_kernel_spmd(nc, [{f"in_{k}": a for k, a in arrays.items()}], core_ids=[0])
    return r.results[0]["out_h"].reshape(B, L, D)
```
